# Optimizing a Trainium2 kernel written in Bass

```python
import numpy as np
import jax
import jax.numpy as jnp

def _softmax(x, axis=-1):
    return jax.nn.softmax(x, axis=axis)

def _gelu(x):
    return jax.nn.gelu(x, approximate=True)

def _silu(x):
    return jax.nn.silu(x)

def _sigmoid(x):
    return jax.nn.sigmoid(x)

def _layernorm(x, axis=-1, eps=1e-05):
    m = jnp.mean(x, axis=axis, keepdims=True)
    v = jnp.var(x, axis=axis, keepdims=True)
    return (x - m) / jnp.sqrt(v + eps)

def _scatter_add(tgt, idx, src, axis=0):
    return tgt.at[idx].add(src)

def _segment_sum(src, seg, n):
    return jax.ops.segment_sum(src, seg, n)
kernel_name = 'mk_seq_preln_d2_jaxref_r8_5cf0f2'

def setup_inputs(seed: int=0):
    np.random.seed(seed)
    _w = jnp.asarray

    def _L0_attn_setup():
        import jax, jax.numpy as jnp
        import numpy as np
        NUM_HEADS = 16
        WINDOW = 32
        LN_EPS = 1e-05
        key = jax.random.key(seed)
        k1, k2, k3 = jax.random.split(key, 3)
        B, L, D = (2, 256, 128)
        x = jax.random.normal(k1, (B, L, D), dtype=jnp.float32)
        w_qkv = jax.random.normal(k2, (3 * D, D), dtype=jnp.float32) * 0.02
        w_out = jax.random.normal(k3, (D, D), dtype=jnp.float32) * 0.02
        gamma = jnp.ones((D,), dtype=jnp.float32)
        beta = jnp.zeros((D,), dtype=jnp.float32)
        return {'x': x, 'w_qkv': w_qkv, 'w_out': w_out, 'gamma': gamma, 'beta': beta}
    _L0_attn_in = _L0_attn_setup()

    def _L0_ffn_setup():
        import jax, jax.numpy as jnp
        import numpy as np
        DIM = 128

        def _reference_tuple_inner(x, W_r, W_k, W_v, mu_r, mu_k):
            B, T, C = x.shape
            x_prev = jnp.concatenate([jnp.zeros((B, 1, C), x.dtype), x[:, :-1, :]], axis=1)
            xr = mu_r * x + (1.0 - mu_r) * x_prev
            xk = mu_k * x + (1.0 - mu_k) * x_prev
            r = jax.nn.sigmoid(jnp.einsum('btc,dc->btd', xr, W_r))
            k = jnp.einsum('btc,dc->btd', xk, W_k)
            k_act = jnp.square(jax.nn.relu(k))
            out = r * jnp.einsum('btc,dc->btd', k_act, W_v)
            new_state = x[:, -1, :]
            return (out, new_state)
        key = jax.random.key(seed)
        ks = jax.random.split(key, 6)
        B, T, C = (8, 256, DIM)
        x = jax.random.normal(ks[0], (B, T, C), dtype=jnp.float32)
        s = 1.0 / np.sqrt(C)
        W_r = jax.random.uniform(ks[1], (C, C), jnp.float32, -s, s)
        W_k = jax.random.uniform(ks[2], (C, C), jnp.float32, -s, s)
        W_v = jax.random.uniform(ks[3], (C, C), jnp.float32, -s, s)
        mu_r = jax.random.uniform(ks[4], (C,), jnp.float32)
        mu_k = jax.random.uniform(ks[5], (C,), jnp.float32)
        return {'x': x, 'W_r': W_r, 'W_k': W_k, 'W_v': W_v, 'mu_r': mu_r, 'mu_k': mu_k}
    _L0_ffn_in = _L0_ffn_setup()

    def _L1_attn_setup():
        import jax, jax.numpy as jnp
        import numpy as np
        DIM = 128
        NUM_HEADS = 16
        HEAD_DIM = DIM // NUM_HEADS
        SCALE = HEAD_DIM ** (-0.5)

        def alibi_slopes(num_heads):
            x = (2 ** 8) ** (1.0 / num_heads)
            return jnp.array([1.0 / x ** (i + 1) for i in range(num_heads)], dtype=jnp.float32)
        key = jax.random.key(seed)
        ks = jax.random.split(key, 6)
        B, N = (2, 256)
        x = jax.random.normal(ks[0], (B, N, DIM), dtype=jnp.float32)
        s = DIM ** (-0.5)
        Wq = jax.random.normal(ks[1], (DIM, DIM), dtype=jnp.float32) * s
        Wk = jax.random.normal(ks[2], (DIM, DIM), dtype=jnp.float32) * s
        Wv = jax.random.normal(ks[3], (DIM, DIM), dtype=jnp.float32) * s
        Wp = jax.random.normal(ks[4], (DIM, DIM), dtype=jnp.float32) * s
        bp = jnp.zeros((DIM,), dtype=jnp.float32)
        return {'x': x, 'Wq': Wq, 'Wk': Wk, 'Wv': Wv, 'Wp': Wp, 'bp': bp}
    _L1_attn_in = _L1_attn_setup()

    def _L1_ffn_setup():
        import jax, jax.numpy as jnp
        import numpy as np
        E = 16
        G = 4
        EPG = E // G
        K = 4
        TOPK_GROUP = 2
        PER_GROUP_K = K // TOPK_GROUP

        def _route(xf, router_w, correction_bias):
            S = xf.shape[0]
            logits = xf @ router_w.T
            scores = jax.nn.sigmoid(logits)
            sb = scores + correction_bias
            grp_top = jax.lax.top_k(sb.reshape(S, G, EPG), PER_GROUP_K)[0]
            group_scores = grp_top.sum(axis=-1)
            _, group_idx = jax.lax.top_k(group_scores, TOPK_GROUP)
            group_mask = jnp.zeros((S, G), sb.dtype).at[jnp.arange(S)[:, None], group_idx].set(1.0)
            score_mask = jnp.broadcast_to(group_mask[:, :, None], (S, G, EPG)).reshape(S, E)
            masked = jnp.where(score_mask > 0, sb, -jnp.inf)
            _, topk_idx = jax.lax.top_k(masked, K)
            w = jnp.take_along_axis(scores, topk_idx, axis=1)
            w = w / (w.sum(axis=-1, keepdims=True) + 1e-20)
            return (topk_idx, w, scores)
        key = jax.random.key(seed)
        ks = jax.random.split(key, 9)
        B, T, C, H, HS = (2, 128, 128, 32, 256)
        std = 0.02
        return {'x': jax.random.normal(ks[0], (B, T, C), jnp.float32), 'router_w': jax.random.normal(ks[1], (E, C), jnp.float32) * std, 'correction_bias': jnp.zeros((E,), jnp.float32), 'gate_w': jax.random.normal(ks[2], (E, C, H), jnp.float32) * std, 'up_w': jax.random.normal(ks[3], (E, C, H), jnp.float32) * std, 'down_w': jax.random.normal(ks[4], (E, H, C), jnp.float32) * std, 'shared_gate_w': jax.random.normal(ks[5], (HS, C), jnp.float32) * std, 'shared_up_w': jax.random.normal(ks[6], (HS, C), jnp.float32) * std, 'shared_down_w': jax.random.normal(ks[7], (C, HS), jnp.float32) * std}
    _L1_ffn_in = _L1_ffn_setup()
    _d = {'L0_attn_x': _L0_attn_in['x'], 'L0_attn_w_qkv': _L0_attn_in['w_qkv'], 'L0_attn_w_out': _L0_attn_in['w_out'], 'L0_attn_gamma': _L0_attn_in['gamma'], 'L0_attn_beta': _L0_attn_in['beta'], 'L0_ffn_W_r': _L0_ffn_in['W_r'], 'L0_ffn_W_k': _L0_ffn_in['W_k'], 'L0_ffn_W_v': _L0_ffn_in['W_v'], 'L0_ffn_mu_r': _L0_ffn_in['mu_r'], 'L0_ffn_mu_k': _L0_ffn_in['mu_k'], 'L1_attn_Wq': _L1_attn_in['Wq'], 'L1_attn_Wk': _L1_attn_in['Wk'], 'L1_attn_Wv': _L1_attn_in['Wv'], 'L1_attn_Wp': _L1_attn_in['Wp'], 'L1_attn_bp': _L1_attn_in['bp'], 'L1_ffn_router_w': _L1_ffn_in['router_w'], 'L1_ffn_correction_bias': _L1_ffn_in['correction_bias'], 'L1_ffn_gate_w': _L1_ffn_in['gate_w'], 'L1_ffn_up_w': _L1_ffn_in['up_w'], 'L1_ffn_down_w': _L1_ffn_in['down_w'], 'L1_ffn_shared_gate_w': _L1_ffn_in['shared_gate_w'], 'L1_ffn_shared_up_w': _L1_ffn_in['shared_up_w'], 'L1_ffn_shared_down_w': _L1_ffn_in['shared_down_w']}
    _x0 = _d['L0_attn_x']
    _d['L0_attn_x'] = jax.random.normal(jax.random.fold_in(jax.random.key(seed), 1), (1, 2048, 128), dtype=_x0.dtype)
    del _x0
    return _d

def reference(L0_attn_x, L0_attn_w_qkv, L0_attn_w_out, L0_attn_gamma, L0_attn_beta, L0_ffn_W_r, L0_ffn_W_k, L0_ffn_W_v, L0_ffn_mu_r, L0_ffn_mu_k, L1_attn_Wq, L1_attn_Wk, L1_attn_Wv, L1_attn_Wp, L1_attn_bp, L1_ffn_router_w, L1_ffn_correction_bias, L1_ffn_gate_w, L1_ffn_up_w, L1_ffn_down_w, L1_ffn_shared_gate_w, L1_ffn_shared_up_w, L1_ffn_shared_down_w):

    def _L0_attn_ref(x, w_qkv, w_out, gamma, beta):
        import jax, jax.numpy as jnp
        import numpy as np
        NUM_HEADS = 16
        WINDOW = 32
        LN_EPS = 1e-05
        B, L, D = x.shape
        H = NUM_HEADS
        HD = D // H
        residual = x
        mu = jnp.mean(x, axis=-1, keepdims=True)
        var = jnp.mean(jnp.square(x - mu), axis=-1, keepdims=True)
        xn = (x - mu) * jax.lax.rsqrt(var + LN_EPS) * gamma + beta
        qkv = jnp.einsum('bld,ed->ble', xn, w_qkv).reshape(B, L, 3, H, HD)
        qkv = jnp.transpose(qkv, (2, 0, 3, 1, 4))
        q, k, v = (qkv[0], qkv[1], qkv[2])
        scores = jnp.einsum('bhqd,bhkd->bhqk', q, k) / jnp.sqrt(jnp.float32(HD))
        idx = jnp.arange(L)
        band = jnp.abs(idx[:, None] - idx[None, :]) <= WINDOW // 2
        scores = jnp.where(band[None, None], scores, -jnp.inf)
        attn = jax.nn.softmax(scores, axis=-1)
        out = jnp.einsum('bhqk,bhkd->bhqd', attn, v)
        out = jnp.transpose(out, (0, 2, 1, 3)).reshape(B, L, D)
        return residual + jnp.einsum('bld,ed->ble', out, w_out)

    def _L0_ffn_ref(x, W_r, W_k, W_v, mu_r, mu_k):
        import jax, jax.numpy as jnp
        import numpy as np
        DIM = 128

        def _reference_tuple_inner(x, W_r, W_k, W_v, mu_r, mu_k):
            B, T, C = x.shape
            x_prev = jnp.concatenate([jnp.zeros((B, 1, C), x.dtype), x[:, :-1, :]], axis=1)
            xr = mu_r * x + (1.0 - mu_r) * x_prev
            xk = mu_k * x + (1.0 - mu_k) * x_prev
            r = jax.nn.sigmoid(jnp.einsum('btc,dc->btd', xr, W_r))
            k = jnp.einsum('btc,dc->btd', xk, W_k)
            k_act = jnp.square(jax.nn.relu(k))
            out = r * jnp.einsum('btc,dc->btd', k_act, W_v)
            new_state = x[:, -1, :]
            return (out, new_state)
        return _reference_tuple_inner(x, W_r, W_k, W_v, mu_r, mu_k)[0]

    def _L1_attn_ref(x, Wq, Wk, Wv, Wp, bp):
        import jax, jax.numpy as jnp
        import numpy as np
        DIM = 128
        NUM_HEADS = 16
        HEAD_DIM = DIM // NUM_HEADS
        SCALE = HEAD_DIM ** (-0.5)

        def alibi_slopes(num_heads):
            x = (2 ** 8) ** (1.0 / num_heads)
            return jnp.array([1.0 / x ** (i + 1) for i in range(num_heads)], dtype=jnp.float32)
        B, N, C = x.shape
        H, D = (NUM_HEADS, HEAD_DIM)
        q = (x @ Wq.T).reshape(B, N, H, D).transpose(0, 2, 1, 3)
        k = (x @ Wk.T).reshape(B, N, H, D).transpose(0, 2, 1, 3)
        v = (x @ Wv.T).reshape(B, N, H, D).transpose(0, 2, 1, 3)
        rel = (jnp.arange(N)[None, :] - jnp.arange(N)[:, None]).astype(jnp.float32)
        bias = alibi_slopes(H)[:, None, None] * rel
        score = jnp.einsum('bhnd,bhmd->bhnm', q, k) / SCALE + bias[None]
        attn = jax.nn.softmax(score, axis=-1)
        out = jnp.einsum('bhnm,bhmd->bhnd', attn, v)
        out = out.transpose(0, 2, 1, 3).reshape(B, N, C)
        return out @ Wp.T + bp

    def _L1_ffn_ref(x, router_w, correction_bias, gate_w, up_w, down_w, shared_gate_w, shared_up_w, shared_down_w):
        import jax, jax.numpy as jnp
        import numpy as np
        E = 16
        G = 4
        EPG = E // G
        K = 4
        TOPK_GROUP = 2
        PER_GROUP_K = K // TOPK_GROUP

        def _route(xf, router_w, correction_bias):
            S = xf.shape[0]
            logits = xf @ router_w.T
            scores = jax.nn.sigmoid(logits)
            sb = scores + correction_bias
            grp_top = jax.lax.top_k(sb.reshape(S, G, EPG), PER_GROUP_K)[0]
            group_scores = grp_top.sum(axis=-1)
            _, group_idx = jax.lax.top_k(group_scores, TOPK_GROUP)
            group_mask = jnp.zeros((S, G), sb.dtype).at[jnp.arange(S)[:, None], group_idx].set(1.0)
            score_mask = jnp.broadcast_to(group_mask[:, :, None], (S, G, EPG)).reshape(S, E)
            masked = jnp.where(score_mask > 0, sb, -jnp.inf)
            _, topk_idx = jax.lax.top_k(masked, K)
            w = jnp.take_along_axis(scores, topk_idx, axis=1)
            w = w / (w.sum(axis=-1, keepdims=True) + 1e-20)
            return (topk_idx, w, scores)
        B, T, C = x.shape
        S = B * T
        xf = x.reshape(S, C)
        sg = xf @ shared_gate_w.T
        su = xf @ shared_up_w.T
        shared_out = jax.nn.silu(sg) * su @ shared_down_w.T
        topk_idx, w, _scores = _route(xf, router_w, correction_bias)
        combine = jnp.zeros((S, E), xf.dtype).at[jnp.arange(S)[:, None], topk_idx].add(w)
        g = jnp.einsum('sc,ech->esh', xf, gate_w)
        u = jnp.einsum('sc,ech->esh', xf, up_w)
        h = jax.nn.silu(g) * u
        hw = h * combine.T[:, :, None]
        routed = jnp.einsum('esh,ehc->sc', hw, down_w)
        return (shared_out + routed).reshape(B, T, C)
    x = L0_attn_x
    x = x + _L0_attn_ref(_layernorm(x, axis=-1), L0_attn_w_qkv, L0_attn_w_out, L0_attn_gamma, L0_attn_beta)
    x = x + _L0_ffn_ref(_layernorm(x, axis=-1), L0_ffn_W_r, L0_ffn_W_k, L0_ffn_W_v, L0_ffn_mu_r, L0_ffn_mu_k)
    x = x + _L1_attn_ref(_layernorm(x, axis=-1), L1_attn_Wq, L1_attn_Wk, L1_attn_Wv, L1_attn_Wp, L1_attn_bp)
    x = x + _L1_ffn_ref(_layernorm(x, axis=-1), L1_ffn_router_w, L1_ffn_correction_bias, L1_ffn_gate_w, L1_ffn_up_w, L1_ffn_down_w, L1_ffn_shared_gate_w, L1_ffn_shared_up_w, L1_ffn_shared_down_w)
    return x

_drawn_inputs = setup_inputs


def setup_inputs(seed=0):
    import zlib

    import numpy as np

    out = dict(_drawn_inputs(seed))
    spreads = {'L0_attn_gamma': (1.0, 0.6),
     'L0_attn_beta': (0.0, 0.8),
     'L1_attn_bp': (0.0, 0.1),
     'L1_ffn_correction_bias': (0.0, 0.8)}
    factors = {'L0_attn_w_qkv': 6.679,
     'L0_attn_w_out': 6.66,
     'L0_ffn_W_r': 3.68,
     'L0_ffn_mu_r': 7.345,
     'L1_ffn_router_w': 8.0,
     'L1_ffn_gate_w': 8.0,
     'L1_ffn_up_w': 8.0,
     'L1_ffn_down_w': 8.0,
     'L1_ffn_shared_gate_w': 8.0,
     'L1_ffn_shared_up_w': 8.0,
     'L1_ffn_shared_down_w': 8.0}
    for name, (base, spread) in spreads.items():
        noise = np.random.default_rng([zlib.crc32(name.encode()), seed]).standard_normal(out[name].shape)
        drawn = base * np.exp(spread * noise) if base else spread * noise
        out[name] = jnp.asarray(drawn.astype(out[name].dtype))
    for name, factor in factors.items():
        out[name] = (out[name] * factor).astype(out[name].dtype)
    return out
```

```python
from contextlib import ExitStack

import concourse.bass as bass
import numpy as np
from concourse import mybir

F32 = mybir.dt.float32
BF16 = mybir.dt.bfloat16
U32 = mybir.dt.uint32
ALU = mybir.AluOpType
ACT = mybir.ActivationFunctionType
AX = mybir.AxisListType

P = 128
T, C = 2048, 128
NT = T // P
H, HD = 16, 8
PAD = 16
CHUNK = 512
NC = T // CHUNK
TPC = CHUNK // P
EPS = 1e-5

HIGH, MID, LOW = range(3)
PAIRS = [(HIGH, HIGH), (HIGH, MID), (HIGH, LOW), (MID, HIGH), (MID, MID), (LOW, HIGH)]
ROW_BIAS = HD * len(PAIRS)
ROW_MAX = ROW_BIAS + 3
ROW_PAD = ROW_MAX + 3
KR = 72
WK = PAD + T + PAD

HALF = 16
QB = P - 2 * HALF
NB = -(-T // QB)
G = 4
HG = H // G
VC = HD + 1
MASKED = -1e30

E, TOPK, EG, TOPG, HE, HS = 16, 4, 4, 2, 32, 256
MT_R = E * HE // P
MT_S = HS // P
MT = MT_R + MT_S


class Count:

    def __init__(self, eng, sem, base=0):
        self.eng, self.sem, self.n = eng, sem, base

    def up(self, ins):
        ins.then_inc(self.sem, 1)
        self.n = self.n + 1

    def settle(self):
        self.eng.wait_ge(self.sem, self.n)


def build(nc, a, out):
    ctx = ExitStack()
    with ctx:
        def sb(name, shape, dt=F32):
            return ctx.enter_context(nc.sbuf_tensor(name, shape, dt))

        def sem(name):
            return ctx.enter_context(nc.semaphore(name))

        QA = sb("QA", [P, H, T], BF16)
        KA = sb("KA", [P, H, WK], BF16)
        X = sb("X", [P, NT, C])
        big = sb("big", [P, G * T])
        OT = big[:, :].rearrange("p (g n) -> p g n", g=G)
        parts = big[:, 0:3 * T].bitcast(BF16).rearrange("p (s i n) -> p s i n", s=2, i=3)
        V = sb("V", [P, NB, H, VC])
        V1 = V[:, 0:NT, :, :]
        ring = sb("ring", [P, 8 * CHUNK + 64])
        PR = ring[:, 0:8 * CHUNK].rearrange("p (b n) -> p b n", b=8)
        XT = ring[:, 0:WK]
        xhat = ring[:, WK:WK + 2 * CHUNK].rearrange("p (b t c) -> p b t c", b=2, t=TPC)
        resid = ring[:, WK + 2 * CHUNK:WK + 4 * CHUNK].rearrange("p (b n) -> p b n", b=2)
        vflat = V[:, :, :, :].rearrange("p a b c -> p (a b c)")
        mix = vflat[:, 0:6 * CHUNK].rearrange("p (b n) -> p b n", b=6)
        On = vflat[:, 0:2 * C].rearrange("p (b c) -> p b c", b=2)
        OnT = vflat[:, 2 * C:4 * C].rearrange("p (b c) -> p b c", b=2)

        wqkv = [sb("wqkv0", [P, 3 * C]), sb("wqkv1", [P, 3 * C])]
        wo = [sb("wo0", [P, C]), sb("wo1", [P, C])]
        wmix = sb("wmix", [P, 3, C])
        vecs = sb("vecs", [P, 6])
        GAMMA, BETA, MU_R, MU_K, OM_R, OM_K = (vecs[:, i:i + 1] for i in range(6))
        ident = sb("ident", [P, P])
        identb = sb("identb", [P, P], BF16)
        maskA = sb("maskA", [QB, HG, P], BF16)
        maskB = sb("maskB", [P, HG, QB], BF16)
        bp = sb("bp", [P, C])
        half = sb("half", [P, TPC])
        stats = sb("stats", [P, TPC, 6])
        mv = sb("mv", [P, NT, 2])
        rs = sb("rs", [P, NT])
        rs1 = sb("rs1", [P, NT])
        tmp4 = sb("tmp4", [P, 3, NT])
        rawmax = sb("rawmax", [P, 2, 32])
        rowmax = sb("rowmax", [P, 16])
        negres = sb("negres", [P, 16])
        mparts = sb("mparts", [P, P], BF16)
        mrow = sb("mrow", [48, P], BF16)
        rz = sb("rz", [P, 2, H])

        qaf = QA[:, :, :].rearrange("p h n -> p (h n)").bitcast(F32)
        gate = qaf[:, 0:512]
        upw = qaf[:, 512:1024]
        down = qaf[:, 1024:1536].rearrange("p (m c) -> p m c", m=MT_R)
        sgate = qaf[:, 1536:1792]
        sup = qaf[:, 1792:2048]
        sdown = qaf[:, 2048:2304].rearrange("p (m c) -> p m c", m=MT_S)
        router = qaf[:, 2304:2320]
        cbias = qaf[:, 2320:2336]
        spread = qaf[:, 2336:2336 + 256].bitcast(BF16).rearrange("p (m n) -> p m n", m=MT_R)
        combT = qaf[:, 2600:2600 + T // 2].bitcast(BF16)
        silu = qaf[:, 3700:3700 + 2 * CHUNK].rearrange("p (b n) -> p b n", b=2)
        hid = qaf[:, 4800:4800 + 2 * MT * CHUNK].rearrange("p (b m n) -> p b m n", b=2, m=MT)
        rt = qaf[:, 11000:11000 + 12 * NT * E].rearrange("p (b t e) -> p b t e", b=12, t=NT)
        combp = qaf[:, 14200:14200 + NT * 24].bitcast(BF16).rearrange("p (t i) -> p t i", t=NT)

        ps = ctx.enter_context(nc.psum_tensor("ps", [P, 8, CHUNK], F32))

        scratch = nc.dram_tensor("scratch", [2, P, 3, T], BF16)
        scr = scratch.ap()

        x_d = a["x"].rearrange("(c t p) n -> c p t n", c=NC, p=P)
        out_d = out.rearrange("(c t p) n -> c p t n", c=NC, p=P)

        x_in = [sem(f"x_in{c}") for c in range(NC)]
        w_in = sem("w_in")
        w2_in = sem("w2_in")
        bp_added = sem("bp_added")
        ones_ready = sem("ones_ready")
        om_ready = sem("om_ready")
        x_ready = [None] + [sem(f"x_ready{n}") for n in (1, 2, 3)]
        stats_ready = [sem(f"stats_ready{n}") for n in range(4)]
        rstd_ready = [sem(f"rstd_ready{n}") for n in range(4)]
        xhat_ready = [sem(f"xhat_ready{n}") for n in range(4)]
        turned = [sem(f"turned{n}") for n in range(4)]
        xt_ready = [sem(f"xt_ready{n}") for n in range(4)]
        dve = sem("dve")
        pool = sem("pool")
        resid_in_x = sem("resid_in_x")

        L = range(2)
        qk_made = [sem(f"qk_made{n}") for n in L]
        high_ready = [sem(f"high_ready{n}") for n in L]
        resid_ready = [sem(f"resid_ready{n}") for n in L]
        mid_ready = [sem(f"mid_ready{n}") for n in L]
        low_ready = [sem(f"low_ready{n}") for n in L]
        v_made = [sem(f"v_made{n}") for n in L]
        v_ready = [sem(f"v_ready{n}") for n in L]
        parts_kept = [sem(f"parts_kept{n}") for n in L]
        rows_in = [sem(f"rows_in{n}") for n in L]
        qk_in = [[sem(f"qk_in{n}_{g}") for g in range(G)] for n in L]
        zeroed = [sem(f"zeroed{n}") for n in L]
        a_made = [sem(f"a_made{n}") for n in L]
        a_read = [sem(f"a_read{n}") for n in L]
        mparts_ready = [sem(f"mparts_ready{n}") for n in L]
        mt_made = [sem(f"mt_made{n}") for n in L]
        mrow_ready = [sem(f"mrow_ready{n}") for n in L]
        mrow_in = [sem(f"mrow_in{n}") for n in L]
        b_made = [sem(f"b_made{n}") for n in L]
        exp_done = [sem(f"exp_done{n}") for n in L]
        pv_done = [sem(f"pv_done{n}") for n in L]
        o_kept = [sem(f"o_kept{n}") for n in L]
        o_turned = [sem(f"o_turned{n}") for n in L]
        on_ready = [sem(f"on_ready{n}") for n in L]
        on_turned = [sem(f"on_turned{n}") for n in L]
        ont_ready = [sem(f"ont_ready{n}") for n in L]
        proj_made = [sem(f"proj_made{n}") for n in L]

        mixed = sem("mixed")
        rk_made = sem("rk_made")
        sig_ready = sem("sig_ready")
        relu_ready = sem("relu_ready")
        kact_ready = sem("kact_ready")
        vm_made = sem("vm_made")

        logits_made = sem("logits_made")
        scores_ready = sem("scores_ready")
        comb_ready = sem("comb_ready")
        comb_turned = sem("comb_turned")
        combT_ready = sem("combT_ready")
        g_made = sem("g_made")
        u_made = sem("u_made")
        silu_ready = sem("silu_ready")
        gu_ready = sem("gu_ready")
        cb_made = sem("cb_made")
        hid_ready = sem("hid_ready")
        down_made = sem("down_made")
        y_ready = sem("y_ready")
        stored = sem("stored")

        block = ctx.enter_context(nc.Block())

        @block.sync
        def _(sp):
            def weight(dst, src, s=w_in):
                sp.dma_start(dst, src).then_inc(s, 16)

            sp.dma_start(X[:, 0:TPC, :], x_d[0]).then_inc(x_in[0], 16)
            weight(ident[:, :], a["ident"])
            weight(vecs[:, 0:4], a["vecs"])
            weight(wqkv[0][:, :], a["wqkv0"])
            for c in range(1, NC):
                sp.dma_start(X[:, c * TPC:(c + 1) * TPC, :], x_d[c]).then_inc(x_in[c], 16)
            weight(identb[:, :], a["identb"], w2_in)
            weight(maskA[:, :, :], a["maskA"], w2_in)
            weight(maskB[:, :, :], a["maskB"], w2_in)
            weight(wo[0][:, :], a["wo0"], w2_in)
            weight(wmix[:, :, :], a["wmix"], w2_in)
            weight(wqkv[1][:, :], a["wqkv1"], w2_in)
            weight(wo[1][:, :], a["wo1"], w2_in)
            weight(bp[:, :], a["bp_rows"], w2_in)

            def operands(n):
                if n == 1:
                    sp.wait_ge(b_made[0], NB * HG)
                    sp.wait_ge(mrow_in[0], 48 * NB)
                if n == 0:
                    sp.dma_start(QA[ROW_BIAS:ROW_BIAS + 3, :, :], a["ones"][:, :, 0:T]).then_inc(rows_in[n], 16)
                    sp.dma_start(QA[ROW_MAX:KR, :, :], a["zeros"][:, :, 0:T]).then_inc(rows_in[n], 16)
                    sp.dma_start(KA[ROW_PAD:KR, :, :], a["zeros"][0:KR - ROW_PAD]).then_inc(rows_in[n], 16)
                    for s in (slice(0, PAD), slice(PAD + T, WK)):
                        sp.dma_start(KA[0:ROW_BIAS, :, s], a["edge"]).then_inc(rows_in[n], 16)
                    sp.dma_start(KA[ROW_MAX:ROW_MAX + 3, :, :], a["ones"]).then_inc(rows_in[n], 16)
                else:
                    sp.dma_start(QA[ROW_MAX:ROW_MAX + 3, :, :], a["zeros"][0:3, :, 0:T]).then_inc(rows_in[n], 16)
                sp.dma_start(KA[ROW_BIAS:ROW_BIAS + 3, :, :], a[f"kbias{n}"]).then_inc(rows_in[n], 16)
                for c in range(NC):
                    cols = slice(c * CHUNK, (c + 1) * CHUNK)
                    for s in range(2):
                        sp.wait_ge(high_ready[n], 2 * c + s + 1)
                        sp.wait_ge(low_ready[n], 2 * c + s + 1)
                        sp.dma_start(scr[s, :, :, cols], parts[:, s, :, cols]).then_inc(parts_kept[n], 16)
                sp.wait_ge(parts_kept[n], 2 * NC * 16)
                for g in range(G):
                    for s in range(2):
                        for i, pair in enumerate(PAIRS):
                            src = scr[s, g * 32:(g + 1) * 32, pair[s], :].rearrange("(h d) n -> d h n", d=HD)
                            rows = slice(HD * i, HD * i + HD)
                            dst = QA[rows, g * HG:(g + 1) * HG, :] if s == 0 else KA[rows, g * HG:(g + 1) * HG, PAD:PAD + T]
                            sp.dma_start(dst, src).then_inc(qk_in[n][g], 16)

            operands(0)
            for t in range(NB):
                sp.wait_ge(mrow_ready[0], t + 1)
                nq = min(QB, T - t * QB)
                for i in range(3):
                    sp.dma_start(QA[ROW_MAX + i:ROW_MAX + i + 1, :, t * QB:t * QB + nq],
                                 mrow[16 * i:16 * i + 16, 0:nq]).then_inc(mrow_in[0], 16)
            operands(1)
            with sp.Fori(0, NC) as qc:
                for g in range(G):
                    sp.wait_ge(mrow_ready[1], qc * G + g + 1)
                    for hh in range(HG):
                        sp.dma_start(QA[ROW_MAX:ROW_MAX + 3, g * HG + hh, bass.ds(qc * CHUNK, CHUNK)],
                                     mrow[12 * hh:12 * hh + 12, :]).then_inc(mrow_in[1], 16)
            sp.wait_ge(b_made[1], NC * G * NT * HG)
            for dst, name in ((gate, "gate"), (upw, "up"), (down, "down"), (sgate, "sgate"), (sup, "sup"),
                              (sdown, "sdown"), (router, "router"), (cbias, "cbias"), (spread, "spread")):
                sp.dma_start(dst, a[name]).then_inc(w_in, 16)
            for c in range(NC):
                sp.wait_ge(y_ready, c + 1)
                sp.dma_start(out_d[c], X[:, c * TPC:(c + 1) * TPC, :]).then_inc(stored, 16)
            sp.wait_ge(stored, 16 * NC)

        @block.tensor
        def _(pe):
            def turn_xhat(n, c, banks):
                pe.wait_ge(xhat_ready[n], c + 1)
                if c >= 2:
                    pe.wait_ge(xt_ready[n], c - 1)
                for i in range(TPC):
                    mm = pe.transpose(ps[:, banks[c % 2], i * P:(i + 1) * P], xhat[:, c % 2, i, :], ident[:, :])
                mm.then_inc(turned[n], 1)

            def qk(n, c):
                pe.wait_ge(xt_ready[2 * n], c + 1)
                for s in range(2):
                    if c >= 1:
                        pe.wait_ge(resid_ready[n], 2 * (c - 1) + s + 1)
                        pe.wait_ge(high_ready[n], 2 * (c - 1) + s + 1)
                    pe.matmul(ps[:, 2 + s, :], wqkv[n][:, s * C:(s + 1) * C],
                              XT[:, PAD + c * CHUNK:PAD + (c + 1) * CHUNK], start=True, stop=True).then_inc(qk_made[n], 1)

            def values(n, blocks):
                for b in blocks:
                    k = b // 4
                    if b % 4 == 0 and k >= 2:
                        pe.wait_ge(v_ready[n], k - 1)
                    first = b * QB if n == 0 else PAD + b * P
                    nk = min(P, WK - first)
                    mm = pe.matmul(ps[0:nk, 4 + k % 2, (b % 4) * P:(b % 4 + 1) * P], XT[:, first:first + nk],
                                   wqkv[n][:, 2 * C:3 * C], start=True, stop=True)
                    if b % 4 == 3 or b == (NB if n == 0 else NT) - 1:
                        mm.then_inc(v_made[n], 1)

            pe.wait_ge(w_in, 16 * 3)
            for c in range(NC):
                turn_xhat(0, c, (0, 1))
                if c >= 1:
                    qk(0, c - 1)
            qk(0, NC - 1)
            pe.wait_ge(zeroed[0], 1)
            values(0, range(NB))

            def project(n, j):
                if j < NT:
                    if j >= 2:
                        pe.wait_ge(on_ready[n], j - 1)
                    for g in range(G):
                        mm = pe.transpose(ps[:, j % 2, g * P:(g + 1) * P], OT[:, g, j * P:(j + 1) * P], ident[:, :])
                    mm.then_inc(o_turned[n], 1)
                k = j - 1
                if 0 <= k < NT:
                    pe.wait_ge(on_ready[n], k + 1)
                    if k >= 2:
                        pe.wait_ge(ont_ready[n], k - 1)
                    pe.transpose(ps[:, 2 + k % 2, 0:P], On[:, k % 2, :], ident[:, :]).then_inc(on_turned[n], 1)
                k = j - 2
                if 0 <= k < NT:
                    pe.wait_ge(ont_ready[n], k + 1)
                    if k >= 2:
                        pe.wait_ge(x_ready[2 * n + 1], k - 1)
                    pe.matmul(ps[:, 4 + k % 2, 0:P], OnT[:, k % 2, :], wo[n][:, :],
                              start=True, stop=True).then_inc(proj_made[n], 1)

            pe.wait_ge(w2_in, 16 * 8)
            pe.wait_ge(rows_in[0], 16 * 7)
            pe.wait_ge(xt_ready[0], NC)
            pe.wait_ge(low_ready[0], 2 * NC)
            pe.wait_ge(v_ready[0], -(-NB // 4))
            pe.wait_ge(zeroed[0], 2)

            def a_scores(t, g):
                nq, k = min(QB, T - t * QB), HG * t + g
                nk = min(P, WK - t * QB)
                if t == 0:
                    pe.wait_ge(qk_in[0][g], 16 * 12)
                if k >= 2:
                    pe.wait_ge(a_read[0], k - 1)
                bank = ps[0:nq, g % 2, :].rearrange("p (h n) -> p h n", h=HG)
                pe.matmul(bank, identb[0:QB, 0:nq], maskA[:, :, :], start=True, stop=False, skip_group_check=True)
                for hh in range(HG):
                    h = g * HG + hh
                    mm = pe.matmul(bank[:, hh, 0:nk], QA[0:KR, h, t * QB:t * QB + nq], KA[0:KR, h, t * QB:t * QB + nk],
                                   start=False, stop=True, skip_group_check=True)
                mm.then_inc(a_made[0], 1)

            def b_scores(t, g):
                nq, k = min(QB, T - t * QB), HG * t + g
                nk = min(P, WK - t * QB)
                if g == 0:
                    pe.wait_ge(mrow_in[0], 48 * (t + 1))
                if k >= 2:
                    pe.wait_ge(exp_done[0], k - 1)
                bank = ps[0:nk, 2 + g % 2, 0:HG * QB].rearrange("p (h n) -> p h n", h=HG)
                pe.matmul(bank, identb[:, 0:nk], maskB[:, :, :], start=True, stop=False, skip_group_check=True)
                for hh in range(HG):
                    h = g * HG + hh
                    mm = pe.matmul(bank[:, hh, 0:nq], KA[0:KR, h, t * QB:t * QB + nk], QA[0:KR, h, t * QB:t * QB + nq],
                                   start=False, stop=True, skip_group_check=True)
                mm.then_inc(b_made[0], 1)

            def sums(t, g):
                nq, k = min(QB, T - t * QB), HG * t + g
                nk = min(P, WK - t * QB)
                pe.wait_ge(exp_done[0], k + 1)
                if g == 0 and t >= 2:
                    pe.wait_ge(o_kept[0], t - 1)
                for hh in range(HG):
                    mm = pe.matmul(ps[32 * hh:32 * hh + VC, 4 + t % 2, g * QB:g * QB + nq], V[0:nk, t, g * HG + hh, :],
                                   PR[0:nk, g, hh * QB:hh * QB + nq], start=True, stop=True, skip_group_check=True)
                mm.then_inc(pv_done[0], 1)

            LEAD = 3
            for i in range(NB + LEAD + 1):
                for g in range(G):
                    if i < NB:
                        a_scores(i, g)
                    if g == 1 and 1 <= i <= NB:
                        pe.wait_ge(mparts_ready[0], i)
                        if i >= 2:
                            pe.wait_ge(mrow_ready[0], i - 1)
                        pe.transpose(ps[:, 6, :].bitcast(BF16)[0:48, 0:QB], mparts[0:QB, 0:48],
                                     identb[0:QB, 0:QB]).then_inc(mt_made[0], 1)
                    if LEAD <= i < NB + LEAD:
                        b_scores(i - LEAD, g)
                    k = HG * (i - LEAD) + g - 1
                    if 0 <= k < HG * NB:
                        sums(k // HG, k % HG)

            pe.wait_ge(o_kept[0], NB)
            for j in range(NT + TPC + 1):
                project(0, j)
                if j >= 8 and j % TPC == 0:
                    turn_xhat(1, j // TPC - 2, (6, 7))
            for c in range(NC + 1):
                if c < NC:
                    pe.wait_ge(mixed, 2 * c + 1)
                    if c == 0:
                        pe.wait_ge(x_ready[1], NT)
                    if c >= 1:
                        pe.wait_ge(sig_ready, c)
                    for i in range(TPC):
                        mm = pe.matmul(ps[:, 0, i * P:(i + 1) * P], mix[:, 0, i * P:(i + 1) * P], wmix[:, 0, :],
                                       start=True, stop=True)
                    mm.then_inc(rk_made, 1)
                    pe.wait_ge(mixed, 2 * c + 2)
                    if c >= 1:
                        pe.wait_ge(relu_ready, c)
                    pe.matmul(ps[:, 1, :], wmix[:, 1, :], mix[:, 1, :], start=True, stop=True).then_inc(rk_made, 1)
                    pe.wait_ge(kact_ready, c + 1)
                    if c >= 1:
                        pe.wait_ge(x_ready[2], c)
                    for i in range(TPC):
                        mm = pe.matmul(ps[:, 2, i * P:(i + 1) * P], mix[:, 3, i * P:(i + 1) * P], wmix[:, 2, :],
                                       start=True, stop=True)
                    mm.then_inc(vm_made, 1)
            pe.wait_ge(x_ready[2], NC)
            for c in range(NC):
                turn_xhat(2, c, (6, 7))
                if c >= 1:
                    qk(1, c - 1)
            qk(1, NC - 1)
            values(1, range(NT))
            pe.wait_ge(rows_in[1], 32)
            pe.wait_ge(v_ready[1], NT // 4)
            pe.wait_ge(low_ready[1], 2 * NC)
            pe.wait_ge(xt_ready[2], NC)
            pe.wait_ge(ones_ready, 1)

            def a_tile(u, g, hh, qt, half_, q0):
                n = u * 32 + hh * 8 + qt * 2 + half_
                if not isinstance(n, int) or n >= 2:
                    pe.wait_ge(a_read[1], n - 1)
                h = g * HG + hh
                for i in range(2):
                    k0 = PAD + half_ * 1024 + i * CHUNK
                    mm = pe.matmul(ps[:, 2 * half_ + i, :], QA[0:KR, h, bass.ds(q0 + qt * P, P)],
                                   KA[0:KR, h, k0:k0 + CHUNK], start=True, stop=True)
                mm.then_inc(a_made[1], 1)

            def b_tile(u, g, kt, hh, q0):
                n = (u * NT + kt) * HG + hh
                if kt or hh >= 2:
                    pe.wait_ge(exp_done[1], n - 1)
                h = g * HG + hh
                pe.matmul(ps[:, 4 + hh % 2, :], KA[0:KR, h, PAD + kt * P:PAD + (kt + 1) * P],
                          QA[0:KR, h, bass.ds(q0, CHUNK)], start=True, stop=True).then_inc(b_made[1], 1)

            def sum_tile(u, g, kt):
                pe.wait_ge(exp_done[1], (u * NT + kt + 1) * HG)
                if kt == 0:
                    pe.wait_ge(o_kept[1], u + 1)
                for hh in range(HG):
                    mm = pe.matmul(ps[32 * hh:32 * hh + VC, 6, :], V1[:, kt, g * HG + hh, :],
                                   PR[:, (kt % 2) * HG + hh, :], start=(kt == 0), stop=(kt == NT - 1),
                                   skip_group_check=True)
                mm.then_inc(pv_done[1], 1)

            def turn_maxima(u):
                pe.wait_ge(mparts_ready[1], u + 1)
                if not isinstance(u, int) or u >= 1:
                    pe.wait_ge(mrow_ready[1], u)
                pe.transpose(ps[:, 7, :].bitcast(BF16)[:, 0:P], mparts[:, :], identb[:, :]).then_inc(mt_made[1], 1)

            A_ALL = [(hh, qt, hf) for hh in range(HG) for qt in range(4) for hf in range(2)]
            AHEAD = 8

            def unit(qc, g, final):
                u = qc * G + g
                q0 = qc * CHUNK

                def a_next(k):
                    s = AHEAD + k
                    g2 = g + 1 + s // 32
                    over = g2 >= G
                    if final and over:
                        return
                    a_tile(u + 1 + s // 32, g2 % G, *A_ALL[s % 32], q0 + (CHUNK if over else 0))

                for kt in range(NT):
                    if kt == 0:
                        pe.wait_ge(mrow_in[1], 64 * (u + 1))
                    for hh in range(HG):
                        b_tile(u, g, kt, hh, q0)
                        if hh % 2 == 1:
                            a_next(2 * kt + hh // 2)
                        if hh == 1 and kt >= 1:
                            sum_tile(u, g, kt - 1)
                    if kt == 13 and not (final and g == G - 1):
                        turn_maxima(u + 1)
                sum_tile(u, g, NT - 1)

            for g in range(G):
                pe.wait_ge(qk_in[1][g], 16 * 12)
            for s in range(32):
                a_tile(0, 0, *A_ALL[s], 0)
            for s in range(AHEAD):
                a_tile(1, 1, *A_ALL[s], 0)
            turn_maxima(0)
            with pe.Fori(0, NC - 1) as qc:
                for g in range(G):
                    unit(qc, g, False)
            for g in range(G):
                unit(NC - 1, g, True)

            pe.wait_ge(o_kept[1], NC * G + 1)
            for j in range(NT + TPC + 1):
                project(1, j)
                if j >= 8 and j % TPC == 0:
                    turn_xhat(3, j // TPC - 2, (6, 7))
            pe.wait_ge(w_in, 16 * 12)
            pe.wait_ge(x_ready[3], NT)
            pe.wait_ge(xt_ready[3], NC)
            for j in range(NT):
                mm = pe.matmul(ps[:, 7, j * E:(j + 1) * E], XT[:, PAD + j * P:PAD + (j + 1) * P], router,
                               start=True, stop=True)
            mm.then_inc(logits_made, 1)

            def gate_up(c, i, m):
                k = c * MT + i
                cols = XT[:, PAD + c * CHUNK:PAD + (c + 1) * CHUNK]
                wg = gate[:, m * P:(m + 1) * P] if m < MT_R else sgate[:, (m - MT_R) * P:(m - MT_R + 1) * P]
                wu = upw[:, m * P:(m + 1) * P] if m < MT_R else sup[:, (m - MT_R) * P:(m - MT_R + 1) * P]
                if k >= 2:
                    pe.wait_ge(silu_ready, k - 1)
                pe.matmul(ps[:, k % 2, :], wg, cols, start=True, stop=True).then_inc(g_made, 1)
                if k >= 2:
                    pe.wait_ge(gu_ready, k - 1)
                pe.matmul(ps[:, 2 + k % 2, :], wu, cols, start=True, stop=True).then_inc(u_made, 1)

            def comb_rows(c, m):
                k = c * MT_R + m
                if k >= 1:
                    pe.wait_ge(hid_ready, c * MT_R + m)
                pe.matmul(ps[:, 4, :], spread[:, m, :], combT[:, c * CHUNK:(c + 1) * CHUNK],
                          start=True, stop=True).then_inc(cb_made, 1)

            def down_proj(c):
                pe.wait_ge(hid_ready, (c + 1) * MT_R)
                pe.wait_ge(gu_ready, (c + 1) * MT)
                if c >= 1:
                    pe.wait_ge(y_ready, c)
                for i in range(TPC):
                    for m in range(MT):
                        wd = down[:, m, :] if m < MT_R else sdown[:, m - MT_R, :]
                        mm = pe.matmul(ps[:, 5, i * P:(i + 1) * P], hid[:, c % 2, m, i * P:(i + 1) * P], wd,
                                       start=(m == 0), stop=(m == MT - 1))
                mm.then_inc(down_made, 1)

            ORDER = [4, 5, 0, 1, 2, 3]
            for c in range(NC):
                for i, m in enumerate(range(MT)):
                    gate_up(c, i, ORDER[i])
                    if c == 0 and i == 1:
                        pe.wait_ge(comb_ready, 1)
                        for j in range(NT):
                            mm = pe.transpose(ps[:, 6, :].bitcast(BF16)[0:48, j % 8 * P:(j % 8 + 1) * P] if j < 8 else
                                              ps[:, 7, :].bitcast(BF16)[0:48, j % 8 * P:(j % 8 + 1) * P],
                                              combp[:, j, :], identb[:, :])
                        mm.then_inc(comb_turned, 1)
                    if i >= 2:
                        if c == 0 and i == 2:
                            pe.wait_ge(combT_ready, 2)
                        comb_rows(c, ORDER[i])
                down_proj(c)

        @block.scalar
        def _(act):
            def keep_xt(n, c, banks):
                act.wait_ge(turned[n], c + 1)
                dst = XT[:, PAD + c * CHUNK:PAD + (c + 1) * CHUNK]
                src = ps[:, banks[c % 2], :]
                if n == 0:
                    act.activation(dst, src, ACT.Identity, bias=BETA, scale=GAMMA).then_inc(xt_ready[n], 1)
                else:
                    act.activation(dst, src, ACT.Copy).then_inc(xt_ready[n], 1)

            def high_part(n, c, s):
                act.wait_ge(qk_made[n], 2 * c + s + 1)
                act.activation(parts[:, s, HIGH, c * CHUNK:(c + 1) * CHUNK], ps[:, 2 + s, :], ACT.Copy)\
                   .then_inc(high_ready[n], 1)

            def keep_values(n, k):
                blocks = NB if n == 0 else NT
                act.wait_ge(v_made[n], k + 1)
                n4 = min(4, blocks - 4 * k)
                for b in range(4 * k, 4 * k + n4):
                    nk = min(P, WK - b * QB) if n == 0 else P
                    ins = act.activation(V[0:nk, b, :, 0:HD],
                                         ps[0:nk, 4 + k % 2, b % 4 * P:(b % 4 + 1) * P].rearrange("p (h d) -> p h d", h=H),
                                         ACT.Copy)
                ins.then_inc(v_ready[n], 1)

            act.wait_ge(w_in, 16 * 3)
            for c in range(NC):
                keep_xt(0, c, (0, 1))
                if c >= 1:
                    high_part(0, c - 1, 0)
                    high_part(0, c - 1, 1)
            high_part(0, NC - 1, 0)
            high_part(0, NC - 1, 1)
            for k in range(-(-NB // 4)):
                keep_values(0, k)

            act.wait_ge(v_made[0], -(-NB // 4))
            act.wait_ge(low_ready[0], 2 * NC)
            act.wait_ge(parts_kept[0], 2 * NC * 16)

            def exps(t, g):
                act.wait_ge(b_made[0], t * HG + g + 1)
                if not isinstance(t, int) or t >= 1:
                    act.wait_ge(pv_done[0], t * HG + g - HG + 1)
                act.activation(PR[:, g, 0:HG * QB], ps[:, 2 + g % 2, 0:HG * QB], ACT.Exp, scale=HD ** -0.5)\
                   .then_inc(exp_done[0], 1)

            def keep_sums(t, par, nq=QB):
                act.wait_ge(pv_done[0], (t + 1) * HG)
                act.activation(OT[:, :, bass.ds(t * QB, nq)],
                               ps[:, 4 + par, 0:G * QB].rearrange("p (g n) -> p g n", g=G)[:, :, 0:nq],
                               ACT.Copy).then_inc(o_kept[0], 1)

            for g in range(G):
                exps(0, g)
            with act.Fori(1, NB - 1, 2) as t:
                for d in range(2):
                    exps(t + d, 0)
                    exps(t + d, 1)
                    keep_sums(t + (d - 1), d)
                    exps(t + d, 2)
                    exps(t + d, 3)
            exps(NB - 1, 0)
            exps(NB - 1, 1)
            keep_sums(NB - 2, NB % 2)
            exps(NB - 1, 2)
            exps(NB - 1, 3)
            keep_sums(NB - 1, (NB - 1) % 2, T - (NB - 1) * QB)

            def turn_back(n, j):
                act.wait_ge(on_turned[n], j + 1)
                if j >= 2:
                    act.wait_ge(proj_made[n], j - 1)
                act.activation(OnT[:, j % 2, :], ps[:, 2 + j % 2, 0:P], ACT.Copy).then_inc(ont_ready[n], 1)

            for j in range(NT + TPC + 1):
                if j < NT:
                    turn_back(0, j)
                if j >= 8 and j % TPC == 0:
                    keep_xt(1, j // TPC - 2, (6, 7))
            for c in range(NC):
                act.wait_ge(rk_made, 2 * c + 1)
                if c >= 1:
                    act.wait_ge(x_ready[2], c)
                act.activation(mix[:, 4, :], ps[:, 0, :], ACT.Sigmoid).then_inc(sig_ready, 1)
                act.wait_ge(rk_made, 2 * c + 2)
                if c >= 1:
                    act.wait_ge(kact_ready, c)
                act.activation(mix[:, 2, :], ps[:, 1, :], ACT.Relu).then_inc(relu_ready, 1)
            for c in range(NC):
                keep_xt(2, c, (6, 7))
                if c >= 1:
                    high_part(1, c - 1, 0)
                    high_part(1, c - 1, 1)
            high_part(1, NC - 1, 0)
            high_part(1, NC - 1, 1)
            act.wait_ge(x_ready[2], NC)
            for k in range(NT // 4):
                keep_values(1, k)
            act.wait_ge(v_made[1], NT // 4)
            act.wait_ge(low_ready[1], 2 * NC)
            act.wait_ge(parts_kept[1], 2 * NC * 16)

            def exp_round(r, first):
                for b in range(8):
                    act.wait_ge(b_made[1], r * 8 + b + 1)
                    if b % 4 == 0 and not first:
                        act.wait_ge(pv_done[1], r * 2 + b // 4 - 1)
                    act.activation(PR[:, b, :], ps[:, 4 + b % 2, :], ACT.Exp, scale=HD ** 0.5)\
                       .then_inc(exp_done[1], 1)

            exp_round(0, True)
            with act.Fori(1, NC * G * NT // 2) as r:
                exp_round(r, False)
            for j in range(NT + TPC + 1):
                if j < NT:
                    turn_back(1, j)
                if j >= 8 and j % TPC == 0:
                    keep_xt(3, j // TPC - 2, (6, 7))
            act.wait_ge(logits_made, 1)
            act.activation(rt[:, 0, :, :], ps[:, 7, 0:NT * E].rearrange("p (t e) -> p t e", t=NT), ACT.Sigmoid)\
               .then_inc(scores_ready, 1)
            for k in range(NC * MT):
                act.wait_ge(g_made, k + 1)
                if k >= 2:
                    act.wait_ge(gu_ready, k - 1)
                act.activation(silu[:, k % 2, :], ps[:, k % 2, :], ACT.Silu).then_inc(silu_ready, 1)
                if k == 1:
                    act.wait_ge(comb_turned, 1)
                    act.wait_ge(zeroed[1], 1)
                    for i in range(2):
                        act.activation(combT[0:48, i * 1024:(i + 1) * 1024], ps[0:48, 6 + i, :].bitcast(BF16),
                                       ACT.Copy).then_inc(combT_ready, 1)

        @block.vector
        def _(v):
            chain = Count(v, dve)

            def stat(n, c):
                t0 = c * TPC
                for i in range(TPC):
                    if n in (1, 3):
                        v.wait_ge(x_ready[n], t0 + i + 1)
                    chain.up(v.bn_stats(stats[:, i, :], X[:, t0 + i, :]))
                chain.settle()
                for i in range(TPC):
                    ins = v.bn_aggr(mv[:, t0 + i, :], stats[:, i, :])
                    if i < TPC - 1:
                        chain.up(ins)
                ins.then_inc(stats_ready[n], 1)
                v.wait_ge(stats_ready[n], c + 1)
                chain.settle()

            def normalise(n, c):
                v.wait_ge(rstd_ready[n], c + 1)
                if c >= 2:
                    v.wait_ge(turned[n], c - 1)
                for i in range(TPC):
                    t = c * TPC + i
                    ins = v.tensor_scalar(xhat[:, c % 2, i, :], X[:, t, :], mv[:, t, 0:1], rs[:, t:t + 1],
                                          ALU.subtract, ALU.mult)
                    if i < TPC - 1:
                        chain.up(ins)
                ins.then_inc(xhat_ready[n], 1)

            def residual_part(n, k):
                c, s = k // 2, k % 2
                v.wait_ge(qk_made[n], k + 1)
                v.wait_ge(high_ready[n], k + 1)
                if k >= 2:
                    v.wait_ge(low_ready[n], k - 1)
                v.tensor_tensor(resid[:, k % 2, :], ps[:, 2 + s, :], parts[:, s, HIGH, c * CHUNK:(c + 1) * CHUNK],
                                ALU.subtract).then_inc(resid_ready[n], 1)

            chain.up(v.memset(mparts[:, :], 0.0))
            for c in range(NC):
                v.wait_ge(x_in[c], 16)
                stat(0, c)
            v.wait_ge(w_in, 48)
            v.tensor_scalar(vecs[:, 4:6], vecs[:, 2:4], -1.0, 1.0, ALU.mult, ALU.add).then_inc(om_ready, 1)
            for c in range(NC):
                normalise(0, c)
                v.wait_ge(xhat_ready[0], c + 1)
                chain.settle()
                for i in range(TPC):
                    t = c * TPC + i
                    ins = v.tensor_scalar(X[:, t, :], X[:, t, :], tmp4[:, 1, t:t + 1], tmp4[:, 2, t:t + 1],
                                          ALU.mult, ALU.add)
                    if i < TPC - 1:
                        chain.up(ins)
                ins.then_inc(resid_in_x, 1)
                if c >= 1:
                    residual_part(0, 2 * c - 2)
                    residual_part(0, 2 * c - 1)
            residual_part(0, 2 * NC - 2)
            residual_part(0, 2 * NC - 1)

            def max_parts(n, src, rows, cnt):
                m = mparts[0:rows, 0:48]
                if n == 0:
                    view = m.rearrange("p (i h) -> p i h", i=3)
                    part = [view[:, i, :] for i in range(3)]
                    res = negres[0:rows, :]
                else:
                    view = m.rearrange("p (h i q) -> p i h q", h=HG, i=3)
                    part = [view[:, i, :, :] for i in range(3)]
                    res = negres[0:rows, :].rearrange("p (h q) -> p h q", h=HG)
                chain.up(v.tensor_scalar(part[HIGH], src, -1.0, None, ALU.mult))
                chain.settle()
                chain.up(v.scalar_tensor_tensor(out=res, in0=src, scalar=-1.0, in1=part[HIGH],
                                                op0=ALU.mult, op1=ALU.subtract))
                chain.settle()
                chain.up(v.tensor_copy(part[MID], res))
                chain.settle()
                v.tensor_tensor(part[LOW], res, part[MID], ALU.subtract).then_inc(mparts_ready[n], 1)

            v.wait_ge(v_ready[0], -(-NB // 4))
            v.memset(ps[:, 4:6, :], 0.0).then_inc(zeroed[0], 1)
            base0 = chain.n

            def maxima(t, copy):
                for g in range(G):
                    v.wait_ge(a_made[0], t * G + g + 1)
                    v.tensor_reduce(rawmax[0:QB, 0, g * HG:(g + 1) * HG],
                                    ps[0:QB, g % 2, :].rearrange("p (h n) -> p h n", h=HG), AX.X, ALU.max)\
                     .then_inc(a_read[0], 1)
                    if g == 1 and copy:
                        keep_row(t - 1)
                v.wait_ge(a_read[0], t * G + G)
                chain.n = base0 + t * 3
                max_parts(0, rawmax[0:QB, 0, 0:H], QB, H)
                v.wait_ge(mparts_ready[0], t + 1)

            def keep_row(t):
                v.wait_ge(mt_made[0], t + 1)
                if not isinstance(t, int) or t >= 1:
                    v.wait_ge(mrow_in[0], t * 48)
                v.tensor_copy(mrow[:, 0:QB], ps[:, 6, :].bitcast(BF16)[0:48, 0:QB]).then_inc(mrow_ready[0], 1)

            maxima(0, False)
            maxima(1, True)
            with v.Fori(2, NB) as t:
                maxima(t, True)
            keep_row(NB - 1)
            chain.n = base0 + 3 * NB

            def normed(n, j):
                v.wait_ge(o_turned[n], j + 1)
                bank = ps[:, j % 2, :].rearrange("p (h n) -> p h n", h=H)
                chain.up(v.reciprocal(rz[:, j % 2, :], bank[:, :, HD]))
                chain.settle()
                if j >= 2:
                    v.wait_ge(on_turned[n], j - 1)
                v.tensor_tensor(On[:, j % 2, :].rearrange("p (h d) -> p h d", h=H), bank[:, :, 0:HD],
                                rz[:, j % 2, :].unsqueeze(2).to_broadcast([P, H, HD]), ALU.mult).then_inc(on_ready[n], 1)

            def add_proj(n, j):
                v.wait_ge(proj_made[n], j + 1)
                v.tensor_tensor(X[:, j, :], ps[:, 4 + j % 2, 0:P], X[:, j, :], ALU.add).then_inc(x_ready[2 * n + 1], 1)

            v.wait_ge(pv_done[0], HG * NB)
            chain.up(v.memset(XT[:, 0:PAD], 0.0))
            for j in range(NT + 4):
                if j < NT:
                    normed(0, j)
                if 2 <= j < NT + 2:
                    add_proj(0, j - 2)
                if j >= 5 and (j - 5) % TPC == 0:
                    stat(1, (j - 5) // TPC)
                if j >= 7 and (j - 7) % TPC == 0:
                    normalise(1, (j - 7) // TPC)
            v.wait_ge(om_ready, 1)
            for c in range(NC):
                x0 = PAD + c * CHUNK
                cur, prev = XT[:, x0:x0 + CHUNK], XT[:, x0 - 1:x0 - 1 + CHUNK]
                v.wait_ge(xt_ready[1], c + 1)
                for s, (mu, om) in enumerate(((MU_R, OM_R), (MU_K, OM_K))):
                    if c >= 1:
                        v.wait_ge(rk_made, 2 * c - 1 + s)
                    chain.up(v.tensor_scalar(mix[:, 5, :], prev, om, None, ALU.mult))
                    chain.settle()
                    v.scalar_tensor_tensor(out=mix[:, s, :], in0=cur, scalar=mu, in1=mix[:, 5, :],
                                           op0=ALU.mult, op1=ALU.add).then_inc(mixed, 1)
                    v.wait_ge(mixed, 2 * c + s + 1)
                v.wait_ge(relu_ready, c + 1)
                if c >= 1:
                    v.wait_ge(vm_made, c)
                v.tensor_tensor(mix[:, 3, :], mix[:, 2, :], mix[:, 2, :], ALU.mult).then_inc(kact_ready, 1)
                v.wait_ge(sig_ready, c + 1)
                v.wait_ge(vm_made, c + 1)
                chain.up(v.tensor_tensor(mix[:, 5, :], ps[:, 2, :], mix[:, 4, :], ALU.mult))
                chain.settle()
                xc = X[:, c * TPC:(c + 1) * TPC, :].rearrange("p t c -> p (t c)")
                v.tensor_tensor(xc, mix[:, 5, :], xc, ALU.add).then_inc(x_ready[2], 1)
                v.wait_ge(x_ready[2], c + 1)
            for c in range(NC):
                stat(2, c)
            for c in range(NC):
                normalise(2, c)
                if c >= 1:
                    residual_part(1, 2 * c - 2)
                    residual_part(1, 2 * c - 1)
            residual_part(1, 2 * NC - 2)
            residual_part(1, 2 * NC - 1)
            v.wait_ge(xt_ready[2], NC)
            v.memset(ps[:, 6, :], 0.0).then_inc(o_kept[1], 1)
            chain.settle()
            base1 = chain.n

            def reduce_tiles(u, par, tiles):
                for k in tiles:
                    v.wait_ge(a_made[1], u * 32 + k + 1)
                    v.tensor_reduce(rawmax[:, par, k:k + 1], ps[:, 2 * (k % 2):2 * (k % 2) + 2, :], AX.XY, ALU.max)\
                     .then_inc(a_read[1], 1)

            def unit_maxima(u, par):
                v.wait_ge(a_read[1], u * 32 + 32)
                chain.n = base1 + u * 4
                halves = rawmax[:, par, :].rearrange("p (a b) -> p a b", b=2)
                chain.up(v.tensor_reduce(rowmax[:, :], halves, AX.X, ALU.max))
                chain.settle()
                max_parts(1, rowmax[:, :].rearrange("p (h q) -> p h q", h=HG), P, 16)
                v.wait_ge(mparts_ready[1], u + 1)
                v.wait_ge(mt_made[1], u + 1)
                if not isinstance(u, int) or u >= 1:
                    v.wait_ge(mrow_in[1], u * 64)
                v.tensor_copy(mrow[:, :], ps[:, 7, :].bitcast(BF16)[0:48, 0:P]).then_inc(mrow_ready[1], 1)

            def keep_unit(u, g, q0):
                v.wait_ge(pv_done[1], u * NT + NT)
                v.tensor_copy(OT[:, g, bass.ds(q0, CHUNK)], ps[:, 6, :]).then_inc(o_kept[1], 1)

            reduce_tiles(0, 0, range(32))
            reduce_tiles(1, 1, range(8))
            unit_maxima(0, 0)
            with v.Fori(0, NC - 1) as qc:
                for g in range(G):
                    u = qc * G + g
                    reduce_tiles(u + 1, (g + 1) % 2, range(8, 32))
                    reduce_tiles(u + 2, g % 2, range(0, 2))
                    unit_maxima(u + 1, (g + 1) % 2)
                    reduce_tiles(u + 2, g % 2, range(2, 8))
                    keep_unit(u, g, qc * CHUNK)
            for g in range(G):
                u = (NC - 1) * G + g
                if g + 1 < G:
                    reduce_tiles(u + 1, (g + 1) % 2, range(8, 32))
                    if g + 2 < G:
                        reduce_tiles(u + 2, g % 2, range(0, 2))
                    unit_maxima(u + 1, (g + 1) % 2)
                    if g + 2 < G:
                        reduce_tiles(u + 2, g % 2, range(2, 8))
                keep_unit(u, g, (NC - 1) * CHUNK)
            chain.n = base1 + 4 * NC * G

            v.wait_ge(bp_added, 1)
            for j in range(NT + 4):
                if j < NT:
                    normed(1, j)
                if 2 <= j < NT + 2:
                    add_proj(1, j - 2)
                if j >= 5 and (j - 5) % TPC == 0:
                    stat(3, (j - 5) // TPC)
                if j >= 7 and (j - 7) % TPC == 0:
                    normalise(3, (j - 7) // TPC)
            v.memset(combT.bitcast(U32), 0).then_inc(zeroed[1], 1)
            v.wait_ge(scores_ready, 1)
            v.wait_ge(w_in, 16 * 12)
            S, SB, WINS, CMP, MASK, SEL, W, TMP = (rt[:, i] for i in range(8))
            gv = lambda x: x.rearrange("p t (g e) -> p (t g) e", g=EG)
            GS = rt[:, 8].rearrange("p t e -> p (t e)")

            def do(ins):
                chain.up(ins)
                chain.settle()

            def small(i):
                return GS[:, 64 * i:64 * (i + 1)]

            do(v.tensor_tensor(SB, S, cbias.unsqueeze(1).to_broadcast([P, NT, E]), ALU.add))
            sb4 = gv(SB)
            t9 = rt[:, 9].rearrange("p t e -> p (t e)")
            big1, lit1 = t9[:, 0:64], t9[:, 64:128]
            big2, lit2 = t9[:, 128:192], t9[:, 192:256]
            chain.up(v.tensor_tensor(big1, sb4[:, :, 0], sb4[:, :, 1], ALU.max))
            chain.up(v.tensor_tensor(lit1, sb4[:, :, 0], sb4[:, :, 1], ALU.min))
            chain.up(v.tensor_tensor(big2, sb4[:, :, 2], sb4[:, :, 3], ALU.max))
            do(v.tensor_tensor(lit2, sb4[:, :, 2], sb4[:, :, 3], ALU.min))
            chain.up(v.tensor_tensor(small(0), big1, big2, ALU.max))
            chain.up(v.tensor_tensor(small(1), big1, big2, ALU.min))
            do(v.tensor_tensor(small(2), lit1, lit2, ALU.max))
            do(v.tensor_tensor(small(1), small(1), small(2), ALU.max))
            do(v.tensor_tensor(small(3), small(0), small(1), ALU.add))

            def wins(score, n, won, cmp):
                do(v.memset(won, 0.0))
                for d in range(1, n):
                    c = cmp[:, :, 0:n - d]
                    do(v.tensor_tensor(c, score[:, :, 0:n - d], score[:, :, d:n], ALU.is_ge))
                    chain.up(v.tensor_tensor(won[:, :, 0:n - d], won[:, :, 0:n - d], c, ALU.add))
                    chain.settle()
                    do(v.scalar_tensor_tensor(out=won[:, :, d:n], in0=won[:, :, d:n], scalar=1.0, in1=c,
                                              op0=ALU.add, op1=ALU.subtract))

            grp = small(3).rearrange("p (t g) -> p t g", g=EG)
            gwon = small(0).rearrange("p (t g) -> p t g", g=EG)
            gcmp = small(1).rearrange("p (t g) -> p t g", g=EG)
            wins(grp, EG, gwon, gcmp)
            do(v.tensor_scalar(small(2), small(0), float(EG - TOPG), None, ALU.is_ge))
            chosen = small(2).unsqueeze(2).to_broadcast([P, NT * EG, E // EG])
            do(v.tensor_copy(gv(MASK), chosen))
            do(v.tensor_tensor(TMP, SB, MASK, ALU.mult))
            do(v.tensor_scalar(CMP, MASK, 1.0, 3e38, ALU.subtract, ALU.mult))
            do(v.tensor_tensor(TMP, TMP, CMP, ALU.add))
            wins(TMP, E, WINS, CMP)
            do(v.tensor_scalar(SEL, WINS, float(E - TOPK), None, ALU.is_ge))
            do(v.tensor_tensor(W, S, SEL, ALU.mult))
            sm = small(0)[:, 0:NT]
            do(v.tensor_reduce(sm, W, AX.X, ALU.add))
            do(v.tensor_scalar(sm, sm, 1e-20, None, ALU.add))
            do(v.reciprocal(small(1)[:, 0:NT], sm))
            do(v.tensor_tensor(W, W, small(1)[:, 0:NT].unsqueeze(2).to_broadcast([P, NT, E]), ALU.mult))
            cp = combp.rearrange("p t (i e) -> p i t e", i=3)
            do(v.tensor_copy(cp[:, HIGH], W))
            do(v.tensor_tensor(TMP, W, cp[:, HIGH], ALU.subtract))
            do(v.tensor_copy(cp[:, MID], TMP))
            v.tensor_tensor(cp[:, LOW], TMP, cp[:, MID], ALU.subtract).then_inc(comb_ready, 1)

            ORDER = [4, 5, 0, 1, 2, 3]
            for c in range(NC):
                for i in range(MT):
                    k = c * MT + i
                    m = ORDER[i]
                    v.wait_ge(silu_ready, k + 1)
                    v.wait_ge(u_made, k + 1)
                    if c >= 2 and i == 0:
                        v.wait_ge(down_made, c - 1)
                    h = hid[:, c % 2, m, :]
                    v.tensor_tensor(h, ps[:, 2 + k % 2, :], silu[:, k % 2, :], ALU.mult).then_inc(gu_ready, 1)
                    if i >= 2:
                        v.wait_ge(gu_ready, k + 1)
                        v.wait_ge(cb_made, c * MT_R + m + 1)
                        v.tensor_tensor(h, ps[:, 4, :], h, ALU.mult).then_inc(hid_ready, 1)
                v.wait_ge(down_made, c + 1)
                xc = X[:, c * TPC:(c + 1) * TPC, :].rearrange("p t c -> p (t c)")
                v.tensor_tensor(xc, ps[:, 5, :], xc, ALU.add).then_inc(y_ready, 1)

        @block.gpsimd
        def _(g_):
            chain = Count(g_, pool)

            def do(ins):
                chain.up(ins)
                chain.settle()

            def rstd(n, c):
                g_.wait_ge(stats_ready[n], c + 1)
                t = slice(c * TPC, (c + 1) * TPC)
                if n:
                    do(g_.tensor_scalar(tmp4[:, 0, t], mv[:, t, 1], EPS, None, ALU.add))
                    g_.tensor_tensor(rs[:, t], tmp4[:, 0, t], half[:, :], ALU.pow).then_inc(rstd_ready[n], 1)
                    return
                do(g_.tensor_scalar(tmp4[:, 0, t], mv[:, t, 1], EPS, None, ALU.add))
                do(g_.tensor_tensor(rs1[:, t], tmp4[:, 0, t], half[:, :], ALU.pow))
                do(g_.tensor_tensor(tmp4[:, 0, t], mv[:, t, 1], rs1[:, t], ALU.mult))
                do(g_.tensor_tensor(tmp4[:, 0, t], tmp4[:, 0, t], rs1[:, t], ALU.mult))
                do(g_.tensor_scalar(tmp4[:, 0, t], tmp4[:, 0, t], EPS, None, ALU.add))
                do(g_.tensor_tensor(tmp4[:, 2, t], tmp4[:, 0, t], half[:, :], ALU.pow))
                do(g_.tensor_tensor(rs[:, t], tmp4[:, 2, t], rs1[:, t], ALU.mult))
                do(g_.tensor_scalar(tmp4[:, 1, t], rs1[:, t], 1.0, None, ALU.add))
                do(g_.tensor_tensor(tmp4[:, 2, t], mv[:, t, 0], rs1[:, t], ALU.mult))
                g_.tensor_scalar(tmp4[:, 2, t], tmp4[:, 2, t], -1.0, None, ALU.mult).then_inc(rstd_ready[n], 1)

            def low_parts(n, k):
                c, s = k // 2, k % 2
                cols = slice(c * CHUNK, (c + 1) * CHUNK)
                g_.wait_ge(resid_ready[n], k + 1)
                g_.tensor_copy(parts[:, s, MID, cols], resid[:, k % 2, :]).then_inc(mid_ready[n], 1)
                g_.wait_ge(mid_ready[n], k + 1)
                g_.tensor_tensor(parts[:, s, LOW, cols], resid[:, k % 2, :], parts[:, s, MID, cols], ALU.subtract)\
                  .then_inc(low_ready[n], 1)

            do(g_.memset(half[:, :], -0.5))
            chain.up(g_.memset(XT[:, 0:PAD], 0.0))
            chain.up(g_.memset(V[:, :, :, HD:VC], 1.0))
            g_.memset(XT[:, PAD + T:WK], 0.0).then_inc(zeroed[0], 1)
            for c in range(NC):
                rstd(0, c)
            for k in range(2 * NC):
                low_parts(0, k)
            for c in range(NC):
                rstd(1, c)
            for c in range(NC):
                rstd(2, c)
            for k in range(2 * NC):
                low_parts(1, k)
            g_.wait_ge(x_ready[2], NC)
            g_.memset(V1[:, :, :, HD:VC], 1.0).then_inc(ones_ready, 1)
            g_.wait_ge(xhat_ready[2], NC)
            g_.wait_ge(w2_in, 16 * 8)
            g_.tensor_tensor(X[:, :, :], X[:, :, :], bp[:, :].unsqueeze(1).to_broadcast([P, NT, C]), ALU.add)\
              .then_inc(bp_added, 1)
            for c in range(NC):
                rstd(3, c)
    return nc


def parts_of(x):
    bf = mybir.dt.np(BF16)
    left, got = np.asarray(x, np.float64), []
    for _ in range(3):
        p = left.astype(np.float32).astype(bf)
        got.append(p)
        left = left - p.astype(np.float64)
    return np.stack(got)


def constants():
    bf = mybir.dt.np(BF16)
    k = {}
    k["ident"] = np.eye(P, dtype=np.float32)
    k["identb"] = np.eye(P, dtype=np.float32).astype(bf)
    q, key = np.arange(QB)[:, None], np.arange(P)[None, :]
    mask = np.where((key - q >= 0) & (key - q <= 2 * HALF), 0.0, MASKED).astype(np.float32)
    k["maskA"] = np.repeat(mask[:, None, :], HG, 1).astype(bf)
    k["maskB"] = np.repeat(mask.T[:, None, :], HG, 1).astype(bf)
    k["ones"] = np.ones((3, H, WK), np.float32).astype(bf)
    k["zeros"] = np.zeros((KR - ROW_MAX, H, WK), np.float32).astype(bf)
    k["edge"] = np.zeros((ROW_BIAS, H, PAD), np.float32).astype(bf)
    edge = np.zeros((3, H, WK), np.float32)
    edge[0, :, 0:PAD] = MASKED
    edge[0, :, PAD + T:] = MASKED
    k["kbias0"] = edge.astype(bf)
    x = (2 ** 8) ** (1.0 / H)
    slopes = np.array([1.0 / x ** (i + 1) for i in range(H)], dtype=np.float32).astype(np.float64)
    bias = np.zeros((3, H, WK), bf)
    bias[:, :, PAD:PAD + T] = parts_of(slopes[:, None] * np.arange(T)[None, :] / np.sqrt(float(HD)))
    k["kbias1"] = bias
    spread = np.zeros((P, MT_R, P), np.float32)
    for i in range(3):
        for e in range(E):
            spread[E * i + e, e // 4, (e % 4) * HE:(e % 4 + 1) * HE] = 1.0
    k["spread"] = spread.astype(bf)
    return k


def kernel(**inputs):
    import numpy as _np
    import concourse.bacc as _bacc
    from concourse import mybir as _mybir
    from concourse.bass_utils import run_bass_kernel_spmd as _run

    f = {n: _np.asarray(x) for n, x in inputs.items()}
    arrays = constants()
    arrays["x"] = f["L0_attn_x"].reshape(T, C)
    arrays["wqkv0"] = f["L0_attn_w_qkv"].T
    arrays["wo0"] = f["L0_attn_w_out"].T
    arrays["vecs"] = _np.stack([f["L0_attn_gamma"], f["L0_attn_beta"], f["L0_ffn_mu_r"], f["L0_ffn_mu_k"]], 1)
    arrays["wmix"] = _np.stack([f["L0_ffn_W_r"].T, f["L0_ffn_W_k"].T, f["L0_ffn_W_v"].T], 1)
    arrays["wqkv1"] = _np.concatenate([f["L1_attn_Wq"].T, f["L1_attn_Wk"].T, f["L1_attn_Wv"].T], 1)
    arrays["wo1"] = f["L1_attn_Wp"].T
    arrays["bp_rows"] = _np.broadcast_to(f["L1_attn_bp"][None, :], (P, C))
    arrays["gate"] = f["L1_ffn_gate_w"].transpose(1, 0, 2).reshape(C, E * HE)
    arrays["up"] = f["L1_ffn_up_w"].transpose(1, 0, 2).reshape(C, E * HE)
    arrays["down"] = f["L1_ffn_down_w"].reshape(MT_R, P, C).transpose(1, 0, 2)
    arrays["sgate"] = f["L1_ffn_shared_gate_w"].T
    arrays["sup"] = f["L1_ffn_shared_up_w"].T
    arrays["sdown"] = f["L1_ffn_shared_down_w"].T.reshape(MT_S, P, C).transpose(1, 0, 2)
    arrays["router"] = f["L1_ffn_router_w"].T
    arrays["cbias"] = _np.broadcast_to(f["L1_ffn_correction_bias"][None, :], (P, E))

    nc = _bacc.Bacc("TRN2", target_bir_lowering=False, num_devices=1)
    given, aps = {}, {}
    for name, v in arrays.items():
        v = _np.ascontiguousarray(v)
        given[f"in_{name}"] = v
        aps[name] = nc.dram_tensor(f"in_{name}", v.shape, _mybir.dt.from_np(v.dtype), kind="ExternalInput").ap()
    out = nc.dram_tensor("out", (T, C), _mybir.dt.from_np(_np.dtype("float32")), kind="ExternalOutput").ap()
    build(nc, aps, out)
    r = _run(nc, [given], core_ids=[0])
    return r.results[0]["out"].reshape(1, T, C)
```

```python
from contextlib import ExitStack

import concourse.bass as bass
import numpy as np
from concourse import mybir

F32 = mybir.dt.float32
BF16 = mybir.dt.bfloat16
U32 = mybir.dt.uint32
ALU = mybir.AluOpType
ACT = mybir.ActivationFunctionType
AX = mybir.AxisListType

P = 128
T, C = 2048, 128
NT = T // P
H, HD = 16, 8
PAD = 16
CHUNK = 512
NC = T // CHUNK
TPC = CHUNK // P
EPS = 1e-5

HIGH, MID, LOW = range(3)
PAIRS = [(HIGH, HIGH), (HIGH, MID), (HIGH, LOW), (MID, HIGH), (MID, MID), (LOW, HIGH)]
RUNS = [[(0, 3, HIGH, 0), (3, 2, MID, 0), (5, 1, LOW, 0)], [(0, 3, HIGH, 1), (3, 2, HIGH, 1), (5, 1, HIGH, 0)]]
ROW_BIAS = HD * len(PAIRS)
ROW_MAX = ROW_BIAS + 3
ROW_PAD = ROW_MAX + 3
KR = 96
WK = PAD + T + PAD

HALF = 16
QB = P - 2 * HALF
NB = -(-T // QB)
G = 4
HG = H // G
VC = HD + 1
MASKED = -1e30

E, TOPK, EG, TOPG, HE, HS = 16, 4, 4, 2, 32, 256
MT_R = E * HE // P
MT_S = HS // P
MT = MT_R + MT_S


class Count:

    def __init__(self, eng, sem, base=0):
        self.eng, self.sem, self.n = eng, sem, base

    def up(self, ins):
        ins.then_inc(self.sem, 1)
        self.n = self.n + 1

    def settle(self):
        self.eng.wait_ge(self.sem, self.n)


def build(nc, a, out):
    ctx = ExitStack()
    with ctx:
        def sb(name, shape, dt=F32):
            return ctx.enter_context(nc.sbuf_tensor(name, shape, dt))

        def sem(name):
            return ctx.enter_context(nc.semaphore(name))

        QA = sb("QA", [P, H, T], BF16)
        KA = sb("KA", [P, H, WK], BF16)
        X = sb("X", [P, NT, C])
        big = sb("big", [P, G * T])
        OT = big[:, :].rearrange("p (g n) -> p g n", g=G)
        parts = big[:, 0:3 * T].bitcast(BF16).rearrange("p (s i n) -> p s i n", s=2, i=3)
        V = sb("V", [P, NB, H, VC])
        V1 = V[:, 0:NT, :, :]
        ring = sb("ring", [P, 8 * CHUNK + 64])
        PR = ring[:, 0:8 * CHUNK].rearrange("p (b n) -> p b n", b=8)
        XT = ring[:, 0:WK]
        xhat = ring[:, WK:WK + 2 * CHUNK].rearrange("p (b t c) -> p b t c", b=2, t=TPC)
        resid = ring[:, WK + 2 * CHUNK:WK + 4 * CHUNK].rearrange("p (b n) -> p b n", b=2)
        vflat = V[:, :, :, :].rearrange("p a b c -> p (a b c)")
        mix = vflat[:, 0:6 * CHUNK].rearrange("p (b n) -> p b n", b=6)
        On = vflat[:, 0:2 * C].rearrange("p (b c) -> p b c", b=2)
        OnT = vflat[:, 2 * C:4 * C].rearrange("p (b c) -> p b c", b=2)

        wqkv = [sb("wqkv0", [P, 3 * C]), sb("wqkv1", [P, 3 * C])]
        wo = [sb("wo0", [P, C]), sb("wo1", [P, C])]
        wmix = sb("wmix", [P, 3, C])
        vecs = sb("vecs", [P, 6])
        GAMMA, BETA, MU_R, MU_K, OM_R, OM_K = (vecs[:, i:i + 1] for i in range(6))
        ident = sb("ident", [P, P])
        identb = sb("identb", [P, P], BF16)
        maskA = sb("maskA", [P, HG, P], BF16)
        maskB = sb("maskB", [P, HG, QB], BF16)
        bp = sb("bp", [P, C])
        half = sb("half", [P, TPC])
        stats = sb("stats", [P, TPC, 6])
        mv = sb("mv", [P, NT, 2])
        rs = sb("rs", [P, NT])
        rs1 = sb("rs1", [P, NT])
        tmp4 = sb("tmp4", [P, 3, NT])
        rawmax = sb("rawmax", [P, 2, 32])
        rowmax = sb("rowmax", [P, 16])
        negres = sb("negres", [P, 16])
        mparts = sb("mparts", [P, P], BF16)
        zero16 = sb("zero16", [P, 16])
        minus_max = sb("minus_max", [P, 16])
        mrow = sb("mrow", [48, P], BF16)
        rz = sb("rz", [P, 2, H])

        qaf = QA[:, :, :].rearrange("p h n -> p (h n)").bitcast(F32)
        gate = qaf[:, 0:512]
        upw = qaf[:, 512:1024]
        down = qaf[:, 1024:1536].rearrange("p (m c) -> p m c", m=MT_R)
        sgate = qaf[:, 1536:1792]
        sup = qaf[:, 1792:2048]
        sdown = qaf[:, 2048:2304].rearrange("p (m c) -> p m c", m=MT_S)
        router = qaf[:, 2304:2320]
        cbias = qaf[:, 2320:2336]
        spread = qaf[:, 2336:2336 + 256].bitcast(BF16).rearrange("p (m n) -> p m n", m=MT_R)
        combT = qaf[:, 2600:2600 + T // 2].bitcast(BF16)
        silu = qaf[:, 3700:3700 + 2 * CHUNK].rearrange("p (b n) -> p b n", b=2)
        hid = qaf[:, 4800:4800 + 2 * MT * CHUNK].rearrange("p (b m n) -> p b m n", b=2, m=MT)
        rt = qaf[:, 11000:11000 + 12 * NT * E].rearrange("p (b t e) -> p b t e", b=12, t=NT)
        combp = qaf[:, 14200:14200 + NT * 24].bitcast(BF16).rearrange("p (t i) -> p t i", t=NT)

        ps = ctx.enter_context(nc.psum_tensor("ps", [P, 8, CHUNK], F32))

        q_kept = nc.dram_tensor("q_kept", [3, HD, H, T], BF16).ap()
        k_kept = nc.dram_tensor("k_kept", [3, HD, H, WK], BF16).ap()

        x_d = a["x"].rearrange("(c t p) n -> c p t n", c=NC, p=P)
        out_d = out.rearrange("(c t p) n -> c p t n", c=NC, p=P)

        x_in = [sem(f"x_in{c}") for c in range(NC)]
        w_in = sem("w_in")
        w2_in = sem("w2_in")
        bp_added = sem("bp_added")
        ones_ready = sem("ones_ready")
        om_ready = sem("om_ready")
        x_ready = [None] + [sem(f"x_ready{n}") for n in (1, 2, 3)]
        stats_ready = [sem(f"stats_ready{n}") for n in range(4)]
        rstd_ready = [sem(f"rstd_ready{n}") for n in range(4)]
        xhat_ready = [sem(f"xhat_ready{n}") for n in range(4)]
        turned = [sem(f"turned{n}") for n in range(4)]
        xt_ready = [sem(f"xt_ready{n}") for n in range(4)]
        dve = sem("dve")
        pool = sem("pool")
        resid_in_x = sem("resid_in_x")

        L = range(2)
        qk_made = [sem(f"qk_made{n}") for n in L]
        high_ready = [sem(f"high_ready{n}") for n in L]
        resid_ready = [sem(f"resid_ready{n}") for n in L]
        mid_ready = [sem(f"mid_ready{n}") for n in L]
        low_ready = [sem(f"low_ready{n}") for n in L]
        v_made = [sem(f"v_made{n}") for n in L]
        v_ready = [sem(f"v_ready{n}") for n in L]
        parts_kept = [sem(f"parts_kept{n}") for n in L]
        rows_in = [sem(f"rows_in{n}") for n in L]
        qk_in = [[sem(f"qk_in{n}_{g}") for g in range(G)] for n in L]
        zeroed = [sem(f"zeroed{n}") for n in L]
        a_made = [sem(f"a_made{n}") for n in L]
        a_read = [sem(f"a_read{n}") for n in L]
        mparts_ready = [sem(f"mparts_ready{n}") for n in L]
        mid_max = sem("mid_max")
        rowmax_ready = sem("rowmax_ready")
        mt_made = [sem(f"mt_made{n}") for n in L]
        mrow_ready = [sem(f"mrow_ready{n}") for n in L]
        mrow_in = [sem(f"mrow_in{n}") for n in L]
        b_made = [sem(f"b_made{n}") for n in L]
        exp_done = [sem(f"exp_done{n}") for n in L]
        pv_done = [sem(f"pv_done{n}") for n in L]
        o_kept = [sem(f"o_kept{n}") for n in L]
        o_turned = [sem(f"o_turned{n}") for n in L]
        on_ready = [sem(f"on_ready{n}") for n in L]
        on_turned = [sem(f"on_turned{n}") for n in L]
        ont_ready = [sem(f"ont_ready{n}") for n in L]
        proj_made = [sem(f"proj_made{n}") for n in L]

        mixed = sem("mixed")
        rk_made = sem("rk_made")
        sig_ready = sem("sig_ready")
        relu_ready = sem("relu_ready")
        kact_ready = sem("kact_ready")
        vm_made = sem("vm_made")

        logits_made = sem("logits_made")
        scores_ready = sem("scores_ready")
        comb_ready = sem("comb_ready")
        comb_turned = sem("comb_turned")
        combT_ready = sem("combT_ready")
        g_made = sem("g_made")
        u_made = sem("u_made")
        silu_ready = sem("silu_ready")
        gu_ready = sem("gu_ready")
        cb_made = sem("cb_made")
        hid_ready = sem("hid_ready")
        down_made = sem("down_made")
        y_ready = sem("y_ready")
        stored = sem("stored")

        block = ctx.enter_context(nc.Block())

        @block.sync
        def _(sp):
            def weight(dst, src, s=w_in):
                sp.dma_start(dst, src).then_inc(s, 16)

            sp.dma_start(X[:, 0:TPC, :], x_d[0]).then_inc(x_in[0], 16)
            weight(ident[:, :], a["ident"])
            weight(vecs[:, 0:4], a["vecs"])
            weight(wqkv[0][:, :], a["wqkv0"])
            for c in range(1, NC):
                sp.dma_start(X[:, c * TPC:(c + 1) * TPC, :], x_d[c]).then_inc(x_in[c], 16)
            weight(identb[:, :], a["identb"], w2_in)
            weight(maskA[:, :, :], a["maskA"], w2_in)
            weight(maskB[:, :, :], a["maskB"], w2_in)
            weight(wo[0][:, :], a["wo0"], w2_in)
            weight(wmix[:, :, :], a["wmix"], w2_in)
            weight(wqkv[1][:, :], a["wqkv1"], w2_in)
            weight(wo[1][:, :], a["wo1"], w2_in)
            weight(bp[:, :], a["bp_rows"], w2_in)

            def operands(n):
                if n == 1:
                    sp.wait_ge(b_made[0], NB * HG)
                    sp.wait_ge(mrow_in[0], 48 * NB)
                if n == 0:
                    sp.dma_start(QA[ROW_BIAS:ROW_BIAS + 3, :, :], a["ones"][:, :, 0:T]).then_inc(rows_in[n], 16)
                    sp.dma_start(QA[ROW_MAX:KR, :, :], a["zeros"][:, :, 0:T]).then_inc(rows_in[n], 16)
                    sp.dma_start(KA[ROW_PAD:KR, :, :], a["zeros"][0:KR - ROW_PAD]).then_inc(rows_in[n], 16)
                    for s in (slice(0, PAD), slice(PAD + T, WK)):
                        sp.dma_start(k_kept[:, :, :, s].rearrange("i d h n -> (i d h) n"), a["edge"])\
                          .then_inc(rows_in[n], 16)
                    sp.dma_start(KA[ROW_MAX:ROW_MAX + 3, :, :], a["ones"]).then_inc(rows_in[n], 16)
                else:
                    sp.dma_start(QA[ROW_MAX:ROW_MAX + 3, :, :], a["zeros"][0:3, :, 0:T]).then_inc(rows_in[n], 16)
                sp.dma_start(KA[ROW_BIAS:ROW_BIAS + 3, :, :], a[f"kbias{n}"]).then_inc(rows_in[n], 16)
                for c in range(NC):
                    cols = slice(c * CHUNK, (c + 1) * CHUNK)
                    for s in range(2):
                        sp.wait_ge(high_ready[n], 2 * c + s + 1)
                        sp.wait_ge(low_ready[n], 2 * c + s + 1)
                        kept = q_kept if s == 0 else k_kept[:, :, :, PAD:PAD + T]
                        sp.dma_start(kept[:, :, :, cols].rearrange("i d h n -> (d h) i n"), parts[:, s, :, cols])\
                          .then_inc(parts_kept[n], 16)
                sp.wait_ge(rows_in[n], 16 * 7 if n == 0 else 32)
                sp.wait_ge(parts_kept[n], 2 * NC * 16)
                for g in range(G):
                    for s in range(2):
                        kept, rows_of = (q_kept, QA) if s == 0 else (k_kept, KA)
                        heads = slice(g * HG, (g + 1) * HG)
                        for first, n_pairs, part, step in RUNS[s]:
                            if step:
                                src = kept[part:part + n_pairs, :, heads, :].rearrange("i d h n -> i d (h n)")
                            else:
                                src = kept[part, :, heads, :].rearrange("d h n -> d (h n)").unsqueeze(0)\
                                    .to_broadcast([n_pairs, HD, HG * (T if s == 0 else WK)])
                            rows = slice(HD * first, HD * (first + n_pairs))
                            dst = rows_of[rows, heads, :].rearrange("p h n -> p (h n)")
                            sp.dma_start(dst, src).then_inc(qk_in[n][g], 16)

            operands(0)
            for t in range(NB):
                sp.wait_ge(mrow_ready[0], t + 1)
                nq = min(QB, T - t * QB)
                for i in range(3):
                    sp.dma_start(QA[ROW_MAX + i:ROW_MAX + i + 1, :, t * QB:t * QB + nq],
                                 mrow[16 * i:16 * i + 16, 0:nq]).then_inc(mrow_in[0], 16)
            operands(1)
            with sp.Fori(0, NC) as qc:
                for g in range(G):
                    sp.wait_ge(mrow_ready[1], qc * G + g + 1)
                    for hh in range(HG):
                        sp.dma_start(QA[ROW_MAX:ROW_MAX + 3, g * HG + hh, bass.ds(qc * CHUNK, CHUNK)],
                                     mrow[12 * hh:12 * hh + 12, :]).then_inc(mrow_in[1], 16)
            sp.wait_ge(b_made[1], NC * G * NT * HG)
            for dst, name in ((gate, "gate"), (upw, "up"), (down, "down"), (sgate, "sgate"), (sup, "sup"),
                              (sdown, "sdown"), (router, "router"), (cbias, "cbias"), (spread, "spread")):
                sp.dma_start(dst, a[name]).then_inc(w_in, 16)
            for c in range(NC):
                sp.wait_ge(y_ready, c + 1)
                sp.dma_start(out_d[c], X[:, c * TPC:(c + 1) * TPC, :]).then_inc(stored, 16)
            sp.wait_ge(stored, 16 * NC)

        @block.tensor
        def _(pe):
            def turn_xhat(n, c, banks):
                pe.wait_ge(xhat_ready[n], c + 1)
                if c >= 2:
                    pe.wait_ge(xt_ready[n], c - 1)
                for i in range(TPC):
                    mm = pe.transpose(ps[:, banks[c % 2], i * P:(i + 1) * P], xhat[:, c % 2, i, :], ident[:, :])
                mm.then_inc(turned[n], 1)

            def qk(n, c):
                pe.wait_ge(xt_ready[2 * n], c + 1)
                for s in range(2):
                    if c >= 1:
                        pe.wait_ge(resid_ready[n], 2 * (c - 1) + s + 1)
                        pe.wait_ge(high_ready[n], 2 * (c - 1) + s + 1)
                    pe.matmul(ps[:, 2 + s, :], wqkv[n][:, s * C:(s + 1) * C],
                              XT[:, PAD + c * CHUNK:PAD + (c + 1) * CHUNK], start=True, stop=True).then_inc(qk_made[n], 1)

            def values(n, blocks):
                for b in blocks:
                    k = b // 4
                    if b % 4 == 0 and k >= 2:
                        pe.wait_ge(v_ready[n], k - 1)
                    first = b * QB if n == 0 else PAD + b * P
                    nk = min(P, WK - first)
                    mm = pe.matmul(ps[0:nk, 4 + k % 2, (b % 4) * P:(b % 4 + 1) * P], XT[:, first:first + nk],
                                   wqkv[n][:, 2 * C:3 * C], start=True, stop=True)
                    if b % 4 == 3 or b == (NB if n == 0 else NT) - 1:
                        mm.then_inc(v_made[n], 1)

            pe.wait_ge(w_in, 16 * 3)
            for c in range(NC):
                turn_xhat(0, c, (0, 1))
                if c >= 1:
                    qk(0, c - 1)
            qk(0, NC - 1)
            pe.wait_ge(zeroed[0], 1)
            values(0, range(NB))

            def project(n, j):
                if j < NT:
                    if j >= 2:
                        pe.wait_ge(on_ready[n], j - 1)
                    for g in range(G):
                        mm = pe.transpose(ps[:, j % 2, g * P:(g + 1) * P], OT[:, g, j * P:(j + 1) * P], ident[:, :])
                    mm.then_inc(o_turned[n], 1)
                k = j - 1
                if 0 <= k < NT:
                    pe.wait_ge(on_ready[n], k + 1)
                    if k >= 2:
                        pe.wait_ge(ont_ready[n], k - 1)
                    pe.transpose(ps[:, 2 + k % 2, 0:P], On[:, k % 2, :], ident[:, :]).then_inc(on_turned[n], 1)
                k = j - 2
                if 0 <= k < NT:
                    pe.wait_ge(ont_ready[n], k + 1)
                    if k >= 2:
                        pe.wait_ge(x_ready[2 * n + 1], k - 1)
                    pe.matmul(ps[:, 4 + k % 2, 0:P], OnT[:, k % 2, :], wo[n][:, :],
                              start=True, stop=True).then_inc(proj_made[n], 1)

            pe.wait_ge(w2_in, 16 * 8)
            pe.wait_ge(rows_in[0], 16 * 7)
            pe.wait_ge(xt_ready[0], NC)
            pe.wait_ge(low_ready[0], 2 * NC)
            pe.wait_ge(v_ready[0], -(-NB // 4))
            pe.wait_ge(zeroed[0], 2)

            def a_scores(t, g):
                nq, k = min(QB, T - t * QB), HG * t + g
                nk = min(P, WK - t * QB)
                if t == 0:
                    pe.wait_ge(qk_in[0][g], 16 * 6)
                if k >= 2:
                    pe.wait_ge(a_read[0], k - 1)
                bank = ps[0:nq, g % 2, :].rearrange("p (h n) -> p h n", h=HG)
                pe.matmul(bank, identb[:, 0:nq], maskA[:, :, :], start=True, stop=False, skip_group_check=True)
                for hh in range(HG):
                    h = g * HG + hh
                    mm = pe.matmul(bank[:, hh, 0:nk], QA[0:KR, h, t * QB:t * QB + nq], KA[0:KR, h, t * QB:t * QB + nk],
                                   start=False, stop=True, skip_group_check=True)
                mm.then_inc(a_made[0], 1)

            def b_scores(t, g):
                nq, k = min(QB, T - t * QB), HG * t + g
                nk = min(P, WK - t * QB)
                if g == 0:
                    pe.wait_ge(mrow_in[0], 48 * (t + 1))
                if k >= 2:
                    pe.wait_ge(exp_done[0], k - 1)
                bank = ps[0:nk, 2 + g % 2, 0:HG * QB].rearrange("p (h n) -> p h n", h=HG)
                pe.matmul(bank, identb[:, 0:nk], maskB[:, :, :], start=True, stop=False, skip_group_check=True)
                for hh in range(HG):
                    h = g * HG + hh
                    mm = pe.matmul(bank[:, hh, 0:nq], KA[0:KR, h, t * QB:t * QB + nk], QA[0:KR, h, t * QB:t * QB + nq],
                                   start=False, stop=True, skip_group_check=True)
                mm.then_inc(b_made[0], 1)

            def sums(t, g):
                nq, k = min(QB, T - t * QB), HG * t + g
                nk = min(P, WK - t * QB)
                pe.wait_ge(exp_done[0], k + 1)
                if g == 0 and t >= 2:
                    pe.wait_ge(o_kept[0], t - 1)
                for hh in range(HG):
                    mm = pe.matmul(ps[32 * hh:32 * hh + VC, 4 + t % 2, g * QB:g * QB + nq], V[0:nk, t, g * HG + hh, :],
                                   PR[0:nk, g, hh * QB:hh * QB + nq], start=True, stop=True, skip_group_check=True)
                mm.then_inc(pv_done[0], 1)

            LEAD = 3
            for i in range(NB + LEAD + 1):
                for g in range(G):
                    if i < NB:
                        a_scores(i, g)
                    if g == 1 and 1 <= i <= NB:
                        pe.wait_ge(mparts_ready[0], i)
                        if i >= 2:
                            pe.wait_ge(mrow_ready[0], i - 1)
                        pe.transpose(ps[:, 6, :].bitcast(BF16)[0:48, 0:QB], mparts[0:QB, 0:48],
                                     identb[0:QB, 0:QB]).then_inc(mt_made[0], 1)
                    if LEAD <= i < NB + LEAD:
                        b_scores(i - LEAD, g)
                    k = HG * (i - LEAD) + g - 1
                    if 0 <= k < HG * NB:
                        sums(k // HG, k % HG)

            pe.wait_ge(o_kept[0], NB)
            for j in range(NT + TPC + 1):
                project(0, j)
                if j >= 8 and j % TPC == 0:
                    turn_xhat(1, j // TPC - 2, (6, 7))
            def receptance_keys(c):
                pe.wait_ge(mixed, 2 * c + 1)
                if c == 0:
                    pe.wait_ge(x_ready[1], NT)
                else:
                    pe.wait_ge(sig_ready, c)
                for i in range(TPC):
                    mm = pe.matmul(ps[:, 0, i * P:(i + 1) * P], mix[:, 0, i * P:(i + 1) * P], wmix[:, 0, :],
                                   start=True, stop=True)
                mm.then_inc(rk_made, 1)
                pe.wait_ge(mixed, 2 * c + 2)
                if c >= 1:
                    pe.wait_ge(relu_ready, c)
                pe.matmul(ps[:, 1, :], wmix[:, 1, :], mix[:, 1, :], start=True, stop=True).then_inc(rk_made, 1)

            receptance_keys(0)
            for c in range(NC + 2):
                if c < NC:
                    pe.wait_ge(kact_ready, c + 1)
                    if c >= 1:
                        pe.wait_ge(x_ready[2], c)
                    for i in range(TPC):
                        mm = pe.matmul(ps[:, 4, i * P:(i + 1) * P], mix[:, 3, i * P:(i + 1) * P], wmix[:, 2, :],
                                       start=True, stop=True)
                    mm.then_inc(vm_made, 1)
                if c + 1 < NC:
                    receptance_keys(c + 1)
                if c >= 2:
                    qk(1, c - 2)
                if 1 <= c <= NC:
                    turn_xhat(2, c - 1, (6, 7))
            values(1, range(NT))
            pe.wait_ge(rows_in[1], 32)
            pe.wait_ge(v_ready[1], NT // 4)
            pe.wait_ge(low_ready[1], 2 * NC)
            pe.wait_ge(xt_ready[2], NC)
            pe.wait_ge(ones_ready, 1)

            def a_tile(u, g, hh, qt, half_, q0):
                n = u * 32 + hh * 8 + qt * 2 + half_
                if not isinstance(n, int) or n >= 2:
                    pe.wait_ge(a_read[1], n - 1)
                h = g * HG + hh
                for i in range(2):
                    k0 = PAD + half_ * 1024 + i * CHUNK
                    mm = pe.matmul(ps[:, 2 * half_ + i, :], QA[0:KR, h, bass.ds(q0 + qt * P, P)],
                                   KA[0:KR, h, k0:k0 + CHUNK], start=True, stop=True)
                mm.then_inc(a_made[1], 1)

            def b_tile(u, g, kt, hh, q0):
                n = (u * NT + kt) * HG + hh
                if not isinstance(n, int) or n >= 2:
                    pe.wait_ge(exp_done[1], n - 1)
                h = g * HG + hh
                pe.matmul(ps[:, 4 + hh % 2, :], KA[0:KR, h, PAD + kt * P:PAD + (kt + 1) * P],
                          QA[0:KR, h, bass.ds(q0, CHUNK)], start=True, stop=True).then_inc(b_made[1], 1)

            def sum_tile(u, g, kt):
                pe.wait_ge(exp_done[1], (u * NT + kt + 1) * HG)
                if kt == 0:
                    pe.wait_ge(o_kept[1], u + 1)
                for hh in range(HG):
                    mm = pe.matmul(ps[32 * hh:32 * hh + VC, 6, :], V1[:, kt, g * HG + hh, :],
                                   PR[:, (kt % 2) * HG + hh, :], start=(kt == 0), stop=(kt == NT - 1),
                                   skip_group_check=True)
                mm.then_inc(pv_done[1], 1)

            def turn_maxima(u):
                pe.wait_ge(mparts_ready[1], u + 1)
                if not isinstance(u, int) or u >= 1:
                    pe.wait_ge(mrow_ready[1], u)
                pe.transpose(ps[:, 7, :].bitcast(BF16)[:, 0:P], mparts[:, :], identb[:, :]).then_inc(mt_made[1], 1)

            A_ALL = [(hh, qt, hf) for hh in range(HG) for qt in range(4) for hf in range(2)]
            AHEAD, TURN_AT = 8, 13

            def unit(qc, g, blocks, final=False):
                u = qc * G + g
                q0 = qc * CHUNK

                def a_next(k):
                    s = AHEAD + k
                    g2 = g + 1 + s // 32
                    over = g2 >= G
                    if final and over:
                        return
                    a_tile(u + 1 + s // 32, g2 % G, *A_ALL[s % 32], q0 + (CHUNK if over else 0))

                for kt in blocks:
                    if kt == 0:
                        pe.wait_ge(mrow_in[1], 16 * HG * (u + 1))
                    b_tile(u, g, kt, 0, q0)
                    b_tile(u, g, kt, 1, q0)
                    a_next(2 * kt)
                    a_next(2 * kt + 1)
                    b_tile(u, g, kt, 2, q0)
                    b_tile(u, g, kt, 3, q0)
                    if kt >= 1:
                        sum_tile(u, g, kt - 1)
                    elif not isinstance(u, int) or u >= 1:
                        sum_tile(u - 1, (g - 1) % G, NT - 1)
                    if kt == TURN_AT and not (final and g == G - 1):
                        turn_maxima(u + 1)

            for g in range(G):
                pe.wait_ge(qk_in[1][g], 16 * 6)
            for s in range(32):
                a_tile(0, 0, *A_ALL[s], 0)
            for s in range(AHEAD):
                a_tile(1, 1, *A_ALL[s], 0)
            turn_maxima(0)
            unit(0, 0, range(1))
            with pe.Fori(0, NC - 1) as qc:
                unit(qc, 0, range(1, NT))
                for g in range(1, G):
                    unit(qc, g, range(NT))
                unit(qc + 1, 0, range(1), False)
            unit(NC - 1, 0, range(1, NT), True)
            for g in range(1, G):
                unit(NC - 1, g, range(NT), True)
            sum_tile(NC * G - 1, G - 1, NT - 1)

            pe.wait_ge(o_kept[1], NC * G + 1)
            for j in range(NT + TPC + 1):
                project(1, j)
                if j >= 8 and j % TPC == 0:
                    turn_xhat(3, j // TPC - 2, (6, 7))
            pe.wait_ge(w_in, 16 * 12)
            pe.wait_ge(x_ready[3], NT)
            pe.wait_ge(xt_ready[3], NC)
            for j in range(NT):
                mm = pe.matmul(ps[:, 7, j * E:(j + 1) * E], XT[:, PAD + j * P:PAD + (j + 1) * P], router,
                               start=True, stop=True)
            mm.then_inc(logits_made, 1)

            def gate_up(c, i, m):
                k = c * MT + i
                cols = XT[:, PAD + c * CHUNK:PAD + (c + 1) * CHUNK]
                wg = gate[:, m * P:(m + 1) * P] if m < MT_R else sgate[:, (m - MT_R) * P:(m - MT_R + 1) * P]
                wu = upw[:, m * P:(m + 1) * P] if m < MT_R else sup[:, (m - MT_R) * P:(m - MT_R + 1) * P]
                if k >= 2:
                    pe.wait_ge(silu_ready, k - 1)
                pe.matmul(ps[:, k % 2, :], wg, cols, start=True, stop=True).then_inc(g_made, 1)
                if k >= 2:
                    pe.wait_ge(gu_ready, k - 1)
                pe.matmul(ps[:, 2 + k % 2, :], wu, cols, start=True, stop=True).then_inc(u_made, 1)

            def comb_rows(c, m):
                k = c * MT_R + m
                if k >= 1:
                    pe.wait_ge(hid_ready, c * MT_R + m)
                pe.matmul(ps[:, 4, :], spread[:, m, :], combT[:, c * CHUNK:(c + 1) * CHUNK],
                          start=True, stop=True).then_inc(cb_made, 1)

            def down_proj(c):
                pe.wait_ge(hid_ready, (c + 1) * MT_R)
                pe.wait_ge(gu_ready, (c + 1) * MT)
                if c >= 1:
                    pe.wait_ge(y_ready, c)
                for i in range(TPC):
                    for m in range(MT):
                        wd = down[:, m, :] if m < MT_R else sdown[:, m - MT_R, :]
                        mm = pe.matmul(ps[:, 5, i * P:(i + 1) * P], hid[:, c % 2, m, i * P:(i + 1) * P], wd,
                                       start=(m == 0), stop=(m == MT - 1))
                mm.then_inc(down_made, 1)

            ORDER = [4, 5, 0, 1, 2, 3]
            for c in range(NC):
                for i, m in enumerate(range(MT)):
                    gate_up(c, i, ORDER[i])
                    if c == 0 and i == 1:
                        pe.wait_ge(comb_ready, 1)
                        for j in range(NT):
                            mm = pe.transpose(ps[:, 6, :].bitcast(BF16)[0:48, j % 8 * P:(j % 8 + 1) * P] if j < 8 else
                                              ps[:, 7, :].bitcast(BF16)[0:48, j % 8 * P:(j % 8 + 1) * P],
                                              combp[:, j, :], identb[:, :])
                        mm.then_inc(comb_turned, 1)
                    if i >= 2:
                        if c == 0 and i == 2:
                            pe.wait_ge(combT_ready, 2)
                        comb_rows(c, ORDER[i])
                down_proj(c)

        @block.scalar
        def _(act):
            def keep_xt(n, c, banks):
                act.wait_ge(turned[n], c + 1)
                dst = XT[:, PAD + c * CHUNK:PAD + (c + 1) * CHUNK]
                src = ps[:, banks[c % 2], :]
                if n == 0:
                    act.activation(dst, src, ACT.Identity, bias=BETA, scale=GAMMA).then_inc(xt_ready[n], 1)
                else:
                    act.activation(dst, src, ACT.Copy).then_inc(xt_ready[n], 1)

            def high_part(n, c, s):
                act.wait_ge(qk_made[n], 2 * c + s + 1)
                act.activation(parts[:, s, HIGH, c * CHUNK:(c + 1) * CHUNK], ps[:, 2 + s, :], ACT.Copy)\
                   .then_inc(high_ready[n], 1)

            def mid_part(n, c, s):
                act.wait_ge(resid_ready[n], 2 * c + s + 1)
                act.activation(parts[:, s, MID, c * CHUNK:(c + 1) * CHUNK], resid[:, s, :], ACT.Copy)\
                   .then_inc(mid_ready[n], 1)

            def split_parts(n, c):
                high_part(n, c, 0)
                high_part(n, c, 1)
                mid_part(n, c, 0)
                mid_part(n, c, 1)

            def keep_values(n, k):
                blocks = NB if n == 0 else NT
                act.wait_ge(v_made[n], k + 1)
                n4 = min(4, blocks - 4 * k)
                for b in range(4 * k, 4 * k + n4):
                    nk = min(P, WK - b * QB) if n == 0 else P
                    ins = act.activation(V[0:nk, b, :, 0:HD],
                                         ps[0:nk, 4 + k % 2, b % 4 * P:(b % 4 + 1) * P].rearrange("p (h d) -> p h d", h=H),
                                         ACT.Copy)
                ins.then_inc(v_ready[n], 1)

            act.wait_ge(w_in, 16 * 3)
            for c in range(NC):
                keep_xt(0, c, (0, 1))
                if c >= 1:
                    split_parts(0, c - 1)
            split_parts(0, NC - 1)
            for k in range(-(-NB // 4)):
                keep_values(0, k)

            act.wait_ge(v_made[0], -(-NB // 4))
            act.wait_ge(low_ready[0], 2 * NC)
            act.wait_ge(parts_kept[0], 2 * NC * 16)

            def exps(t, g):
                act.wait_ge(b_made[0], t * HG + g + 1)
                if not isinstance(t, int) or t >= 1:
                    act.wait_ge(pv_done[0], t * HG + g - HG + 1)
                act.activation(PR[:, g, 0:HG * QB], ps[:, 2 + g % 2, 0:HG * QB], ACT.Exp, scale=HD ** -0.5)\
                   .then_inc(exp_done[0], 1)

            def keep_sums(t, par, nq=QB):
                act.wait_ge(pv_done[0], (t + 1) * HG)
                act.activation(OT[:, :, bass.ds(t * QB, nq)],
                               ps[:, 4 + par, 0:G * QB].rearrange("p (g n) -> p g n", g=G)[:, :, 0:nq],
                               ACT.Copy).then_inc(o_kept[0], 1)

            for g in range(G):
                exps(0, g)
            with act.Fori(1, NB - 1, 2) as t:
                for d in range(2):
                    exps(t + d, 0)
                    exps(t + d, 1)
                    keep_sums(t + (d - 1), d)
                    exps(t + d, 2)
                    exps(t + d, 3)
            exps(NB - 1, 0)
            exps(NB - 1, 1)
            keep_sums(NB - 2, NB % 2)
            exps(NB - 1, 2)
            exps(NB - 1, 3)
            keep_sums(NB - 1, (NB - 1) % 2, T - (NB - 1) * QB)

            def turn_back(n, j):
                act.wait_ge(on_turned[n], j + 1)
                if j >= 2:
                    act.wait_ge(proj_made[n], j - 1)
                act.activation(OnT[:, j % 2, :], ps[:, 2 + j % 2, 0:P], ACT.Copy).then_inc(ont_ready[n], 1)

            for j in range(NT + TPC + 1):
                if j < NT:
                    turn_back(0, j)
                if j >= 8 and j % TPC == 0:
                    keep_xt(1, j // TPC - 2, (6, 7))
            for c in range(NC + 2):
                if c < NC:
                    act.wait_ge(rk_made, 2 * c + 1)
                    if c >= 1:
                        act.wait_ge(x_ready[2], c)
                    act.activation(mix[:, 4, :], ps[:, 0, :], ACT.Sigmoid).then_inc(sig_ready, 1)
                    act.wait_ge(rk_made, 2 * c + 2)
                    if c >= 1:
                        act.wait_ge(kact_ready, c)
                    act.activation(mix[:, 2, :], ps[:, 1, :], ACT.Relu).then_inc(relu_ready, 1)
                if c >= 2:
                    split_parts(1, c - 2)
                if 1 <= c <= NC:
                    act.wait_ge(mixed, 2 * min(c + 1, NC))
                    keep_xt(2, c - 1, (6, 7))
            act.wait_ge(x_ready[2], NC)
            for k in range(NT // 4):
                keep_values(1, k)
            act.wait_ge(v_made[1], NT // 4)
            act.wait_ge(low_ready[1], 2 * NC)
            act.wait_ge(parts_kept[1], 2 * NC * 16)

            def exp_round(r, first):
                for b in range(8):
                    act.wait_ge(b_made[1], r * 8 + b + 1)
                    if b % 4 == 0 and not first:
                        act.wait_ge(pv_done[1], r * 2 + b // 4 - 1)
                    act.activation(PR[:, b, :], ps[:, 4 + b % 2, :], ACT.Exp, scale=HD ** 0.5)\
                       .then_inc(exp_done[1], 1)

            exp_round(0, True)
            with act.Fori(1, NC * G * NT // 2) as r:
                exp_round(r, False)
            for j in range(NT + TPC + 1):
                if j < NT:
                    turn_back(1, j)
                if j >= 8 and j % TPC == 0:
                    keep_xt(3, j // TPC - 2, (6, 7))
            act.wait_ge(logits_made, 1)
            act.activation(rt[:, 0, :, :], ps[:, 7, 0:NT * E].rearrange("p (t e) -> p t e", t=NT), ACT.Sigmoid)\
               .then_inc(scores_ready, 1)
            for k in range(NC * MT):
                act.wait_ge(g_made, k + 1)
                if k >= 2:
                    act.wait_ge(gu_ready, k - 1)
                act.activation(silu[:, k % 2, :], ps[:, k % 2, :], ACT.Silu).then_inc(silu_ready, 1)
                if k == 1:
                    act.wait_ge(comb_turned, 1)
                    act.wait_ge(zeroed[1], 1)
                    for i in range(2):
                        act.activation(combT[0:48, i * 1024:(i + 1) * 1024], ps[0:48, 6 + i, :].bitcast(BF16),
                                       ACT.Copy).then_inc(combT_ready, 1)

        @block.vector
        def _(v):
            chain = Count(v, dve)

            def stat(n, c):
                t0 = c * TPC
                for i in range(TPC):
                    if n in (1, 3):
                        v.wait_ge(x_ready[n], t0 + i + 1)
                    chain.up(v.bn_stats(stats[:, i, :], X[:, t0 + i, :]))
                chain.settle()
                for i in range(TPC):
                    ins = v.bn_aggr(mv[:, t0 + i, :], stats[:, i, :])
                    if i < TPC - 1:
                        chain.up(ins)
                ins.then_inc(stats_ready[n], 1)
                v.wait_ge(stats_ready[n], c + 1)
                chain.settle()

            def normalise(n, c):
                v.wait_ge(rstd_ready[n], c + 1)
                if c >= 2:
                    v.wait_ge(turned[n], c - 1)
                for i in range(TPC):
                    t = c * TPC + i
                    ins = v.tensor_scalar(xhat[:, c % 2, i, :], X[:, t, :], mv[:, t, 0:1], rs[:, t:t + 1],
                                          ALU.subtract, ALU.mult)
                    if i < TPC - 1:
                        chain.up(ins)
                ins.then_inc(xhat_ready[n], 1)

            def left_by_high(n, c):
                for s in range(2):
                    k = 2 * c + s
                    v.wait_ge(high_ready[n], k + 1)
                    if c >= 1:
                        v.wait_ge(low_ready[n], k - 1)
                    v.tensor_tensor(resid[:, s, :], ps[:, 2 + s, :], parts[:, s, HIGH, c * CHUNK:(c + 1) * CHUNK],
                                    ALU.subtract).then_inc(resid_ready[n], 1)

            def left_by_mid(n, c):
                cols = slice(c * CHUNK, (c + 1) * CHUNK)
                for s in range(2):
                    v.wait_ge(mid_ready[n], 2 * c + s + 1)
                    v.tensor_tensor(parts[:, s, LOW, cols], resid[:, s, :], parts[:, s, MID, cols], ALU.subtract)\
                     .then_inc(low_ready[n], 1)

            def low_parts(n, c):
                left_by_high(n, c)
                left_by_mid(n, c)

            chain.up(v.memset(mparts[:, :], 0.0))
            for c in range(NC):
                v.wait_ge(x_in[c], 16)
                stat(0, c)
            v.wait_ge(w_in, 48)
            v.tensor_scalar(vecs[:, 4:6], vecs[:, 2:4], -1.0, 1.0, ALU.mult, ALU.add).then_inc(om_ready, 1)
            for c in range(NC):
                normalise(0, c)
                v.wait_ge(xhat_ready[0], c + 1)
                chain.settle()
                for i in range(TPC):
                    t = c * TPC + i
                    ins = v.tensor_scalar(X[:, t, :], X[:, t, :], tmp4[:, 1, t:t + 1], tmp4[:, 2, t:t + 1],
                                          ALU.mult, ALU.add)
                    if i < TPC - 1:
                        chain.up(ins)
                ins.then_inc(resid_in_x, 1)
                if c >= 1:
                    low_parts(0, c - 1)
            low_parts(0, NC - 1)

            def max_parts(n, src, rows, cnt):
                m = mparts[0:rows, 0:48]
                view = m.rearrange("p (i h) -> p i h", i=3)
                part = [view[:, i, :] for i in range(3)]
                res = negres[0:rows, :]
                chain.up(v.tensor_scalar(part[HIGH], src, -1.0, None, ALU.mult))
                chain.settle()
                chain.up(v.scalar_tensor_tensor(out=res, in0=src, scalar=-1.0, in1=part[HIGH],
                                                op0=ALU.mult, op1=ALU.subtract))
                chain.settle()
                chain.up(v.tensor_copy(part[MID], res))
                chain.settle()
                v.tensor_tensor(part[LOW], res, part[MID], ALU.subtract).then_inc(mparts_ready[n], 1)

            v.wait_ge(v_ready[0], -(-NB // 4))
            v.memset(ps[:, 4:6, :], 0.0).then_inc(zeroed[0], 1)
            base0 = chain.n

            def maxima(t, copy):
                for g in range(G):
                    v.wait_ge(a_made[0], t * G + g + 1)
                    v.tensor_reduce(rawmax[0:QB, 0, g * HG:(g + 1) * HG],
                                    ps[0:QB, g % 2, :].rearrange("p (h n) -> p h n", h=HG), AX.X, ALU.max)\
                     .then_inc(a_read[0], 1)
                    if g == 1 and copy:
                        keep_row(t - 1)
                v.wait_ge(a_read[0], t * G + G)
                chain.n = base0 + t * 3
                max_parts(0, rawmax[0:QB, 0, 0:H], QB, H)
                v.wait_ge(mparts_ready[0], t + 1)

            def keep_row(t):
                v.wait_ge(mt_made[0], t + 1)
                if not isinstance(t, int) or t >= 1:
                    v.wait_ge(mrow_in[0], t * 48)
                v.tensor_copy(mrow[:, 0:QB], ps[:, 6, :].bitcast(BF16)[0:48, 0:QB]).then_inc(mrow_ready[0], 1)

            maxima(0, False)
            maxima(1, True)
            with v.Fori(2, NB) as t:
                maxima(t, True)
            keep_row(NB - 1)
            chain.n = base0 + 3 * NB

            def normed(n, j):
                v.wait_ge(o_turned[n], j + 1)
                bank = ps[:, j % 2, :].rearrange("p (h n) -> p h n", h=H)
                chain.up(v.reciprocal(rz[:, j % 2, :], bank[:, :, HD]))
                chain.settle()
                if j >= 2:
                    v.wait_ge(on_turned[n], j - 1)
                v.tensor_tensor(On[:, j % 2, :].rearrange("p (h d) -> p h d", h=H), bank[:, :, 0:HD],
                                rz[:, j % 2, :].unsqueeze(2).to_broadcast([P, H, HD]), ALU.mult).then_inc(on_ready[n], 1)

            def add_proj(n, j):
                v.wait_ge(proj_made[n], j + 1)
                v.tensor_tensor(X[:, j, :], ps[:, 4 + j % 2, 0:P], X[:, j, :], ALU.add).then_inc(x_ready[2 * n + 1], 1)

            v.wait_ge(pv_done[0], HG * NB)
            chain.up(v.memset(XT[:, 0:PAD], 0.0))
            for j in range(NT + 4):
                if j < NT:
                    normed(0, j)
                if 2 <= j < NT + 2:
                    add_proj(0, j - 2)
                if j >= 5 and (j - 5) % TPC == 0:
                    stat(1, (j - 5) // TPC)
                if j >= 7 and (j - 7) % TPC == 0:
                    normalise(1, (j - 7) // TPC)
            def mix_tokens(c):
                x0 = PAD + c * CHUNK
                cur, prev = XT[:, x0:x0 + CHUNK], XT[:, x0 - 1:x0 - 1 + CHUNK]
                v.wait_ge(xt_ready[1], c + 1)
                for s, (mu, om) in enumerate(((MU_R, OM_R), (MU_K, OM_K))):
                    if c >= 1:
                        v.wait_ge(rk_made, 2 * c - 1 + s)
                    chain.up(v.tensor_scalar(mix[:, 5, :], prev, om, None, ALU.mult))
                    chain.settle()
                    v.scalar_tensor_tensor(out=mix[:, s, :], in0=cur, scalar=mu, in1=mix[:, 5, :],
                                           op0=ALU.mult, op1=ALU.add).then_inc(mixed, 1)
                    v.wait_ge(mixed, 2 * c + s + 1)

            def gate_values(c):
                v.wait_ge(sig_ready, c + 1)
                v.wait_ge(vm_made, c + 1)
                chain.up(v.tensor_tensor(mix[:, 5, :], ps[:, 4, :], mix[:, 4, :], ALU.mult))
                chain.settle()
                xc = X[:, c * TPC:(c + 1) * TPC, :].rearrange("p t c -> p (t c)")
                v.tensor_tensor(xc, mix[:, 5, :], xc, ALU.add).then_inc(x_ready[2], 1)
                v.wait_ge(x_ready[2], c + 1)

            v.wait_ge(om_ready, 1)
            mix_tokens(0)
            for c in range(NC + 2):
                if c < NC:
                    v.wait_ge(relu_ready, c + 1)
                    if c >= 1:
                        v.wait_ge(vm_made, c)
                    v.tensor_tensor(mix[:, 3, :], mix[:, 2, :], mix[:, 2, :], ALU.mult).then_inc(kact_ready, 1)
                if c + 1 < NC:
                    mix_tokens(c + 1)
                if c >= 2:
                    left_by_high(1, c - 2)
                if 1 <= c <= NC:
                    normalise(2, c - 1)
                if c < NC:
                    gate_values(c)
                    stat(2, c)
                if c >= 2:
                    left_by_mid(1, c - 2)
            v.wait_ge(xt_ready[2], NC)
            v.memset(ps[:, 6, :], 0.0).then_inc(o_kept[1], 1)
            chain.settle()

            def reduce_tiles(u, par, tiles):
                for k in tiles:
                    v.wait_ge(a_made[1], u * 32 + k + 1)
                    v.tensor_reduce(rawmax[:, par, k:k + 1], ps[:, 2 * (k % 2):2 * (k % 2) + 2, :], AX.XY, ALU.max)\
                     .then_inc(a_read[1], 1)

            def unit_maxima(u, par):
                v.wait_ge(a_read[1], u * 32 + 32)
                halves = rawmax[:, par, :].rearrange("p (a b) -> p a b", b=2)
                v.tensor_reduce(rowmax[:, :], halves, AX.X, ALU.max).then_inc(rowmax_ready, 1)

            def keep_rows(u):
                v.wait_ge(mt_made[1], u + 1)
                if not isinstance(u, int) or u >= 1:
                    v.wait_ge(mrow_in[1], 16 * HG * u)
                v.tensor_copy(mrow[:, :], ps[:, 7, :].bitcast(BF16)[0:48, 0:P]).then_inc(mrow_ready[1], 1)

            def keep_unit(u, g, q0):
                v.wait_ge(pv_done[1], u * NT + NT)
                v.tensor_copy(OT[:, g, bass.ds(q0, CHUNK)], ps[:, 6, :]).then_inc(o_kept[1], 1)

            def reduce_unit(u, g, more=8):
                reduce_tiles(u + 1, (g + 1) % 2, range(10, 32))
                unit_maxima(u + 1, (g + 1) % 2)
                reduce_tiles(u + 2, g % 2, range(0, min(4, more)))
                keep_rows(u + 1)
                reduce_tiles(u + 2, g % 2, range(min(4, more), more))

            reduce_tiles(0, 0, range(32))
            unit_maxima(0, 0)
            reduce_tiles(1, 1, range(8))
            keep_rows(0)
            reduce_tiles(1, 1, range(8, 10))
            with v.Fori(0, NC - 1) as qc:
                for g in range(G):
                    u = qc * G + g
                    reduce_unit(u, g)
                    reduce_tiles(u + 2, g % 2, range(8, 10))
                    keep_unit(u, g, qc * CHUNK)
            for g in range(G):
                u = (NC - 1) * G + g
                if g + 1 < G:
                    reduce_unit(u, g, 8 if g + 2 < G else 0)
                if g + 2 < G:
                    reduce_tiles(u + 2, g % 2, range(8, 10))
                keep_unit(u, g, (NC - 1) * CHUNK)

            v.wait_ge(bp_added, 1)
            for j in range(NT + 4):
                if j < NT:
                    normed(1, j)
                if 2 <= j < NT + 2:
                    add_proj(1, j - 2)
                if j >= 5 and (j - 5) % TPC == 0:
                    stat(3, (j - 5) // TPC)
                if j >= 7 and (j - 7) % TPC == 0:
                    normalise(3, (j - 7) // TPC)
            v.memset(combT.bitcast(U32), 0).then_inc(zeroed[1], 1)
            v.wait_ge(scores_ready, 1)
            v.wait_ge(w_in, 16 * 12)
            S, SB, WINS, CMP, MASK, SEL, W, TMP = (rt[:, i] for i in range(8))
            gv = lambda x: x.rearrange("p t (g e) -> p (t g) e", g=EG)
            GS = rt[:, 8].rearrange("p t e -> p (t e)")

            def do(ins):
                chain.up(ins)
                chain.settle()

            def small(i):
                return GS[:, 64 * i:64 * (i + 1)]

            do(v.tensor_tensor(SB, S, cbias.unsqueeze(1).to_broadcast([P, NT, E]), ALU.add))
            sb4 = gv(SB)
            t9 = rt[:, 9].rearrange("p t e -> p (t e)")
            big1, lit1 = t9[:, 0:64], t9[:, 64:128]
            big2, lit2 = t9[:, 128:192], t9[:, 192:256]
            chain.up(v.tensor_tensor(big1, sb4[:, :, 0], sb4[:, :, 1], ALU.max))
            chain.up(v.tensor_tensor(lit1, sb4[:, :, 0], sb4[:, :, 1], ALU.min))
            chain.up(v.tensor_tensor(big2, sb4[:, :, 2], sb4[:, :, 3], ALU.max))
            do(v.tensor_tensor(lit2, sb4[:, :, 2], sb4[:, :, 3], ALU.min))
            chain.up(v.tensor_tensor(small(0), big1, big2, ALU.max))
            chain.up(v.tensor_tensor(small(1), big1, big2, ALU.min))
            do(v.tensor_tensor(small(2), lit1, lit2, ALU.max))
            do(v.tensor_tensor(small(1), small(1), small(2), ALU.max))
            do(v.tensor_tensor(small(3), small(0), small(1), ALU.add))

            def wins(score, n, won, cmp):
                do(v.memset(won, 0.0))
                for d in range(1, n):
                    c = cmp[:, :, 0:n - d]
                    do(v.tensor_tensor(c, score[:, :, 0:n - d], score[:, :, d:n], ALU.is_ge))
                    chain.up(v.tensor_tensor(won[:, :, 0:n - d], won[:, :, 0:n - d], c, ALU.add))
                    chain.settle()
                    do(v.scalar_tensor_tensor(out=won[:, :, d:n], in0=won[:, :, d:n], scalar=1.0, in1=c,
                                              op0=ALU.add, op1=ALU.subtract))

            grp = small(3).rearrange("p (t g) -> p t g", g=EG)
            gwon = small(0).rearrange("p (t g) -> p t g", g=EG)
            gcmp = small(1).rearrange("p (t g) -> p t g", g=EG)
            wins(grp, EG, gwon, gcmp)
            do(v.tensor_scalar(small(2), small(0), float(EG - TOPG), None, ALU.is_ge))
            chosen = small(2).unsqueeze(2).to_broadcast([P, NT * EG, E // EG])
            do(v.tensor_copy(gv(MASK), chosen))
            do(v.tensor_tensor(TMP, SB, MASK, ALU.mult))
            do(v.tensor_scalar(CMP, MASK, 1.0, 3e38, ALU.subtract, ALU.mult))
            do(v.tensor_tensor(TMP, TMP, CMP, ALU.add))
            wins(TMP, E, WINS, CMP)
            do(v.tensor_scalar(SEL, WINS, float(E - TOPK), None, ALU.is_ge))
            do(v.tensor_tensor(W, S, SEL, ALU.mult))
            sm = small(0)[:, 0:NT]
            do(v.tensor_reduce(sm, W, AX.X, ALU.add))
            do(v.tensor_scalar(sm, sm, 1e-20, None, ALU.add))
            do(v.reciprocal(small(1)[:, 0:NT], sm))
            do(v.tensor_tensor(W, W, small(1)[:, 0:NT].unsqueeze(2).to_broadcast([P, NT, E]), ALU.mult))
            cp = combp.rearrange("p t (i e) -> p i t e", i=3)
            do(v.tensor_copy(cp[:, HIGH], W))
            do(v.tensor_tensor(TMP, W, cp[:, HIGH], ALU.subtract))
            do(v.tensor_copy(cp[:, MID], TMP))
            v.tensor_tensor(cp[:, LOW], TMP, cp[:, MID], ALU.subtract).then_inc(comb_ready, 1)

            ORDER = [4, 5, 0, 1, 2, 3]
            for c in range(NC):
                for i in range(MT):
                    k = c * MT + i
                    m = ORDER[i]
                    v.wait_ge(silu_ready, k + 1)
                    v.wait_ge(u_made, k + 1)
                    if c >= 2 and i == 0:
                        v.wait_ge(down_made, c - 1)
                    h = hid[:, c % 2, m, :]
                    v.tensor_tensor(h, ps[:, 2 + k % 2, :], silu[:, k % 2, :], ALU.mult).then_inc(gu_ready, 1)
                    if i >= 2:
                        v.wait_ge(gu_ready, k + 1)
                        v.wait_ge(cb_made, c * MT_R + m + 1)
                        v.tensor_tensor(h, ps[:, 4, :], h, ALU.mult).then_inc(hid_ready, 1)
                v.wait_ge(down_made, c + 1)
                xc = X[:, c * TPC:(c + 1) * TPC, :].rearrange("p t c -> p (t c)")
                v.tensor_tensor(xc, ps[:, 5, :], xc, ALU.add).then_inc(y_ready, 1)

        @block.gpsimd
        def _(g_):
            chain = Count(g_, pool)

            def do(ins):
                chain.up(ins)
                chain.settle()

            def rstd(n, c):
                g_.wait_ge(stats_ready[n], c + 1)
                t = slice(c * TPC, (c + 1) * TPC)
                if n:
                    do(g_.tensor_scalar(tmp4[:, 0, t], mv[:, t, 1], EPS, None, ALU.add))
                    g_.tensor_tensor(rs[:, t], tmp4[:, 0, t], half[:, :], ALU.pow).then_inc(rstd_ready[n], 1)
                    return
                do(g_.tensor_scalar(tmp4[:, 0, t], mv[:, t, 1], EPS, None, ALU.add))
                do(g_.tensor_tensor(rs1[:, t], tmp4[:, 0, t], half[:, :], ALU.pow))
                do(g_.tensor_tensor(tmp4[:, 0, t], mv[:, t, 1], rs1[:, t], ALU.mult))
                do(g_.tensor_tensor(tmp4[:, 0, t], tmp4[:, 0, t], rs1[:, t], ALU.mult))
                do(g_.tensor_scalar(tmp4[:, 0, t], tmp4[:, 0, t], EPS, None, ALU.add))
                do(g_.tensor_tensor(tmp4[:, 2, t], tmp4[:, 0, t], half[:, :], ALU.pow))
                do(g_.tensor_tensor(rs[:, t], tmp4[:, 2, t], rs1[:, t], ALU.mult))
                do(g_.tensor_scalar(tmp4[:, 1, t], rs1[:, t], 1.0, None, ALU.add))
                do(g_.tensor_tensor(tmp4[:, 2, t], mv[:, t, 0], rs1[:, t], ALU.mult))
                g_.tensor_scalar(tmp4[:, 2, t], tmp4[:, 2, t], -1.0, None, ALU.mult).then_inc(rstd_ready[n], 1)

            do(g_.memset(half[:, :], -0.5))
            chain.up(g_.memset(XT[:, 0:PAD], 0.0))
            chain.up(g_.memset(V[:, :, :, HD:VC], 1.0))
            g_.memset(XT[:, PAD + T:WK], 0.0).then_inc(zeroed[0], 1)
            for c in range(NC):
                rstd(0, c)
            for c in range(NC):
                rstd(1, c)
            for c in range(NC):
                rstd(2, c)
            g_.wait_ge(x_ready[2], NC)
            g_.memset(V1[:, :, :, HD:VC], 1.0).then_inc(ones_ready, 1)
            g_.wait_ge(xhat_ready[2], NC)
            g_.wait_ge(w2_in, 16 * 8)
            g_.tensor_tensor(X[:, :, :], X[:, :, :], bp[:, :].unsqueeze(1).to_broadcast([P, NT, C]), ALU.add)\
              .then_inc(bp_added, 1)
            do(g_.memset(zero16[:, :], 0.0))
            base = chain.n

            def split_maxima(u):
                chain.n = base + u * 3
                view = mparts[:, 0:48].rearrange("p (h i q) -> p i h q", h=HG, i=3)
                top, left, zero = (x[:, :].rearrange("p (h q) -> p h q", h=HG) for x in (minus_max, negres, zero16))
                g_.wait_ge(rowmax_ready, u + 1)
                do(g_.tensor_tensor(minus_max[:, :], zero16[:, :], rowmax[:, :], ALU.subtract))
                if not isinstance(u, int) or u >= 1:
                    g_.wait_ge(mt_made[1], u)
                do(g_.tensor_tensor(view[:, HIGH], top, zero, ALU.add))
                do(g_.tensor_tensor(left, top, view[:, HIGH], ALU.subtract))
                g_.tensor_tensor(view[:, MID], left, zero, ALU.add).then_inc(mid_max, 1)
                g_.wait_ge(mid_max, u + 1)
                g_.tensor_tensor(view[:, LOW], left, view[:, MID], ALU.subtract)\
                  .then_inc(mparts_ready[1], 1)

            split_maxima(0)
            with g_.Fori(1, NC * G) as u:
                split_maxima(u)
            chain.n = base + 3 * NC * G
            for c in range(NC):
                rstd(3, c)
    return nc


def parts_of(x):
    bf = mybir.dt.np(BF16)
    left, got = np.asarray(x, np.float64), []
    for _ in range(3):
        p = left.astype(np.float32).astype(bf)
        got.append(p)
        left = left - p.astype(np.float64)
    return np.stack(got)


def constants():
    bf = mybir.dt.np(BF16)
    k = {}
    k["ident"] = np.eye(P, dtype=np.float32)
    k["identb"] = np.eye(P, dtype=np.float32).astype(bf)
    q, key = np.arange(QB)[:, None], np.arange(P)[None, :]
    mask = np.where((key - q >= 0) & (key - q <= 2 * HALF), 0.0, MASKED).astype(np.float32)
    k["maskA"] = np.repeat(np.pad(mask, ((0, P - QB), (0, 0)))[:, None, :], HG, 1).astype(bf)
    k["maskB"] = np.repeat(mask.T[:, None, :], HG, 1).astype(bf)
    k["ones"] = np.ones((3, H, WK), np.float32).astype(bf)
    k["zeros"] = np.zeros((KR - ROW_MAX, H, WK), np.float32).astype(bf)
    k["edge"] = np.zeros((3 * HD * H, PAD), np.float32).astype(bf)
    edge = np.zeros((3, H, WK), np.float32)
    edge[0, :, 0:PAD] = MASKED
    edge[0, :, PAD + T:] = MASKED
    k["kbias0"] = edge.astype(bf)
    x = (2 ** 8) ** (1.0 / H)
    slopes = np.array([1.0 / x ** (i + 1) for i in range(H)], dtype=np.float32).astype(np.float64)
    bias = np.zeros((3, H, WK), bf)
    bias[:, :, PAD:PAD + T] = parts_of(slopes[:, None] * np.arange(T)[None, :] / np.sqrt(float(HD)))
    k["kbias1"] = bias
    spread = np.zeros((P, MT_R, P), np.float32)
    for i in range(3):
        for e in range(E):
            spread[E * i + e, e // 4, (e % 4) * HE:(e % 4 + 1) * HE] = 1.0
    k["spread"] = spread.astype(bf)
    return k


def kernel(**inputs):
    import numpy as _np
    import concourse.bacc as _bacc
    from concourse import mybir as _mybir
    from concourse.bass_utils import run_bass_kernel_spmd as _run

    f = {n: _np.asarray(x) for n, x in inputs.items()}
    arrays = constants()
    arrays["x"] = f["L0_attn_x"].reshape(T, C)
    order = _np.arange(C).reshape(H, HD).T.reshape(-1)
    arrays["wqkv0"] = f["L0_attn_w_qkv"].T[:, _np.concatenate([order, C + order, 2 * C + _np.arange(C)])]
    arrays["wo0"] = f["L0_attn_w_out"].T
    arrays["vecs"] = _np.stack([f["L0_attn_gamma"], f["L0_attn_beta"], f["L0_ffn_mu_r"], f["L0_ffn_mu_k"]], 1)
    arrays["wmix"] = _np.stack([f["L0_ffn_W_r"].T, f["L0_ffn_W_k"].T, f["L0_ffn_W_v"].T], 1)
    arrays["wqkv1"] = _np.concatenate([f["L1_attn_Wq"].T[:, order], f["L1_attn_Wk"].T[:, order], f["L1_attn_Wv"].T], 1)
    arrays["wo1"] = f["L1_attn_Wp"].T
    arrays["bp_rows"] = _np.broadcast_to(f["L1_attn_bp"][None, :], (P, C))
    arrays["gate"] = f["L1_ffn_gate_w"].transpose(1, 0, 2).reshape(C, E * HE)
    arrays["up"] = f["L1_ffn_up_w"].transpose(1, 0, 2).reshape(C, E * HE)
    arrays["down"] = f["L1_ffn_down_w"].reshape(MT_R, P, C).transpose(1, 0, 2)
    arrays["sgate"] = f["L1_ffn_shared_gate_w"].T
    arrays["sup"] = f["L1_ffn_shared_up_w"].T
    arrays["sdown"] = f["L1_ffn_shared_down_w"].T.reshape(MT_S, P, C).transpose(1, 0, 2)
    arrays["router"] = f["L1_ffn_router_w"].T
    arrays["cbias"] = _np.broadcast_to(f["L1_ffn_correction_bias"][None, :], (P, E))

    nc = _bacc.Bacc("TRN2", target_bir_lowering=False, num_devices=1)
    given, aps = {}, {}
    for name, v in arrays.items():
        v = _np.ascontiguousarray(v)
        given[f"in_{name}"] = v
        aps[name] = nc.dram_tensor(f"in_{name}", v.shape, _mybir.dt.from_np(v.dtype), kind="ExternalInput").ap()
    out = nc.dram_tensor("out", (T, C), _mybir.dt.from_np(_np.dtype("float32")), kind="ExternalOutput").ap()
    build(nc, aps, out)
    r = _run(nc, [given], core_ids=[0])
    return r.results[0]["out"].reshape(1, T, C)
```

```python
from contextlib import ExitStack

import concourse.bass as bass
import numpy as np
from concourse import mybir

F32 = mybir.dt.float32
BF16 = mybir.dt.bfloat16
U32 = mybir.dt.uint32
ALU = mybir.AluOpType
ACT = mybir.ActivationFunctionType
AX = mybir.AxisListType

P = 128
T, C = 2048, 128
NT = T // P
H, HD = 16, 8
PAD = 16
CHUNK = 512
NC = T // CHUNK
TPC = CHUNK // P
EPS = 1e-5

HIGH, MID, LOW = range(3)
PAIRS = [(HIGH, HIGH), (HIGH, MID), (HIGH, LOW), (MID, HIGH), (MID, MID), (LOW, HIGH)]
RUNS = [[(0, 3, HIGH, 0), (3, 2, MID, 0), (5, 1, LOW, 0)], [(0, 3, HIGH, 1), (3, 2, HIGH, 1), (5, 1, HIGH, 0)]]
ROW_BIAS = HD * len(PAIRS)
ROW_MAX = ROW_BIAS + 3
ROW_PAD = ROW_MAX + 3
KR = 96
WK = PAD + T + PAD

HALF = 16
QB = P - 2 * HALF
NB = -(-T // QB)
G = 4
HG = H // G
VC = HD + 1
SECOND_HALF = (PAD + T // 2 - P) // QB + 1
ADD_LAG, STAT_LAG, NORM_LAG, TURN_LAG, KEEP_LAG = 3, 6, 7, 10, 9
FIRST_UNIT = list(range(0, 32, 2)) + list(range(1, 32, 2))
MASKED = -1e30
A_BANKS = (0, 1, 7)
LAST_BANKS = (4, 5, 0, 1)

E, TOPK, EG, TOPG, HE, HS = 16, 4, 4, 2, 32, 256
MT_R = E * HE // P
MT_S = HS // P
MT = MT_R + MT_S
MT_ORDER = list(range(MT_R, MT)) + list(range(MT_R))
EARLY = 14


class Count:

    def __init__(self, eng, sem, base=0):
        self.eng, self.sem, self.n = eng, sem, base

    def up(self, ins):
        ins.then_inc(self.sem, 1)
        self.n = self.n + 1

    def settle(self):
        self.eng.wait_ge(self.sem, self.n)


def build(nc, a, out):
    ctx = ExitStack()
    with ctx:
        def sb(name, shape, dt=F32):
            return ctx.enter_context(nc.sbuf_tensor(name, shape, dt))

        def sem(name):
            return ctx.enter_context(nc.semaphore(name))

        QA = sb("QA", [P, H, T], BF16)
        KA = sb("KA", [P, H, WK], BF16)
        X = sb("X", [P, NT, C])
        big = sb("big", [P, G * T])
        OT = big[:, :].rearrange("p (g n) -> p g n", g=G)
        q_parts = big[:, 0:3 * T // 2].bitcast(BF16).rearrange("p (i n) -> p i n", i=3)
        k_parts = big[:, 3 * T // 2:3 * (T + WK) // 2].bitcast(BF16).rearrange("p (i n) -> p i n", i=3)
        V = sb("V", [P, NB, H, VC])
        V1 = V[:, 0:NT, :, :]
        ring = sb("ring", [P, 8 * CHUNK + 64])
        PR = ring[:, 0:8 * CHUNK].rearrange("p (b n) -> p b n", b=8)
        XT = ring[:, 0:WK]
        xhat = ring[:, WK:WK + 2 * CHUNK].rearrange("p (b t c) -> p b t c", b=2, t=TPC)
        resid = ring[:, WK + 2 * CHUNK:WK + 4 * CHUNK].rearrange("p (b n) -> p b n", b=2)
        masked = ring[0:QB, 4 * CHUNK:8 * CHUNK].rearrange("p (b h n) -> p b h n", b=G, h=HG)
        vflat = V[:, :, :, :].rearrange("p a b c -> p (a b c)")
        mix = vflat[:, 0:6 * CHUNK].rearrange("p (b n) -> p b n", b=6)
        On = vflat[:, 0:2 * C].rearrange("p (b c) -> p b c", b=2)
        OnT = vflat[:, 2 * C:4 * C].rearrange("p (b c) -> p b c", b=2)

        wqkv = [sb("wqkv0", [P, 3 * C]), sb("wqkv1", [P, 3 * C])]
        wo = [sb("wo0", [P, C]), sb("wo1", [P, C])]
        wmix = sb("wmix", [P, 3, C])
        vecs = sb("vecs", [P, 6])
        GAMMA, BETA, MU_R, MU_K, OM_R, OM_K = (vecs[:, i:i + 1] for i in range(6))
        ident = sb("ident", [P, P])
        identb = sb("identb", [P, P], BF16)
        maskA = sb("maskA", [QB, P])
        maskB = sb("maskB", [P, HG, QB], BF16)
        bp = sb("bp", [P, C])
        half = sb("half", [P, TPC])
        stats = sb("stats", [P, TPC, 6])
        mv = sb("mv", [P, NT, 2])
        rs = sb("rs", [P, NT])
        rs1 = sb("rs1", [P, NT])
        tmp4 = sb("tmp4", [P, 3, NT])
        shift = rs1
        rawmax = sb("rawmax", [P, 2, 32])
        block_max = rawmax[0:QB, :, :].rearrange("p a b -> p (a b)")[:, 0:3 * H].rearrange("p (b h) -> p b h", b=3)
        rowmax = sb("rowmax", [P, 16])
        negres = sb("negres", [P, 16])
        mparts = sb("mparts", [P, P], BF16)
        zero16 = sb("zero16", [P, 16])
        minus_max = sb("minus_max", [P, 16])
        mrow = sb("mrow", [48, P], BF16)
        rz = sb("rz", [P, 2, H])

        qaf = QA[:, :, :].rearrange("p h n -> p (h n)").bitcast(F32)
        gate = qaf[:, 0:512]
        upw = qaf[:, 512:1024]
        down = qaf[:, 1024:1536].rearrange("p (m c) -> p m c", m=MT_R)
        sgate = qaf[:, 1536:1792]
        sup = qaf[:, 1792:2048]
        sdown = qaf[:, 2048:2304].rearrange("p (m c) -> p m c", m=MT_S)
        router = qaf[:, 2304:2320]
        cbias = qaf[:, 2320:2336]
        spread = qaf[:, 2336:2336 + 256].bitcast(BF16).rearrange("p (m n) -> p m n", m=MT_R)
        combT = qaf[:, 2600:2600 + T // 2].bitcast(BF16)
        silu = qaf[:, 3700:3700 + 2 * CHUNK].rearrange("p (b n) -> p b n", b=2)
        hid = qaf[:, 4800:4800 + 3 * MT * CHUNK].rearrange("p (b m n) -> p b m n", b=3, m=MT)
        kaf = KA[:, :, :].rearrange("p h n -> p (h n)").bitcast(F32)
        rt = kaf[:, 0:16 * NT * E].rearrange("p (b t e) -> p b t e", b=16, t=NT)
        pre = kaf[:, 10 * NT * E:16 * NT * E].rearrange("p (b t e) -> p b t e", b=3, t=NT)
        combp = kaf[:, 16 * NT * E:16 * NT * E + NT * 24].bitcast(BF16).rearrange("p (t i) -> p t i", t=NT)

        ps = ctx.enter_context(nc.psum_tensor("ps", [P, 8, CHUNK], F32))

        q_kept = nc.dram_tensor("q_kept", [3, HD, H, T], BF16).ap()
        k_kept = nc.dram_tensor("k_kept", [3, HD, H, WK], BF16).ap()

        x_d = a["x"].rearrange("(c t p) n -> c p t n", c=NC, p=P)
        out_d = out.rearrange("(c t p) n -> c p t n", c=NC, p=P)

        x_in = [sem(f"x_in{c}") for c in range(NC)]
        w_in = sem("w_in")
        w2_in = sem("w2_in")
        bp_added = sem("bp_added")
        ones_ready = sem("ones_ready")
        om_ready = sem("om_ready")
        x_ready = [None] + [sem(f"x_ready{n}") for n in (1, 2, 3)]
        stats_ready = [sem(f"stats_ready{n}") for n in range(4)]
        rstd_ready = [sem(f"rstd_ready{n}") for n in range(4)]
        xhat_ready = [sem(f"xhat_ready{n}") for n in range(4)]
        turned = [sem(f"turned{n}") for n in range(4)]
        xt_ready = [sem(f"xt_ready{n}") for n in range(4)]
        dve = sem("dve")
        pool = sem("pool")
        resid_in_x = sem("resid_in_x")

        L = range(2)
        qk_made = [sem(f"qk_made{n}") for n in L]
        high_ready = [sem(f"high_ready{n}") for n in L]
        resid_ready = [sem(f"resid_ready{n}") for n in L]
        mid_ready = [sem(f"mid_ready{n}") for n in L]
        low_ready = [sem(f"low_ready{n}") for n in L]
        v_made = [sem(f"v_made{n}") for n in L]
        v_ready = [sem(f"v_ready{n}") for n in L]
        parts_kept = [sem(f"parts_kept{n}") for n in L]
        rows_in = [sem(f"rows_in{n}") for n in L]
        first_in = sem("first_in")
        qk_in = [[sem(f"qk_in{n}_{g}") for g in range(G)] for n in L]
        zeroed = [sem(f"zeroed{n}") for n in L]
        a_made = [sem(f"a_made{n}") for n in L]
        a_read = [sem(f"a_read{n}") for n in L]
        mparts_ready = [sem(f"mparts_ready{n}") for n in L]
        mid_max = [sem(f"mid_max{n}") for n in L]
        rowmax_ready = sem("rowmax_ready")
        mt_made = [sem(f"mt_made{n}") for n in L]
        mrow_ready = [sem(f"mrow_ready{n}") for n in L]
        mrow_in = [sem(f"mrow_in{n}") for n in L]
        b_made = [sem(f"b_made{n}") for n in L]
        exp_done = [sem(f"exp_done{n}") for n in L]
        pv_done = [sem(f"pv_done{n}") for n in L]
        o_kept = [sem(f"o_kept{n}") for n in L]
        o_turned = [sem(f"o_turned{n}") for n in L]
        on_ready = [sem(f"on_ready{n}") for n in L]
        on_turned = [sem(f"on_turned{n}") for n in L]
        ont_ready = [sem(f"ont_ready{n}") for n in L]
        proj_made = [sem(f"proj_made{n}") for n in L]

        mixed = sem("mixed")
        rk_made = sem("rk_made")
        sig_ready = sem("sig_ready")
        relu_ready = sem("relu_ready")
        kact_ready = sem("kact_ready")
        vm_made = sem("vm_made")

        logits_made = sem("logits_made")
        scores_ready = sem("scores_ready")
        comb_ready = sem("comb_ready")
        comb_turned = sem("comb_turned")
        combT_ready = sem("combT_ready")
        g_made = sem("g_made")
        u_made = sem("u_made")
        silu_ready = sem("silu_ready")
        gu_ready = sem("gu_ready")
        cb_made = sem("cb_made")
        hid_ready = sem("hid_ready")
        down_made = sem("down_made")
        y_ready = sem("y_ready")
        stored = sem("stored")

        block = ctx.enter_context(nc.Block())

        def part(s, i, c):
            first = c * CHUNK + s * PAD
            return (q_parts, k_parts)[s][:, i, first:first + CHUNK]

        @block.sync
        def _(sp):
            def weight(dst, src, s=w_in):
                sp.dma_start(dst, src).then_inc(s, 16)

            sp.dma_start(X[:, 0:TPC, :], x_d[0]).then_inc(x_in[0], 16)
            weight(ident[:, :], a["ident"])
            weight(vecs[:, 0:4], a["vecs"])
            weight(wqkv[0][:, :], a["wqkv0"])
            for c in range(1, NC):
                sp.dma_start(X[:, c * TPC:(c + 1) * TPC, :], x_d[c]).then_inc(x_in[c], 16)
            weight(identb[:, :], a["identb"], w2_in)
            weight(maskA[:, :], a["maskA"], w2_in)
            weight(maskB[:, :, :], a["maskB"], w2_in)
            weight(wo[0][:, :], a["wo0"], w2_in)
            weight(wmix[:, :, :], a["wmix"], w2_in)
            weight(wqkv[1][:, :], a["wqkv1"], w2_in)
            weight(wo[1][:, :], a["wo1"], w2_in)
            weight(bp[:, :], a["bp_rows"], w2_in)

            def operands(n):
                if n == 1:
                    sp.wait_ge(b_made[0], NB * HG)
                    sp.wait_ge(mrow_in[0], 48 * NB)
                if n == 0:
                    sp.dma_start(QA[ROW_BIAS:ROW_BIAS + 3, :, :], a["ones"][:, :, 0:T]).then_inc(rows_in[n], 16)
                    sp.dma_start(QA[ROW_MAX:KR, :, :], a["zeros"][:, :, 0:T]).then_inc(rows_in[n], 16)
                    sp.dma_start(KA[ROW_PAD:KR, :, :], a["zeros"][0:KR - ROW_PAD]).then_inc(rows_in[n], 16)
                    sp.dma_start(KA[ROW_MAX:ROW_MAX + 3, :, :], a["ones"]).then_inc(rows_in[n], 16)
                else:
                    sp.dma_start(QA[ROW_MAX:ROW_MAX + 3, :, :], a["zeros"][0:3, :, 0:T]).then_inc(rows_in[n], 16)
                sp.dma_start(KA[ROW_BIAS:ROW_BIAS + 3, :, :], a[f"kbias{n}"]).then_inc(rows_in[n], 16)
                for c in range(NC):
                    for s in range(2):
                        sp.wait_ge(high_ready[n], 2 * c + s + 1)
                        sp.wait_ge(low_ready[n], 2 * c + s + 1)
                        first = c * CHUNK + (PAD if s and (c or n) else 0)
                        end = (c + 1) * CHUNK + (PAD if s else 0) + (PAD if s and c == NC - 1 and n == 0 else 0)
                        if n == 0 and c == 0 and s == 1:
                            sp.wait_ge(zeroed[0], 1)
                        kept, source = ((q_kept, q_parts), (k_kept, k_parts))[s]
                        sp.dma_start(kept[:, :, :, first:end].rearrange("i d h n -> (d h) i n"), source[:, :, first:end])\
                          .then_inc(parts_kept[n], 16)
                    if c == NC // 2 - 1:
                        sp.wait_ge(parts_kept[n], 16 * NC)
                        for i in range(len(PAIRS)):
                            load_pair(i, 0, slice(0, H if n == 0 else HG), qk_in[0][0] if n == 0 else first_in)
                if n == 0:
                    return
                sp.wait_ge(parts_kept[n], 2 * NC * 16)
                for i in range(len(PAIRS)):
                    load_pair(i, 1, slice(0, HG), qk_in[1][0])
                for g in range(1, G):
                    for s in range(2):
                        kept, rows_of = (q_kept, QA) if s == 0 else (k_kept, KA)
                        heads = slice(g * HG, (g + 1) * HG)
                        for first, n_pairs, part_, step in RUNS[s]:
                            if step:
                                src = kept[part_:part_ + n_pairs, :, heads, :].rearrange("i d h n -> i d (h n)")
                            else:
                                src = kept[part_, :, heads, :].rearrange("d h n -> d (h n)").unsqueeze(0)\
                                    .to_broadcast([n_pairs, HD, HG * (T if s == 0 else WK)])
                            rows = slice(HD * first, HD * (first + n_pairs))
                            dst = rows_of[rows, heads, :].rearrange("p h n -> p (h n)")
                            sp.dma_start(dst, src).then_inc(qk_in[n][g], 16)

            def load_pair(i, half_, heads, loaded):
                q_cols = slice(half_ * T // 2, (half_ + 1) * T // 2)
                k_cols = (slice(0, PAD + T // 2), slice(PAD + T // 2, WK))[half_]
                rows = slice(HD * i, HD * (i + 1))
                sp.dma_start(QA[rows, heads, q_cols], q_kept[PAIRS[i][0], :, heads, q_cols]).then_inc(loaded, 16)
                sp.dma_start(KA[rows, heads, k_cols], k_kept[PAIRS[i][1], :, heads, k_cols]).then_inc(loaded, 16)

            operands(0)
            for t in range(NB):
                sp.wait_ge(mrow_ready[0], t + 1)
                nq = min(QB, T - t * QB)
                for i in range(3):
                    sp.dma_start(QA[ROW_MAX + i:ROW_MAX + i + 1, :, t * QB:t * QB + nq],
                                 mrow[16 * i:16 * i + 16, 0:nq]).then_inc(mrow_in[0], 16)
                if t < len(PAIRS):
                    if t == 0:
                        sp.wait_ge(parts_kept[0], 2 * NC * 16)
                    load_pair(t, 1, slice(0, H), qk_in[0][1])
            operands(1)
            with sp.Fori(0, NC) as qc:
                for g in range(G):
                    sp.wait_ge(mrow_ready[1], qc * G + g + 1)
                    for hh in range(HG):
                        sp.dma_start(QA[ROW_MAX:ROW_MAX + 3, g * HG + hh, bass.ds(qc * CHUNK, CHUNK)],
                                     mrow[12 * hh:12 * hh + 12, :]).then_inc(mrow_in[1], 16)
            sp.wait_ge(b_made[1], NC * G * NT * HG)
            for dst, name in ((gate, "gate"), (upw, "up"), (down, "down"), (sgate, "sgate"), (sup, "sup"),
                              (sdown, "sdown"), (router, "router"), (cbias, "cbias"), (spread, "spread")):
                sp.dma_start(dst, a[name]).then_inc(w_in, 16)
            for c in range(NC):
                sp.wait_ge(y_ready, c + 1)
                sp.dma_start(out_d[c], X[:, c * TPC:(c + 1) * TPC, :]).then_inc(stored, 16)
            sp.wait_ge(stored, 16 * NC)

        @block.tensor
        def _(pe):
            def turn_xhat(n, c, banks):
                pe.wait_ge(xhat_ready[n], c + 1)
                if c >= 2:
                    pe.wait_ge(xt_ready[n], c - 1)
                for i in range(TPC):
                    mm = pe.transpose(ps[:, banks[c % 2], i * P:(i + 1) * P], xhat[:, c % 2, i, :], ident[:, :])
                mm.then_inc(turned[n], 1)

            def qk(n, c):
                pe.wait_ge(xt_ready[2 * n], c + 1)
                for s in range(2):
                    if c >= 1:
                        pe.wait_ge(resid_ready[n], 2 * (c - 1) + s + 1)
                        pe.wait_ge(high_ready[n], 2 * (c - 1) + s + 1)
                    pe.matmul(ps[:, 2 + s, :], wqkv[n][:, s * C:(s + 1) * C],
                              XT[:, PAD + c * CHUNK:PAD + (c + 1) * CHUNK], start=True, stop=True).then_inc(qk_made[n], 1)

            def values(n, blocks):
                for b in blocks:
                    k = b // 4
                    if b % 4 == 0 and k >= 2:
                        pe.wait_ge(v_ready[n], k - 1)
                    first = b * QB if n == 0 else PAD + b * P
                    nk = min(P, WK - first)
                    mm = pe.matmul(ps[0:nk, 4 + k % 2, (b % 4) * P:(b % 4 + 1) * P], XT[:, first:first + nk],
                                   wqkv[n][:, 2 * C:3 * C], start=True, stop=True)
                    if b % 4 == 3 or b == (NB if n == 0 else NT) - 1:
                        mm.then_inc(v_made[n], 1)

            pe.wait_ge(w_in, 16 * 3)
            turn_xhat(0, 0, (0, 1))
            turn_xhat(0, 1, (0, 1))
            for c in range(NC):
                qk(0, c)
                if c + 2 < NC:
                    turn_xhat(0, c + 2, (0, 1))
            pe.wait_ge(zeroed[0], 1)
            values(0, range(NB))

            def project(n, j):
                if j < NT:
                    if j >= 2:
                        pe.wait_ge(on_ready[n], j - 1)
                    for g in range(G):
                        mm = pe.transpose(ps[:, j % 2, g * P:(g + 1) * P], OT[:, g, j * P:(j + 1) * P], ident[:, :])
                    mm.then_inc(o_turned[n], 1)
                k = j - 2
                if 0 <= k < NT:
                    pe.wait_ge(on_ready[n], k + 1)
                    if k >= 2:
                        pe.wait_ge(ont_ready[n], k - 1)
                    pe.transpose(ps[:, 2 + k % 2, 0:P], On[:, k % 2, :], ident[:, :]).then_inc(on_turned[n], 1)
                k = j - 3
                if 0 <= k < NT:
                    pe.wait_ge(ont_ready[n], k + 1)
                    if k >= 2:
                        pe.wait_ge(x_ready[2 * n + 1], k - 1)
                    pe.matmul(ps[:, 4 + k % 2, 0:P], OnT[:, k % 2, :], wo[n][:, :],
                              start=True, stop=True).then_inc(proj_made[n], 1)

            pe.wait_ge(w2_in, 16 * 8)
            pe.wait_ge(rows_in[0], 16 * 5)
            pe.wait_ge(xt_ready[0], NC)
            pe.wait_ge(low_ready[0], 2 * NC)
            pe.wait_ge(v_ready[0], -(-NB // 4))
            pe.wait_ge(zeroed[0], 2)

            def a_scores(t, g):
                nq, k = min(QB, T - t * QB), HG * t + g
                nk = min(P, WK - t * QB)
                if g == 0 and t in (0, SECOND_HALF):
                    pe.wait_ge(qk_in[0][t // SECOND_HALF], 16 * 2 * len(PAIRS))
                if k >= 3:
                    pe.wait_ge(a_read[0], k - 2)
                bank = ps[0:nq, A_BANKS[k % 3], :].rearrange("p (h n) -> p h n", h=HG)
                for hh in range(HG):
                    h = g * HG + hh
                    mm = pe.matmul(bank[:, hh, 0:nk], QA[0:KR, h, t * QB:t * QB + nq], KA[0:KR, h, t * QB:t * QB + nk],
                                   start=True, stop=True, skip_group_check=True)
                mm.then_inc(a_made[0], 1)

            def b_scores(t, g):
                nq, k = min(QB, T - t * QB), HG * t + g
                nk = min(P, WK - t * QB)
                if g == 0:
                    pe.wait_ge(mrow_in[0], 48 * (t + 1))
                if k >= 2:
                    pe.wait_ge(exp_done[0], k - 1)
                bank = ps[0:nk, 2 + g % 2, 0:HG * QB].rearrange("p (h n) -> p h n", h=HG)
                pe.matmul(bank, identb[:, 0:nk], maskB[:, :, :], start=True, stop=False, skip_group_check=True)
                for hh in range(HG):
                    h = g * HG + hh
                    mm = pe.matmul(bank[:, hh, 0:nq], KA[0:KR, h, t * QB:t * QB + nk], QA[0:KR, h, t * QB:t * QB + nq],
                                   start=False, stop=True, skip_group_check=True)
                mm.then_inc(b_made[0], 1)

            def sums(t, g):
                nq, k = min(QB, T - t * QB), HG * t + g
                nk = min(P, WK - t * QB)
                pe.wait_ge(exp_done[0], k + 1)
                if g == 0 and t >= 2:
                    pe.wait_ge(o_kept[0], t - 1)
                for hh in range(HG):
                    mm = pe.matmul(ps[32 * hh:32 * hh + VC, 4 + t % 2, g * QB:g * QB + nq], V[0:nk, t, g * HG + hh, :],
                                   PR[0:nk, g, hh * QB:hh * QB + nq], start=True, stop=True, skip_group_check=True)
                mm.then_inc(pv_done[0], 1)

            LEAD = 3
            for i in range(NB + LEAD + 1):
                for g in range(G):
                    if i < NB:
                        a_scores(i, g)
                    if g == 3 and 1 <= i <= NB:
                        pe.wait_ge(mparts_ready[0], i)
                        if i >= 2:
                            pe.wait_ge(mrow_ready[0], i - 1)
                        pe.transpose(ps[:, 6, :].bitcast(BF16)[0:48, 0:QB], mparts[0:QB, 0:48],
                                     identb[0:QB, 0:QB]).then_inc(mt_made[0], 1)
                    if LEAD <= i < NB + LEAD:
                        b_scores(i - LEAD, g)
                    k = HG * (i - LEAD) + g - 1
                    if 0 <= k < HG * NB:
                        sums(k // HG, k % HG)

            pe.wait_ge(o_kept[0], NB)

            def receptance_keys(c):
                pe.wait_ge(mixed, 2 * c + 1)
                if c == 0:
                    pe.wait_ge(x_ready[1], NT)
                else:
                    pe.wait_ge(sig_ready, c)
                for i in range(TPC):
                    mm = pe.matmul(ps[:, 0, i * P:(i + 1) * P], mix[:, 0, i * P:(i + 1) * P], wmix[:, 0, :],
                                   start=True, stop=True)
                mm.then_inc(rk_made, 1)
                pe.wait_ge(mixed, 2 * c + 2)
                if c >= 1:
                    pe.wait_ge(relu_ready, c)
                pe.matmul(ps[:, 1, :], wmix[:, 1, :], mix[:, 1, :], start=True, stop=True).then_inc(rk_made, 1)

            for j in range(NT + TURN_LAG - TPC):
                project(0, j)
                if j >= TURN_LAG and (j - TURN_LAG) % TPC == 0:
                    turn_xhat(1, (j - TURN_LAG) // TPC, (6, 7))
            receptance_keys(0)
            turn_xhat(1, NC - 1, (6, 7))
            for c in range(NC + 2):
                if c < NC:
                    pe.wait_ge(kact_ready, c + 1)
                    if c >= 1:
                        pe.wait_ge(x_ready[2], c)
                    for i in range(TPC):
                        mm = pe.matmul(ps[:, 4, i * P:(i + 1) * P], mix[:, 3, i * P:(i + 1) * P], wmix[:, 2, :],
                                       start=True, stop=True)
                    mm.then_inc(vm_made, 1)
                if c + 1 < NC:
                    receptance_keys(c + 1)
                if 1 <= c <= NC:
                    turn_xhat(2, c - 1, (6, 7))
                if c >= 2:
                    qk(1, c - 2)
            pe.wait_ge(x_ready[2], NC)
            pe.wait_ge(low_ready[1], 2 * NC)

            def a_tile(u, g, k, hh, qt, half_, q0):
                n = u * 32 + k
                if not isinstance(n, int) or n >= 2:
                    pe.wait_ge(a_read[1], n - 1)
                h = g * HG + hh
                for i in range(2):
                    k0 = PAD + half_ * 1024 + i * CHUNK
                    mm = pe.matmul(ps[:, 2 * (k % 2) + i, :], QA[0:KR, h, bass.ds(q0 + qt * P, P)],
                                   KA[0:KR, h, k0:k0 + CHUNK], start=True, stop=True)
                mm.then_inc(a_made[1], 1)

            def b_tile(u, g, kt, hh, q0, last):
                n = (u * NT + kt) * HG + hh
                if last and hh >= 2 and kt == 0:
                    pe.wait_ge(a_read[1], NC * G * 32)
                elif last and kt >= 1:
                    pe.wait_ge(exp_done[1], n - 3)
                elif not isinstance(n, int) or n >= 2:
                    pe.wait_ge(exp_done[1], n - 1)
                h = g * HG + hh
                bank = LAST_BANKS[hh] if last else 4 + hh % 2
                pe.matmul(ps[:, bank, :], KA[0:KR, h, PAD + kt * P:PAD + (kt + 1) * P],
                          QA[0:KR, h, bass.ds(q0, CHUNK)], start=True, stop=True).then_inc(b_made[1], 1)

            def sum_tile(u, g, kt):
                pe.wait_ge(exp_done[1], (u * NT + kt + 1) * HG)
                if kt == 0:
                    pe.wait_ge(o_kept[1], u + 1)
                for hh in range(HG):
                    mm = pe.matmul(ps[32 * hh:32 * hh + VC, 6, :], V1[:, kt, g * HG + hh, :],
                                   PR[:, (kt % 2) * HG + hh, :], start=(kt == 0), stop=(kt == NT - 1),
                                   skip_group_check=True)
                mm.then_inc(pv_done[1], 1)

            def turn_maxima(u):
                pe.wait_ge(mparts_ready[1], u + 1)
                if not isinstance(u, int) or u >= 1:
                    pe.wait_ge(mrow_ready[1], u)
                pe.transpose(ps[:, 7, :].bitcast(BF16)[:, 0:P], mparts[:, :], identb[:, :]).then_inc(mt_made[1], 1)

            A_ALL = [(hh, qt, hf) for hh in range(HG) for qt in range(4) for hf in range(2)]
            AHEAD, TURN_AT = 8, 13

            def unit(qc, g, blocks, final=False):
                u = qc * G + g
                q0 = qc * CHUNK

                def a_next(k):
                    s = AHEAD + k
                    g2 = g + 1 + s // 32
                    over = g2 >= G
                    if final and over:
                        return
                    a_tile(u + 1 + s // 32, g2 % G, s % 32, *A_ALL[s % 32], q0 + (CHUNK if over else 0))

                for kt in blocks:
                    if kt == 0:
                        pe.wait_ge(mrow_in[1], 16 * HG * (u + 1))
                    last = final and g == G - 1
                    b_tile(u, g, kt, 0, q0, last)
                    b_tile(u, g, kt, 1, q0, last)
                    a_next(2 * kt)
                    a_next(2 * kt + 1)
                    b_tile(u, g, kt, 2, q0, last)
                    b_tile(u, g, kt, 3, q0, last)
                    if kt >= 1:
                        sum_tile(u, g, kt - 1)
                    elif not isinstance(u, int) or u >= 1:
                        sum_tile(u - 1, (g - 1) % G, NT - 1)
                    if kt == TURN_AT and not (final and g == G - 1):
                        turn_maxima(u + 1)

            pe.wait_ge(rows_in[1], 32)
            pe.wait_ge(first_in, 16 * 2 * len(PAIRS))
            for k, tile in enumerate(FIRST_UNIT):
                if k == 16:
                    pe.wait_ge(qk_in[1][0], 16 * 2 * len(PAIRS))
                a_tile(0, 0, k, *A_ALL[tile], 0)
                if k < NT:
                    values(1, [k])
            pe.wait_ge(v_ready[1], NT // 4)
            pe.wait_ge(xt_ready[2], NC)
            pe.wait_ge(ones_ready, 1)
            pe.wait_ge(qk_in[1][1], 16 * 6)
            for s in range(AHEAD):
                if s == 4:
                    turn_maxima(0)
                a_tile(1, 1, s, *A_ALL[s], 0)
            for g in range(2, G):
                pe.wait_ge(qk_in[1][g], 16 * 6)
            unit(0, 0, range(1))
            with pe.Fori(0, NC - 1) as qc:
                unit(qc, 0, range(1, NT))
                for g in range(1, G):
                    unit(qc, g, range(NT))
                unit(qc + 1, 0, range(1), False)
            unit(NC - 1, 0, range(1, NT), True)
            for g in range(1, G):
                unit(NC - 1, g, range(NT), True)
            sum_tile(NC * G - 1, G - 1, NT - 1)

            def gate_up(c, i):
                k, m = c * MT + i, MT_ORDER[i]
                cols = XT[:, PAD + c * CHUNK:PAD + (c + 1) * CHUNK]
                wg = gate[:, m * P:(m + 1) * P] if m < MT_R else sgate[:, (m - MT_R) * P:(m - MT_R + 1) * P]
                wu = upw[:, m * P:(m + 1) * P] if m < MT_R else sup[:, (m - MT_R) * P:(m - MT_R + 1) * P]
                if k >= 2:
                    pe.wait_ge(silu_ready, k - 1)
                pe.matmul(ps[:, k % 2, :], wg, cols, start=True, stop=True).then_inc(g_made, 1)
                if k >= 2:
                    pe.wait_ge(gu_ready, k - 1)
                pe.matmul(ps[:, 2 + k % 2, :], wu, cols, start=True, stop=True).then_inc(u_made, 1)

            def comb_rows(c, m):
                k = c * MT_R + m
                if k >= 2:
                    pe.wait_ge(hid_ready, k - 1)
                pe.matmul(ps[:, 4 + 2 * (k % 2), :], spread[:, m, :], combT[:, c * CHUNK:(c + 1) * CHUNK],
                          start=True, stop=True).then_inc(cb_made, 1)

            def down_proj(c):
                pe.wait_ge(hid_ready, (c + 1) * MT_R)
                if c >= 2:
                    pe.wait_ge(y_ready, c - 1)
                for i in range(TPC):
                    for m in range(MT):
                        wd = down[:, m, :] if m < MT_R else sdown[:, m - MT_R, :]
                        mm = pe.matmul(ps[:, 5 + 2 * (c % 2), i * P:(i + 1) * P], hid[:, c % 3, m, i * P:(i + 1) * P],
                                       wd, start=(m == 0), stop=(m == MT - 1))
                    if i == TPC - 1:
                        mm.then_inc(down_made, 1)
                    if c + 1 < NC:
                        comb_rows(c + 1, i)

            def logits(tiles):
                for j in tiles:
                    mm = pe.matmul(ps[:, 5, j * E:(j + 1) * E], XT[:, PAD + j * P:PAD + (j + 1) * P], router,
                                   start=True, stop=True)
                mm.then_inc(logits_made, 1)

            pe.wait_ge(o_kept[1], NC * G + 1)
            for j in range(NT + TURN_LAG - TPC):
                project(1, j)
                if j >= TURN_LAG and (j - TURN_LAG) % TPC == 0:
                    turn_xhat(3, (j - TURN_LAG) // TPC, (6, 7))
            pe.wait_ge(w_in, 16 * 12)
            pe.wait_ge(x_ready[3], NT)
            pe.wait_ge(xt_ready[3], NC - 1)
            logits(range(NT - TPC))
            turn_xhat(3, NC - 1, (6, 7))
            pe.wait_ge(xt_ready[3], NC)
            logits(range(NT - TPC, NT))

            for k in range(EARLY):
                gate_up(k // MT, k % MT)
            pe.wait_ge(comb_ready, 1)
            for j in range(NT):
                bank = ps[:, 6 + j // 8, :].bitcast(BF16)
                mm = pe.transpose(bank[0:48, j % 8 * P:(j % 8 + 1) * P], combp[:, j, :], identb[:, :])
            mm.then_inc(comb_turned, 1)
            gate_up(EARLY // MT, EARLY % MT)
            pe.wait_ge(combT_ready, 2)
            for m in range(MT_R):
                comb_rows(0, m)
                k = EARLY + 1 + m
                if k < 3 * MT:
                    gate_up(k // MT, k % MT)
            for c in range(NC):
                down_proj(c)
                if c == 0:
                    for i in range(MT):
                        gate_up(3, i)

        @block.scalar
        def _(act):
            def keep_xt(n, c, banks):
                act.wait_ge(turned[n], c + 1)
                dst = XT[:, PAD + c * CHUNK:PAD + (c + 1) * CHUNK]
                src = ps[:, banks[c % 2], :]
                if n == 0:
                    act.activation(dst, src, ACT.Identity, bias=BETA, scale=GAMMA).then_inc(xt_ready[n], 1)
                else:
                    act.activation(dst, src, ACT.Copy).then_inc(xt_ready[n], 1)

            def normalise(n, c):
                act.wait_ge(rstd_ready[n], c + 1)
                if c >= 2:
                    act.wait_ge(turned[n], c - 1)
                for i in range(TPC):
                    t = c * TPC + i
                    ins = act.activation(xhat[:, c % 2, i, :], X[:, t, :], ACT.Identity, bias=shift[:, t:t + 1],
                                         scale=rs[:, t:t + 1])
                ins.then_inc(xhat_ready[n], 1)

            def high_part(n, c, s):
                act.wait_ge(qk_made[n], 2 * c + s + 1)
                act.activation(part(s, HIGH, c), ps[:, 2 + s, :], ACT.Copy)\
                   .then_inc(high_ready[n], 1)

            def mid_part(n, c, s):
                act.wait_ge(resid_ready[n], 2 * c + s + 1)
                act.activation(part(s, MID, c), resid[:, s, :], ACT.Copy)\
                   .then_inc(mid_ready[n], 1)

            def split_parts(n, c):
                high_part(n, c, 0)
                high_part(n, c, 1)
                mid_part(n, c, 0)
                mid_part(n, c, 1)

            def keep_values(n, k):
                blocks = NB if n == 0 else NT
                act.wait_ge(v_made[n], k + 1)
                n4 = min(4, blocks - 4 * k)
                for b in range(4 * k, 4 * k + n4):
                    nk = min(P, WK - b * QB) if n == 0 else P
                    ins = act.activation(V[0:nk, b, :, 0:HD],
                                         ps[0:nk, 4 + k % 2, b % 4 * P:(b % 4 + 1) * P]
                                         .rearrange("p (h d) -> p h d", h=H),
                                         ACT.Copy)
                ins.then_inc(v_ready[n], 1)

            act.wait_ge(w_in, 16 * 3)
            keep_xt(0, 0, (0, 1))
            keep_xt(0, 1, (0, 1))
            for c in range(NC):
                high_part(0, c, 0)
                high_part(0, c, 1)
                if c + 2 < NC:
                    keep_xt(0, c + 2, (0, 1))
                mid_part(0, c, 0)
                mid_part(0, c, 1)
            for k in range(-(-NB // 4)):
                keep_values(0, k)

            act.wait_ge(v_made[0], -(-NB // 4))
            act.wait_ge(low_ready[0], 2 * NC)
            act.wait_ge(parts_kept[0], 2 * NC * 16)

            def exps(t, g):
                act.wait_ge(b_made[0], t * HG + g + 1)
                if not isinstance(t, int) or t >= 1:
                    act.wait_ge(pv_done[0], t * HG + g - HG + 1)
                act.activation(PR[:, g, 0:HG * QB], ps[:, 2 + g % 2, 0:HG * QB], ACT.Exp, scale=HD ** -0.5)\
                   .then_inc(exp_done[0], 1)

            def keep_sums(t, par, nq=QB):
                act.wait_ge(pv_done[0], (t + 1) * HG)
                act.activation(OT[:, :, bass.ds(t * QB, nq)],
                               ps[:, 4 + par, 0:G * QB].rearrange("p (g n) -> p g n", g=G)[:, :, 0:nq],
                               ACT.Copy).then_inc(o_kept[0], 1)

            for g in range(G):
                exps(0, g)
            with act.Fori(1, NB - 1, 2) as t:
                for d in range(2):
                    exps(t + d, 0)
                    exps(t + d, 1)
                    keep_sums(t + (d - 1), d)
                    exps(t + d, 2)
                    exps(t + d, 3)
            exps(NB - 1, 0)
            exps(NB - 1, 1)
            keep_sums(NB - 2, NB % 2)
            exps(NB - 1, 2)
            exps(NB - 1, 3)
            keep_sums(NB - 1, (NB - 1) % 2, T - (NB - 1) * QB)

            def turn_back(n, j):
                act.wait_ge(on_turned[n], j + 1)
                if j >= 2:
                    act.wait_ge(proj_made[n], j - 1)
                act.activation(OnT[:, j % 2, :], ps[:, 2 + j % 2, 0:P], ACT.Copy).then_inc(ont_ready[n], 1)

            def gates(c):
                act.wait_ge(rk_made, 2 * c + 1)
                if c >= 1:
                    act.wait_ge(x_ready[2], c)
                act.activation(mix[:, 4, :], ps[:, 0, :], ACT.Sigmoid).then_inc(sig_ready, 1)
                act.wait_ge(rk_made, 2 * c + 2)
                if c >= 1:
                    act.wait_ge(kact_ready, c)
                act.activation(mix[:, 2, :], ps[:, 1, :], ACT.Relu).then_inc(relu_ready, 1)

            for j in range(NT + KEEP_LAG - TPC):
                if j < NT:
                    turn_back(0, j)
                if j >= NORM_LAG and (j - NORM_LAG) % TPC == 0 and j - NORM_LAG < NT:
                    normalise(1, (j - NORM_LAG) // TPC)
                if j >= KEEP_LAG and (j - KEEP_LAG) % TPC == 0:
                    keep_xt(1, (j - KEEP_LAG) // TPC, (6, 7))
            gates(0)
            keep_xt(1, NC - 1, (6, 7))
            for c in range(NC + 2):
                if 1 <= c < NC:
                    gates(c)
                if 1 <= c <= NC:
                    normalise(2, c - 1)
                    act.wait_ge(mixed, 2 * min(c + 1, NC))
                    keep_xt(2, c - 1, (6, 7))
                if c >= 2:
                    split_parts(1, c - 2)
            act.wait_ge(x_ready[2], NC)
            for k in range(NT // 4):
                keep_values(1, k)
            act.wait_ge(v_made[1], NT // 4)
            act.wait_ge(low_ready[1], 2 * NC)
            act.wait_ge(parts_kept[1], 2 * NC * 16)

            def exp_round(r, first=False, last=False):
                for b in range(8):
                    act.wait_ge(b_made[1], r * 8 + b + 1)
                    if b % 4 == 0 and not first:
                        act.wait_ge(pv_done[1], r * 2 + b // 4 - 1)
                    bank = LAST_BANKS[b % HG] if last else 4 + b % 2
                    act.activation(PR[:, b, :], ps[:, bank, :], ACT.Exp, scale=HD ** 0.5)\
                       .then_inc(exp_done[1], 1)

            exp_round(0, first=True)
            with act.Fori(1, (NC * G - 1) * NT // 2) as r:
                exp_round(r)
            with act.Fori((NC * G - 1) * NT // 2, NC * G * NT // 2) as r:
                exp_round(r, last=True)
            for j in range(NT + KEEP_LAG - TPC + 1):
                if j < NT:
                    turn_back(1, j)
                if j >= NORM_LAG and (j - NORM_LAG) % TPC == 0 and j - NORM_LAG < NT:
                    normalise(3, (j - NORM_LAG) // TPC)
                if j >= KEEP_LAG and (j - KEEP_LAG) % TPC == 0:
                    keep_xt(3, (j - KEEP_LAG) // TPC, (6, 7))
            act.wait_ge(logits_made, 2)
            act.activation(rt[:, 0, :, :], ps[:, 5, 0:NT * E].rearrange("p (t e) -> p t e", t=NT), ACT.Sigmoid)\
               .then_inc(scores_ready, 1)
            for k in range(NC * MT):
                act.wait_ge(g_made, k + 1)
                if k >= 2:
                    act.wait_ge(gu_ready, k - 1)
                act.activation(silu[:, k % 2, :], ps[:, k % 2, :], ACT.Silu).then_inc(silu_ready, 1)
                if k == EARLY - 1:
                    act.wait_ge(comb_turned, 1)
                    act.wait_ge(zeroed[1], 1)
                    for i in range(2):
                        act.activation(combT[0:48, i * 1024:(i + 1) * 1024], ps[0:48, 6 + i, :].bitcast(BF16),
                                       ACT.Copy).then_inc(combT_ready, 1)

        @block.vector
        def _(v):
            chain = Count(v, dve)

            def stat(n, c):
                t0 = c * TPC
                for i in range(TPC):
                    if n in (1, 3):
                        v.wait_ge(x_ready[n], t0 + i + 1)
                    chain.up(v.bn_stats(stats[:, i, :], X[:, t0 + i, :]))
                chain.settle()
                for i in range(TPC):
                    ins = v.bn_aggr(mv[:, t0 + i, :], stats[:, i, :])
                    if i < TPC - 1:
                        chain.up(ins)
                ins.then_inc(stats_ready[n], 1)
                v.wait_ge(stats_ready[n], c + 1)
                chain.settle()

            def normalise(n, c):
                v.wait_ge(rstd_ready[n], c + 1)
                if c >= 2:
                    v.wait_ge(turned[n], c - 1)
                for i in range(TPC):
                    t = c * TPC + i
                    ins = v.tensor_scalar(xhat[:, c % 2, i, :], X[:, t, :], mv[:, t, 0:1], rs[:, t:t + 1],
                                          ALU.subtract, ALU.mult)
                    if i < TPC - 1:
                        chain.up(ins)
                ins.then_inc(xhat_ready[n], 1)

            def left_by_high(n, c):
                for s in range(2):
                    k = 2 * c + s
                    v.wait_ge(high_ready[n], k + 1)
                    if c >= 1:
                        v.wait_ge(low_ready[n], k - 1)
                    v.tensor_tensor(resid[:, s, :], ps[:, 2 + s, :], part(s, HIGH, c), ALU.subtract)\
                     .then_inc(resid_ready[n], 1)

            def left_by_mid(n, c):
                for s in range(2):
                    v.wait_ge(mid_ready[n], 2 * c + s + 1)
                    v.tensor_tensor(part(s, LOW, c), resid[:, s, :], part(s, MID, c), ALU.subtract)\
                     .then_inc(low_ready[n], 1)

            chain.up(v.memset(mparts[:, :], 0.0))
            for c in range(NC):
                v.wait_ge(x_in[c], 16)
                stat(0, c)
            v.wait_ge(w_in, 48)
            v.tensor_scalar(vecs[:, 4:6], vecs[:, 2:4], -1.0, 1.0, ALU.mult, ALU.add).then_inc(om_ready, 1)
            def norm_and_stream(c):
                normalise(0, c)
                v.wait_ge(xhat_ready[0], c + 1)
                chain.settle()
                for i in range(TPC):
                    t = c * TPC + i
                    ins = v.tensor_scalar(X[:, t, :], X[:, t, :], tmp4[:, 1, t:t + 1], tmp4[:, 2, t:t + 1],
                                          ALU.mult, ALU.add)
                    if i < TPC - 1:
                        chain.up(ins)
                ins.then_inc(resid_in_x, 1)

            norm_and_stream(0)
            norm_and_stream(1)
            for c in range(NC):
                left_by_high(0, c)
                if c + 2 < NC:
                    norm_and_stream(c + 2)
                left_by_mid(0, c)

            v.wait_ge(v_ready[0], -(-NB // 4))
            v.memset(ps[:, 4:6, :], 0.0).then_inc(zeroed[0], 1)
            def maxima(t, t3, copy=True):
                for g in range(G):
                    bank = ps[0:QB, A_BANKS[(t3 * G + g) % 3], :]
                    v.wait_ge(a_made[0], t * G + g + 1)
                    for hh in range(HG):
                        h = g * HG + hh
                        ins = v.tensor_tensor_reduce(masked[:, g, hh, :], bank[:, hh * P:(hh + 1) * P], maskA[:, :],
                                                     1.0, -3e38, ALU.add, ALU.max, block_max[:, t3, h:h + 1])
                    ins.then_inc(a_read[0], 1)
                    if g == 3 and copy:
                        keep_row(t - 1)

            def keep_row(t):
                v.wait_ge(mt_made[0], t + 1)
                if not isinstance(t, int) or t >= 1:
                    v.wait_ge(mrow_in[0], t * 48)
                v.tensor_copy(mrow[:, 0:QB], ps[:, 6, :].bitcast(BF16)[0:48, 0:QB]).then_inc(mrow_ready[0], 1)

            v.wait_ge(w2_in, 16 * 8)
            for t in range(NB):
                maxima(t, t % 3, t >= 1)
            keep_row(NB - 1)

            def inverse_sums(n, j):
                v.wait_ge(o_turned[n], j + 1)
                bank = ps[:, j % 2, :].rearrange("p (h n) -> p h n", h=H)
                chain.up(v.reciprocal(rz[:, j % 2, :], bank[:, :, HD]))

            def normed(n, j):
                bank = ps[:, j % 2, :].rearrange("p (h n) -> p h n", h=H)
                chain.settle()
                if j >= 2:
                    v.wait_ge(on_turned[n], j - 1)
                v.tensor_tensor(On[:, j % 2, :].rearrange("p (h d) -> p h d", h=H), bank[:, :, 0:HD],
                                rz[:, j % 2, :].unsqueeze(2).to_broadcast([P, H, HD]), ALU.mult).then_inc(on_ready[n], 1)

            def add_proj(n, j):
                v.wait_ge(proj_made[n], j + 1)
                v.tensor_tensor(X[:, j, :], ps[:, 4 + j % 2, 0:P], X[:, j, :], ALU.add).then_inc(x_ready[2 * n + 1], 1)

            v.wait_ge(pv_done[0], HG * NB)
            chain.up(v.memset(XT[:, 0:PAD], 0.0))
            for j in range(NT + STAT_LAG - TPC + 1):
                if j < NT:
                    inverse_sums(0, j)
                if ADD_LAG <= j < NT + ADD_LAG:
                    add_proj(0, j - ADD_LAG)
                if j < NT:
                    normed(0, j)
                if j >= STAT_LAG and (j - STAT_LAG) % TPC == 0:
                    stat(1, (j - STAT_LAG) // TPC)
            def mix_tokens(c):
                x0 = PAD + c * CHUNK
                cur, prev = XT[:, x0:x0 + CHUNK], XT[:, x0 - 1:x0 - 1 + CHUNK]
                v.wait_ge(xt_ready[1], c + 1)
                for s, (mu, om) in enumerate(((MU_R, OM_R), (MU_K, OM_K))):
                    if c >= 1:
                        v.wait_ge(rk_made, 2 * c - 1 + s)
                    chain.up(v.tensor_scalar(mix[:, 5, :], prev, om, None, ALU.mult))
                    chain.settle()
                    v.scalar_tensor_tensor(out=mix[:, s, :], in0=cur, scalar=mu, in1=mix[:, 5, :],
                                           op0=ALU.mult, op1=ALU.add).then_inc(mixed, 1)
                    v.wait_ge(mixed, 2 * c + s + 1)

            def gate_values(c):
                v.wait_ge(sig_ready, c + 1)
                v.wait_ge(vm_made, c + 1)
                chain.up(v.tensor_tensor(mix[:, 5, :], ps[:, 4, :], mix[:, 4, :], ALU.mult))
                chain.settle()
                xc = X[:, c * TPC:(c + 1) * TPC, :].rearrange("p t c -> p (t c)")
                v.tensor_tensor(xc, mix[:, 5, :], xc, ALU.add).then_inc(x_ready[2], 1)
                v.wait_ge(x_ready[2], c + 1)

            v.wait_ge(om_ready, 1)
            mix_tokens(0)
            for c in range(NC + 2):
                if c < NC:
                    v.wait_ge(relu_ready, c + 1)
                    if c >= 1:
                        v.wait_ge(vm_made, c)
                    v.tensor_tensor(mix[:, 3, :], mix[:, 2, :], mix[:, 2, :], ALU.mult).then_inc(kact_ready, 1)
                if c + 1 < NC:
                    mix_tokens(c + 1)
                if c < NC:
                    gate_values(c)
                    stat(2, c)
                if c >= 2:
                    left_by_high(1, c - 2)
                    left_by_mid(1, c - 2)
            v.wait_ge(xt_ready[2], NC)
            v.memset(ps[:, 6, :], 0.0).then_inc(o_kept[1], 1)
            chain.settle()

            def reduce_tiles(u, par, tiles):
                for k in tiles:
                    v.wait_ge(a_made[1], u * 32 + k + 1)
                    v.tensor_reduce(rawmax[:, par, k:k + 1], ps[:, 2 * (k % 2):2 * (k % 2) + 2, :], AX.XY, ALU.max)\
                     .then_inc(a_read[1], 1)

            def unit_maxima(u, par):
                v.wait_ge(a_read[1], u * 32 + 32)
                halves = rawmax[:, par, :].rearrange("p (a b) -> p a b", b=2)
                v.tensor_reduce(rowmax[:, :], halves, AX.X, ALU.max).then_inc(rowmax_ready, 1)

            def keep_rows(u):
                v.wait_ge(mt_made[1], u + 1)
                if not isinstance(u, int) or u >= 1:
                    v.wait_ge(mrow_in[1], 16 * HG * u)
                v.tensor_copy(mrow[:, :], ps[:, 7, :].bitcast(BF16)[0:48, 0:P]).then_inc(mrow_ready[1], 1)

            def keep_unit(u, g, q0):
                v.wait_ge(pv_done[1], u * NT + NT)
                v.tensor_copy(OT[:, g, bass.ds(q0, CHUNK)], ps[:, 6, :]).then_inc(o_kept[1], 1)

            def reduce_unit(u, g, more=8):
                reduce_tiles(u + 1, (g + 1) % 2, range(10, 32))
                unit_maxima(u + 1, (g + 1) % 2)
                reduce_tiles(u + 2, g % 2, range(0, min(4, more)))
                keep_rows(u + 1)
                reduce_tiles(u + 2, g % 2, range(min(4, more), more))

            for k, tile in enumerate(FIRST_UNIT):
                v.wait_ge(a_made[1], k + 1)
                v.tensor_reduce(rawmax[:, 0, tile:tile + 1], ps[:, 2 * (k % 2):2 * (k % 2) + 2, :], AX.XY, ALU.max)\
                 .then_inc(a_read[1], 1)
            unit_maxima(0, 0)
            reduce_tiles(1, 1, range(4))
            keep_rows(0)
            reduce_tiles(1, 1, range(4, 10))
            with v.Fori(0, NC - 1) as qc:
                for g in range(G):
                    u = qc * G + g
                    reduce_unit(u, g)
                    reduce_tiles(u + 2, g % 2, range(8, 10))
                    keep_unit(u, g, qc * CHUNK)
            for g in range(G):
                u = (NC - 1) * G + g
                if g + 1 < G:
                    reduce_unit(u, g, 8 if g + 2 < G else 0)
                if g + 2 < G:
                    reduce_tiles(u + 2, g % 2, range(8, 10))
                keep_unit(u, g, (NC - 1) * CHUNK)

            v.wait_ge(bp_added, 1)
            for j in range(NT + STAT_LAG - TPC + 1):
                if j < NT:
                    inverse_sums(1, j)
                if ADD_LAG <= j < NT + ADD_LAG:
                    add_proj(1, j - ADD_LAG)
                if j < NT:
                    normed(1, j)
                if j >= STAT_LAG and (j - STAT_LAG) % TPC == 0:
                    stat(3, (j - STAT_LAG) // TPC)
            v.memset(combT.bitcast(U32), 0).then_inc(zeroed[1], 1)
            chain.up(v.memset(pre[:, :, :, :], 0.0))
            v.wait_ge(scores_ready, 1)
            v.wait_ge(w_in, 16 * 12)
            S, SB, TOP, CMP, MASK, SEL, W, TMP = (rt[:, i] for i in range(8))
            TOP8 = TOP[:, :, 0:8]
            gv = lambda x: x.rearrange("p t (g e) -> p (t g) e", g=EG)
            GS = rt[:, 8].rearrange("p t e -> p (t e)")

            def do(ins):
                chain.up(ins)
                chain.settle()

            def small(i):
                return GS[:, 64 * i:64 * (i + 1)]

            do(v.tensor_tensor(SB, S, cbias.unsqueeze(1).to_broadcast([P, NT, E]), ALU.add))
            sb4 = gv(SB)
            t9 = rt[:, 9].rearrange("p t e -> p (t e)")
            big1, lit1 = t9[:, 0:64], t9[:, 64:128]
            big2, lit2 = t9[:, 128:192], t9[:, 192:256]
            chain.up(v.tensor_tensor(big1, sb4[:, :, 0], sb4[:, :, 1], ALU.max))
            chain.up(v.tensor_tensor(lit1, sb4[:, :, 0], sb4[:, :, 1], ALU.min))
            chain.up(v.tensor_tensor(big2, sb4[:, :, 2], sb4[:, :, 3], ALU.max))
            do(v.tensor_tensor(lit2, sb4[:, :, 2], sb4[:, :, 3], ALU.min))
            chain.up(v.tensor_tensor(small(0), big1, big2, ALU.max))
            chain.up(v.tensor_tensor(small(1), big1, big2, ALU.min))
            do(v.tensor_tensor(small(2), lit1, lit2, ALU.max))
            do(v.tensor_tensor(small(1), small(1), small(2), ALU.max))
            do(v.tensor_tensor(small(3), small(0), small(1), ALU.add))

            hidden = Count(v, gu_ready)

            def hidden_units():
                k = hidden.n
                c, m = k // MT, MT_ORDER[k % MT]
                v.wait_ge(silu_ready, k + 1)
                v.wait_ge(u_made, k + 1)
                if c >= 3 and k % MT == 0:
                    v.wait_ge(down_made, c - 2)
                hidden.up(v.tensor_tensor(hid[:, c % 3, m, :], ps[:, 2 + k % 2, :], silu[:, k % 2, :], ALU.mult))

            def add_experts(c):
                v.wait_ge(down_made, c + 1)
                xc = X[:, c * TPC:(c + 1) * TPC, :].rearrange("p t c -> p (t c)")
                v.tensor_tensor(xc, ps[:, 5 + 2 * (c % 2), :], xc, ALU.add).then_inc(y_ready, 1)

            def wins(score, n, won, cmp):
                do(v.memset(won, 0.0))
                for d in range(1, n):
                    c = cmp[:, :, 0:n - d]
                    do(v.tensor_tensor(c, score[:, :, 0:n - d], score[:, :, d:n], ALU.is_ge))
                    chain.up(v.tensor_tensor(won[:, :, 0:n - d], won[:, :, 0:n - d], c, ALU.add))
                    chain.settle()
                    chain.up(v.scalar_tensor_tensor(out=won[:, :, d:n], in0=won[:, :, d:n], scalar=1.0, in1=c,
                                                    op0=ALU.add, op1=ALU.subtract))
                    hidden_units()
                    chain.settle()

            grp = small(3).rearrange("p (t g) -> p t g", g=EG)
            gwon = small(0).rearrange("p (t g) -> p t g", g=EG)
            gcmp = small(1).rearrange("p (t g) -> p t g", g=EG)
            wins(grp, EG, gwon, gcmp)
            do(v.tensor_scalar(small(2), small(0), float(EG - TOPG), None, ALU.is_ge))
            chosen = small(2).unsqueeze(2).to_broadcast([P, NT * EG, E // EG])
            do(v.tensor_copy(gv(MASK), chosen))
            do(v.tensor_tensor(TMP, SB, MASK, ALU.mult))
            do(v.tensor_scalar(CMP, MASK, 1.0, 3e38, ALU.subtract, ALU.mult))
            do(v.tensor_tensor(TMP, TMP, CMP, ALU.add))
            for t in range(NT):
                chain.up(v.max(TOP8[:, t, :], TMP[:, t, :]))
                if t % 4 == 3:
                    hidden_units()
            chain.settle()
            kth = TOP8[:, :, TOPK - 1:TOPK].to_broadcast([P, NT, E])
            chain.up(v.tensor_tensor(SEL, TMP, kth, ALU.is_gt))
            chain.up(v.tensor_tensor(pre[:, 0, :, E:], TMP, kth, ALU.is_equal))
            hidden_units()
            chain.settle()
            wanted = small(0)[:, 0:NT]
            chain.up(v.tensor_reduce(wanted, SEL, AX.X, ALU.add))
            chain.up(v.tensor_tensor(pre[:, 1, :, E:], pre[:, 0, :, E:], pre[:, 0, :, E - 1:2 * E - 1], ALU.add))
            hidden_units()
            chain.settle()
            chain.up(v.tensor_scalar(wanted, wanted, -1.0, float(TOPK), ALU.mult, ALU.add))
            for d, src, dst in ((2, 1, 2), (4, 2, 1), (8, 1, 2)):
                chain.up(v.tensor_tensor(pre[:, dst, :, E:], pre[:, src, :, E:], pre[:, src, :, E - d:2 * E - d],
                                         ALU.add))
                hidden_units()
                chain.settle()
            do(v.tensor_tensor(CMP, pre[:, 2, :, E:], wanted.unsqueeze(2).to_broadcast([P, NT, E]), ALU.is_le))
            do(v.tensor_tensor(CMP, CMP, pre[:, 0, :, E:], ALU.mult))
            do(v.tensor_tensor(SEL, SEL, CMP, ALU.add))
            do(v.tensor_tensor(W, S, SEL, ALU.mult))
            sm = small(0)[:, 0:NT]
            do(v.tensor_reduce(sm, W, AX.X, ALU.add))
            do(v.tensor_scalar(sm, sm, 1e-20, None, ALU.add))
            do(v.reciprocal(small(1)[:, 0:NT], sm))
            do(v.tensor_tensor(W, W, small(1)[:, 0:NT].unsqueeze(2).to_broadcast([P, NT, E]), ALU.mult))
            cp = combp.rearrange("p t (i e) -> p i t e", i=3)
            do(v.tensor_copy(cp[:, HIGH], W))
            do(v.tensor_tensor(TMP, W, cp[:, HIGH], ALU.subtract))
            do(v.tensor_copy(cp[:, MID], TMP))
            v.tensor_tensor(cp[:, LOW], TMP, cp[:, MID], ALU.subtract).then_inc(comb_ready, 1)

            def weight_units(c, beside=0):
                for i in range(MT_R):
                    v.wait_ge(cb_made, c * MT_R + i + 1)
                    v.wait_ge(gu_ready, c * MT + MT_S + i + 1)
                    h = hid[:, c % 3, i, :]
                    v.tensor_tensor(h, ps[:, 4 + 2 * (i % 2), :], h, ALU.mult).then_inc(hid_ready, 1)
                    if hidden.n < beside:
                        hidden_units()

            while hidden.n < EARLY + 1:
                hidden_units()
            weight_units(0, 3 * MT)
            for c in range(NC):
                if c + 1 < NC:
                    weight_units(c + 1)
                add_experts(c)
                if c == 0:
                    for i in range(MT):
                        hidden_units()

        @block.gpsimd
        def _(g_):
            chain = Count(g_, pool)

            def do(ins):
                chain.up(ins)
                chain.settle()

            def rstd(n, c):
                g_.wait_ge(stats_ready[n], c + 1)
                t = slice(c * TPC, (c + 1) * TPC)
                if n:
                    chain.up(g_.tensor_scalar(tmp4[:, 1, t], mv[:, t, 0], -1.0, None, ALU.mult))
                    do(g_.tensor_scalar(tmp4[:, 0, t], mv[:, t, 1], EPS, None, ALU.add))
                    do(g_.tensor_tensor(rs[:, t], tmp4[:, 0, t], half[:, :], ALU.pow))
                    g_.tensor_tensor(shift[:, t], tmp4[:, 1, t], rs[:, t], ALU.mult).then_inc(rstd_ready[n], 1)
                    return
                do(g_.tensor_scalar(tmp4[:, 0, t], mv[:, t, 1], EPS, None, ALU.add))
                do(g_.tensor_tensor(rs1[:, t], tmp4[:, 0, t], half[:, :], ALU.pow))
                do(g_.tensor_tensor(tmp4[:, 0, t], mv[:, t, 1], rs1[:, t], ALU.mult))
                do(g_.tensor_tensor(tmp4[:, 0, t], tmp4[:, 0, t], rs1[:, t], ALU.mult))
                do(g_.tensor_scalar(tmp4[:, 0, t], tmp4[:, 0, t], EPS, None, ALU.add))
                do(g_.tensor_tensor(tmp4[:, 2, t], tmp4[:, 0, t], half[:, :], ALU.pow))
                do(g_.tensor_tensor(rs[:, t], tmp4[:, 2, t], rs1[:, t], ALU.mult))
                do(g_.tensor_scalar(tmp4[:, 1, t], rs1[:, t], 1.0, None, ALU.add))
                do(g_.tensor_tensor(tmp4[:, 2, t], mv[:, t, 0], rs1[:, t], ALU.mult))
                g_.tensor_scalar(tmp4[:, 2, t], tmp4[:, 2, t], -1.0, None, ALU.mult).then_inc(rstd_ready[n], 1)

            do(g_.memset(half[:, :], -0.5))
            chain.up(g_.memset(XT[:, 0:PAD], 0.0))
            chain.up(g_.memset(V[:, :, :, HD:VC], 1.0))
            for ends in (slice(0, PAD), slice(PAD + T, WK)):
                chain.up(g_.memset(k_parts[:, :, ends], 0.0))
            chain.settle()
            g_.memset(XT[:, PAD + T:WK], 0.0).then_inc(zeroed[0], 1)
            for c in range(NC):
                rstd(0, c)
            def split_maxima(n, u, base, top):
                chain.n = base + u * 3
                rows = QB if n == 0 else P
                minus, left, zero = (x[0:rows, :] for x in (minus_max, negres, zero16))
                if n == 0:
                    view = mparts[0:rows, 0:48].rearrange("p (i h) -> p i h", i=3)
                    g_.wait_ge(a_read[0], u * G + G)
                else:
                    view = mparts[:, 0:48].rearrange("p (h i q) -> p i h q", h=HG, i=3)
                    g_.wait_ge(rowmax_ready, u + 1)
                do(g_.tensor_tensor(minus, zero, top, ALU.subtract))
                if not isinstance(u, int) or u >= 1:
                    g_.wait_ge(mt_made[n], u)
                if n == 1:
                    minus, left, zero = (x.rearrange("p (h q) -> p h q", h=HG) for x in (minus, left, zero))
                do(g_.tensor_tensor(view[:, HIGH], minus, zero, ALU.add))
                do(g_.tensor_tensor(left, minus, view[:, HIGH], ALU.subtract))
                g_.tensor_tensor(view[:, MID], left, zero, ALU.add).then_inc(mid_max[n], 1)
                g_.wait_ge(mid_max[n], u + 1)
                g_.tensor_tensor(view[:, LOW], left, view[:, MID], ALU.subtract).then_inc(mparts_ready[n], 1)

            do(g_.memset(zero16[:, :], 0.0))
            base = chain.n
            split_maxima(0, 0, base, block_max[:, 0, :])
            with g_.Fori(1, NB, 3) as t:
                for d in range(3):
                    split_maxima(0, t + d, base, block_max[:, (1 + d) % 3, :])
            chain.n = base + 3 * NB

            for c in range(NC):
                rstd(1, c)
            for c in range(NC):
                rstd(2, c)
            g_.wait_ge(x_ready[2], NC)
            g_.memset(V1[:, :, :, HD:VC], 1.0).then_inc(ones_ready, 1)
            g_.wait_ge(xhat_ready[2], NC)
            g_.wait_ge(w2_in, 16 * 8)
            g_.tensor_tensor(X[:, :, :], X[:, :, :], bp[:, :].unsqueeze(1).to_broadcast([P, NT, C]), ALU.add)\
              .then_inc(bp_added, 1)
            base = chain.n
            split_maxima(1, 0, base, rowmax[:, :])
            with g_.Fori(1, NC * G) as u:
                split_maxima(1, u, base, rowmax[:, :])
            chain.n = base + 3 * NC * G
            for c in range(NC):
                rstd(3, c)
    return nc


def parts_of(x):
    bf = mybir.dt.np(BF16)
    left, got = np.asarray(x, np.float64), []
    for _ in range(3):
        p = left.astype(np.float32).astype(bf)
        got.append(p)
        left = left - p.astype(np.float64)
    return np.stack(got)


def constants():
    bf = mybir.dt.np(BF16)
    k = {}
    k["ident"] = np.eye(P, dtype=np.float32)
    k["identb"] = np.eye(P, dtype=np.float32).astype(bf)
    q, key = np.arange(QB)[:, None], np.arange(P)[None, :]
    mask = np.where((key - q >= 0) & (key - q <= 2 * HALF), 0.0, MASKED).astype(np.float32)
    k["maskA"] = mask
    k["maskB"] = np.repeat(mask.T[:, None, :], HG, 1).astype(bf)
    k["ones"] = np.ones((3, H, WK), np.float32).astype(bf)
    k["zeros"] = np.zeros((KR - ROW_MAX, H, WK), np.float32).astype(bf)
    edge = np.zeros((3, H, WK), np.float32)
    edge[0, :, 0:PAD] = MASKED
    edge[0, :, PAD + T:] = MASKED
    k["kbias0"] = edge.astype(bf)
    x = (2 ** 8) ** (1.0 / H)
    slopes = np.array([1.0 / x ** (i + 1) for i in range(H)], dtype=np.float32).astype(np.float64)
    bias = np.zeros((3, H, WK), bf)
    bias[:, :, PAD:PAD + T] = parts_of(slopes[:, None] * np.arange(T)[None, :] / np.sqrt(float(HD)))
    k["kbias1"] = bias
    spread = np.zeros((P, MT_R, P), np.float32)
    for i in range(3):
        for e in range(E):
            spread[E * i + e, e // 4, (e % 4) * HE:(e % 4 + 1) * HE] = 1.0
    k["spread"] = spread.astype(bf)
    return k


def kernel(**inputs):
    import numpy as _np
    import concourse.bacc as _bacc
    from concourse import mybir as _mybir
    from concourse.bass_utils import run_bass_kernel_spmd as _run

    f = {n: _np.asarray(x) for n, x in inputs.items()}
    arrays = constants()
    arrays["x"] = f["L0_attn_x"].reshape(T, C)
    order = _np.arange(C).reshape(H, HD).T.reshape(-1)
    arrays["wqkv0"] = f["L0_attn_w_qkv"].T[:, _np.concatenate([order, C + order, 2 * C + _np.arange(C)])]
    arrays["wo0"] = f["L0_attn_w_out"].T
    arrays["vecs"] = _np.stack([f["L0_attn_gamma"], f["L0_attn_beta"], f["L0_ffn_mu_r"], f["L0_ffn_mu_k"]], 1)
    arrays["wmix"] = _np.stack([f["L0_ffn_W_r"].T, f["L0_ffn_W_k"].T, f["L0_ffn_W_v"].T], 1)
    arrays["wqkv1"] = _np.concatenate([f["L1_attn_Wq"].T[:, order], f["L1_attn_Wk"].T[:, order], f["L1_attn_Wv"].T], 1)
    arrays["wo1"] = f["L1_attn_Wp"].T
    arrays["bp_rows"] = _np.broadcast_to(f["L1_attn_bp"][None, :], (P, C))
    arrays["gate"] = f["L1_ffn_gate_w"].transpose(1, 0, 2).reshape(C, E * HE)
    arrays["up"] = f["L1_ffn_up_w"].transpose(1, 0, 2).reshape(C, E * HE)
    arrays["down"] = f["L1_ffn_down_w"].reshape(MT_R, P, C).transpose(1, 0, 2)
    arrays["sgate"] = f["L1_ffn_shared_gate_w"].T
    arrays["sup"] = f["L1_ffn_shared_up_w"].T
    arrays["sdown"] = f["L1_ffn_shared_down_w"].T.reshape(MT_S, P, C).transpose(1, 0, 2)
    arrays["router"] = f["L1_ffn_router_w"].T
    arrays["cbias"] = _np.broadcast_to(f["L1_ffn_correction_bias"][None, :], (P, E))

    nc = _bacc.Bacc("TRN2", target_bir_lowering=False, num_devices=1)
    given, aps = {}, {}
    for name, v in arrays.items():
        v = _np.ascontiguousarray(v)
        given[f"in_{name}"] = v
        aps[name] = nc.dram_tensor(f"in_{name}", v.shape, _mybir.dt.from_np(v.dtype), kind="ExternalInput").ap()
    out = nc.dram_tensor("out", (T, C), _mybir.dt.from_np(_np.dtype("float32")), kind="ExternalOutput").ap()
    build(nc, aps, out)
    r = _run(nc, [given], core_ids=[0])
    return r.results[0]["out"].reshape(1, T, C)
```
